# Optimizing a Trainium2 kernel written in Bass

```python
import numpy as np
import jax
import jax.numpy as jnp

def _softmax(x, axis=-1):
    return jax.nn.softmax(x, axis=axis)

def _gelu(x):
    return jax.nn.gelu(x, approximate=True)

def _silu(x):
    return jax.nn.silu(x)

def _sigmoid(x):
    return jax.nn.sigmoid(x)

def _layernorm(x, axis=-1, eps=1e-05):
    m = jnp.mean(x, axis=axis, keepdims=True)
    v = jnp.var(x, axis=axis, keepdims=True)
    return (x - m) / jnp.sqrt(v + eps)

def _scatter_add(tgt, idx, src, axis=0):
    return tgt.at[idx].add(src)

def _segment_sum(src, seg, n):
    return jax.ops.segment_sum(src, seg, n)
kernel_name = 'mk_sandwich_d1_jaxref_r8_a16a4b'

def setup_inputs(seed: int=0):
    np.random.seed(seed)
    _w = jnp.asarray

    def _L0_attn_setup():
        import math
        import jax, jax.numpy as jnp
        import numpy as np
        LN_EPS = 1e-05

        def _relative_sinusoidal(t, hd, dtype):
            pos = jnp.arange(-(t - 1), t, dtype=dtype)[:, None]
            div = jnp.exp(jnp.arange(0, hd, 2, dtype=dtype) * (-math.log(10000.0) / hd))
            pe = jnp.zeros((2 * t - 1, hd), dtype=dtype)
            pe = pe.at[:, 0::2].set(jnp.sin(pos * div))
            pe = pe.at[:, 1::2].set(jnp.cos(pos * div))
            return pe
        key = jax.random.key(seed)
        ks = jax.random.split(key, 4)
        b, t, dim, H = (2, 256, 128, 16)
        hd = dim // H
        s = 0.02
        return {'x': jax.random.normal(ks[0], (b, t, dim), jnp.float32), 'ln_g': jnp.ones((dim,), jnp.float32), 'ln_b': jnp.zeros((dim,), jnp.float32), 'w_qkv': jax.random.normal(ks[1], (dim, 3 * dim), jnp.float32) * s, 'b_qkv': jnp.zeros((3 * dim,), jnp.float32), 'w_rel': jax.random.normal(ks[2], (hd, H), jnp.float32) * s, 'w_out': jax.random.normal(ks[3], (dim, dim), jnp.float32) * s, 'b_out': jnp.zeros((dim,), jnp.float32)}
    _L0_attn_in = _L0_attn_setup()

    def _L0_ffn_setup():
        import jax, jax.numpy as jnp
        import numpy as np
        E, K, NG, TG = (64, 8, 8, 4)
        CAP = 128
        SCALE = 2.5

        def _route(x_flat, gate_weight, e_bias):
            T = x_flat.shape[0]
            logits = x_flat.astype(jnp.float32) @ gate_weight.astype(jnp.float32).T
            scores = jax.nn.sigmoid(logits)
            sfc = scores + e_bias[None, :]
            group_scores = jax.lax.top_k(sfc.reshape(T, NG, E // NG), 2)[0].sum(-1)
            _, gidx = jax.lax.top_k(group_scores, TG)
            gmask = jnp.zeros((T, NG), jnp.float32).at[jnp.arange(T)[:, None], gidx].set(1.0)
            smask = jnp.repeat(gmask, E // NG, axis=1)
            tmp = jnp.where(smask > 0, sfc, 0.0)
            _, topk_idx = jax.lax.top_k(tmp, K)
            topk_w = jnp.take_along_axis(scores, topk_idx, axis=1)
            topk_w = topk_w / (topk_w.sum(-1, keepdims=True) + 1e-20)
            return (topk_idx, topk_w * SCALE)

        def _moe_forward(hidden_states, gate_weight, e_bias, w1, w2, w3, shared_gate, shared_up, shared_down):
            B, S, H = hidden_states.shape
            T = B * S
            x = hidden_states.reshape(T, H)
            topk_idx, topk_w = _route(x, gate_weight, e_bias)
            Sk = T * K
            flat_e = topk_idx.reshape(-1)
            order = jnp.argsort(flat_e)
            sorted_e = flat_e[order]
            counts = jax.ops.segment_sum(jnp.ones((Sk,), jnp.int32), flat_e, num_segments=E)
            offsets = jnp.cumsum(counts) - counts
            pos = jnp.arange(Sk) - offsets[sorted_e]
            tok_sorted = x[order // K]
            xe = jnp.zeros((E, CAP, H), x.dtype).at[sorted_e, pos].set(tok_sorted, mode='drop')
            h = jax.nn.silu(jnp.einsum('ech,efh->ecf', xe, w1)) * jnp.einsum('ech,efh->ecf', xe, w3)
            ye = jnp.einsum('ecf,ehf->ech', h, w2)
            pos_c = jnp.minimum(pos, CAP - 1)
            vals = ye[sorted_e, pos_c]
            vals = jnp.where((pos < CAP)[:, None], vals, 0.0)
            flat_w = topk_w.reshape(-1)[order].astype(vals.dtype)
            flat_t = (jnp.arange(Sk) // K)[order]
            out = jax.ops.segment_sum(vals * flat_w[:, None], flat_t, num_segments=T)
            shared = jax.nn.silu(x @ shared_gate.T) * (x @ shared_up.T) @ shared_down.T
            return (out + shared).reshape(B, S, H)
        key = jax.random.key(seed)
        ks = jax.random.split(key, 9)
        B, S, H, F = (1, 256, 128, 64)
        bound = 1.0 / 32.0
        return {'hidden_states': jax.random.normal(ks[0], (B, S, H), jnp.float32), 'gate_weight': jax.random.uniform(ks[1], (E, H), jnp.float32, -bound, bound), 'e_bias': jnp.zeros((E,), jnp.float32), 'w1': jax.random.normal(ks[2], (E, F, H), jnp.float32) * 0.02, 'w2': jax.random.normal(ks[3], (E, H, F), jnp.float32) * 0.02, 'w3': jax.random.normal(ks[4], (E, F, H), jnp.float32) * 0.02, 'shared_gate': jax.random.normal(ks[5], (2 * F, H), jnp.float32) * 0.02, 'shared_up': jax.random.normal(ks[6], (2 * F, H), jnp.float32) * 0.02, 'shared_down': jax.random.normal(ks[7], (H, 2 * F), jnp.float32) * 0.02}
    _L0_ffn_in = _L0_ffn_setup()
    _d = {'L0_attn_x': _L0_attn_in['x'], 'L0_attn_ln_g': _L0_attn_in['ln_g'], 'L0_attn_ln_b': _L0_attn_in['ln_b'], 'L0_attn_w_qkv': _L0_attn_in['w_qkv'], 'L0_attn_b_qkv': _L0_attn_in['b_qkv'], 'L0_attn_w_rel': _L0_attn_in['w_rel'], 'L0_attn_w_out': _L0_attn_in['w_out'], 'L0_attn_b_out': _L0_attn_in['b_out'], 'L0_ffn_gate_weight': _L0_ffn_in['gate_weight'], 'L0_ffn_e_bias': _L0_ffn_in['e_bias'], 'L0_ffn_w1': _L0_ffn_in['w1'], 'L0_ffn_w2': _L0_ffn_in['w2'], 'L0_ffn_w3': _L0_ffn_in['w3'], 'L0_ffn_shared_gate': _L0_ffn_in['shared_gate'], 'L0_ffn_shared_up': _L0_ffn_in['shared_up'], 'L0_ffn_shared_down': _L0_ffn_in['shared_down']}
    _x0 = _d['L0_attn_x']
    _d['L0_attn_x'] = jax.random.normal(jax.random.fold_in(jax.random.key(seed), 1), (4, 1024, 128), dtype=_x0.dtype)
    del _x0
    return _d

def reference(L0_attn_x, L0_attn_ln_g, L0_attn_ln_b, L0_attn_w_qkv, L0_attn_b_qkv, L0_attn_w_rel, L0_attn_w_out, L0_attn_b_out, L0_ffn_gate_weight, L0_ffn_e_bias, L0_ffn_w1, L0_ffn_w2, L0_ffn_w3, L0_ffn_shared_gate, L0_ffn_shared_up, L0_ffn_shared_down):

    def _L0_attn_ref(x, ln_g, ln_b, w_qkv, b_qkv, w_rel, w_out, b_out):
        import math
        import jax, jax.numpy as jnp
        import numpy as np
        LN_EPS = 1e-05

        def _relative_sinusoidal(t, hd, dtype):
            pos = jnp.arange(-(t - 1), t, dtype=dtype)[:, None]
            div = jnp.exp(jnp.arange(0, hd, 2, dtype=dtype) * (-math.log(10000.0) / hd))
            pe = jnp.zeros((2 * t - 1, hd), dtype=dtype)
            pe = pe.at[:, 0::2].set(jnp.sin(pos * div))
            pe = pe.at[:, 1::2].set(jnp.cos(pos * div))
            return pe
        b, t, dim = x.shape
        hd, H = w_rel.shape
        scale = hd ** (-0.5)
        mu = jnp.mean(x, axis=-1, keepdims=True)
        var = jnp.mean(jnp.square(x - mu), axis=-1, keepdims=True)
        xn = (x - mu) * jax.lax.rsqrt(var + LN_EPS) * ln_g + ln_b
        qkv = (xn @ w_qkv + b_qkv).reshape(b, t, 3, H, hd)
        qkv = jnp.transpose(qkv, (2, 0, 3, 1, 4))
        q, k, v = (qkv[0], qkv[1], qkv[2])
        scores = jnp.einsum('bhqd,bhkd->bhqk', q, k) * scale
        rel_pe = _relative_sinusoidal(t, hd, scores.dtype)
        rel_bias = rel_pe @ w_rel
        idx = jnp.arange(t)[:, None] - jnp.arange(t)[None, :] + (t - 1)
        bias = jnp.transpose(rel_bias[idx], (2, 0, 1))[None]
        attn = jax.nn.softmax(scores + bias, axis=-1)
        out = jnp.einsum('bhqk,bhkd->bhqd', attn, v)
        out = jnp.transpose(out, (0, 2, 1, 3)).reshape(b, t, dim)
        return out @ w_out + b_out

    def _L0_ffn_ref(hidden_states, gate_weight, e_bias, w1, w2, w3, shared_gate, shared_up, shared_down):
        import jax, jax.numpy as jnp
        import numpy as np
        E, K, NG, TG = (64, 8, 8, 4)
        CAP = 128
        SCALE = 2.5

        def _route(x_flat, gate_weight, e_bias):
            T = x_flat.shape[0]
            logits = x_flat.astype(jnp.float32) @ gate_weight.astype(jnp.float32).T
            scores = jax.nn.sigmoid(logits)
            sfc = scores + e_bias[None, :]
            group_scores = jax.lax.top_k(sfc.reshape(T, NG, E // NG), 2)[0].sum(-1)
            _, gidx = jax.lax.top_k(group_scores, TG)
            gmask = jnp.zeros((T, NG), jnp.float32).at[jnp.arange(T)[:, None], gidx].set(1.0)
            smask = jnp.repeat(gmask, E // NG, axis=1)
            tmp = jnp.where(smask > 0, sfc, 0.0)
            _, topk_idx = jax.lax.top_k(tmp, K)
            topk_w = jnp.take_along_axis(scores, topk_idx, axis=1)
            topk_w = topk_w / (topk_w.sum(-1, keepdims=True) + 1e-20)
            return (topk_idx, topk_w * SCALE)

        def _moe_forward(hidden_states, gate_weight, e_bias, w1, w2, w3, shared_gate, shared_up, shared_down):
            B, S, H = hidden_states.shape
            T = B * S
            x = hidden_states.reshape(T, H)
            topk_idx, topk_w = _route(x, gate_weight, e_bias)
            Sk = T * K
            flat_e = topk_idx.reshape(-1)
            order = jnp.argsort(flat_e)
            sorted_e = flat_e[order]
            counts = jax.ops.segment_sum(jnp.ones((Sk,), jnp.int32), flat_e, num_segments=E)
            offsets = jnp.cumsum(counts) - counts
            pos = jnp.arange(Sk) - offsets[sorted_e]
            tok_sorted = x[order // K]
            xe = jnp.zeros((E, CAP, H), x.dtype).at[sorted_e, pos].set(tok_sorted, mode='drop')
            h = jax.nn.silu(jnp.einsum('ech,efh->ecf', xe, w1)) * jnp.einsum('ech,efh->ecf', xe, w3)
            ye = jnp.einsum('ecf,ehf->ech', h, w2)
            pos_c = jnp.minimum(pos, CAP - 1)
            vals = ye[sorted_e, pos_c]
            vals = jnp.where((pos < CAP)[:, None], vals, 0.0)
            flat_w = topk_w.reshape(-1)[order].astype(vals.dtype)
            flat_t = (jnp.arange(Sk) // K)[order]
            out = jax.ops.segment_sum(vals * flat_w[:, None], flat_t, num_segments=T)
            shared = jax.nn.silu(x @ shared_gate.T) * (x @ shared_up.T) @ shared_down.T
            return (out + shared).reshape(B, S, H)
        return _moe_forward(hidden_states, gate_weight, e_bias, w1, w2, w3, shared_gate, shared_up, shared_down)
    x = L0_attn_x
    x = x + _layernorm(_L0_attn_ref(_layernorm(x, axis=-1), L0_attn_ln_g, L0_attn_ln_b, L0_attn_w_qkv, L0_attn_b_qkv, L0_attn_w_rel, L0_attn_w_out, L0_attn_b_out), axis=-1)
    x = x + _layernorm(_L0_ffn_ref(_layernorm(x, axis=-1), L0_ffn_gate_weight, L0_ffn_e_bias, L0_ffn_w1, L0_ffn_w2, L0_ffn_w3, L0_ffn_shared_gate, L0_ffn_shared_up, L0_ffn_shared_down), axis=-1)
    return x

_drawn_inputs = setup_inputs


def setup_inputs(seed=0):
    import zlib

    import numpy as np

    out = dict(_drawn_inputs(seed))
    spreads = {'L0_attn_ln_g': (1.0, 0.6),
     'L0_attn_ln_b': (0.0, 0.1),
     'L0_attn_b_qkv': (0.0, 0.1),
     'L0_attn_b_out': (0.0, 0.1),
     'L0_ffn_e_bias': (0.0, 0.1)}
    factors = {'L0_attn_w_rel': 39.392}
    for name, (base, spread) in spreads.items():
        noise = np.random.default_rng([zlib.crc32(name.encode()), seed]).standard_normal(out[name].shape)
        drawn = base * np.exp(spread * noise) if base else spread * noise
        out[name] = jnp.asarray(drawn.astype(out[name].dtype))
    for name, factor in factors.items():
        out[name] = (out[name] * factor).astype(out[name].dtype)
    return out
```

```python
from contextlib import ExitStack

import numpy as np

import concourse.bass as bass
from concourse import mybir

F32 = mybir.dt.float32
BF16 = mybir.dt.bfloat16
U32 = mybir.dt.uint32
ALU = mybir.AluOpType
ACT = mybir.ActivationFunctionType
AX = mybir.AxisListType

P = 128
B, T, DIM = 4, 1024, 128
H, HD = 16, 8
N = B * T
TILES = N // P
CHUNK = 512
CHUNKS = N // CHUNK
PER = CHUNK // P
EPS = 1e-5
SCALE = float(HD) ** -0.5
HG = 4
GROUPS = H // HG
VW = 32

TERMS = [(0, 0), (0, 1), (1, 0), (1, 1), (0, 2), (2, 0)]
QK_ROWS = HD * len(TERMS)
SCORE_ROWS = 2 * QK_ROWS
SHIFT_ROWS = 3
STACK_ROWS = SCORE_ROWS + SHIFT_ROWS


def wait_apart(engine, registers, met, *waits):
    for register, (_, count) in zip(registers, waits):
        engine.reg_mov(register, count)
    engine.wait_ge(*met)
    for register, (semaphore, _) in zip(registers, waits):
        engine.wait_ge(semaphore, register)


def exact_pieces(dve, nc, src, rest, pieces, done, count):
    nc.vector.tensor_copy(pieces[0], src).then_inc(done, 1)
    dve.wait_ge(done, count + 1)
    nc.vector.tensor_tensor(rest, src, pieces[0], ALU.subtract).then_inc(done, 1)
    dve.wait_ge(done, count + 2)
    nc.vector.tensor_copy(pieces[1], rest).then_inc(done, 1)
    dve.wait_ge(done, count + 3)
    nc.vector.tensor_tensor(pieces[2], rest, pieces[1], ALU.subtract).then_inc(done, 1)
    return 4


def project_tokens(nc, x, ln_g, ln_b, w_qkv, b_qkv, ident_in, q_pieces, k_pieces, v_padded):
    with ExitStack() as ctx:
        sb = lambda name, shape, dt=F32: ctx.enter_context(nc.sbuf_tensor(name, shape, dt))
        ps = lambda name: ctx.enter_context(nc.psum_tensor(name, [P, CHUNK], F32))
        sem = lambda name: ctx.enter_context(nc.semaphore(name))

        xc = sb("xc", [P, PER, DIM])
        stats = sb("stats", [P, PER, 6])
        mv = sb("mv", [P, PER, 2])
        var2 = sb("var2", [P, PER])
        std = sb("std", [P, PER])
        rstd = sb("rstd", [P, PER])
        xn = sb("xn", [P, PER, DIM])
        xnT = sb("xnT", [P, CHUNK])
        w = sb("w", [P, 3 * DIM])
        ident = sb("ident", [P, P])
        gcol = sb("gcol", [P, 1])
        bcol = sb("bcol", [P, 1])
        bqcol = sb("bqcol", [P, 1])
        bkcol = sb("bkcol", [P, 1])
        bv = sb("bv", [P, DIM])
        full = [sb("qfull", [P, CHUNK]), sb("kfull", [P, CHUNK])]
        rest = [sb("qrest", [P, CHUNK]), sb("krest", [P, CHUNK])]
        pieces = [sb("qpieces", [P, 3, CHUNK], BF16), sb("kpieces", [P, 3, CHUNK], BF16)]
        vst = sb("vst", [P, PER, H, VW])

        psT, psQ, psK, psV = ps("psT"), ps("psQ"), ps("psK"), ps("psV")

        const_in = sem("const_in")
        x_in = sem("x_in")
        stats_done = sem("stats_done")
        aggr_done = sem("aggr_done")
        var_done = sem("var_done")
        std_done = sem("std_done")
        rstd_done = sem("rstd_done")
        xn_done = sem("xn_done")
        turned = sem("turned")
        xnT_done = sem("xnT_done")
        qk_ready = sem("qk_ready")
        v_ready = sem("v_ready")
        full_done = sem("full_done")
        split_done = sem("split_done")
        pads_done = sem("pads_done")
        v_done = sem("v_done")
        stored = sem("stored")
        scaled_b = sem("scaled_b")

        CONSTS = 8
        block = ctx.enter_context(nc.Block())

        @block.sync
        def _(sp):
            for dst, src in (
                (w[:], w_qkv),
                (ident[:], ident_in),
                (gcol[:], ln_g.rearrange("(p o) -> p o", o=1)),
                (bcol[:], ln_b.rearrange("(p o) -> p o", o=1)),
                (bqcol[:], b_qkv[0:DIM].rearrange("(p o) -> p o", o=1)),
                (bkcol[:], b_qkv[DIM:2 * DIM].rearrange("(p o) -> p o", o=1)),
                (bv[:], b_qkv[2 * DIM:3 * DIM].rearrange("(o d) -> o d", o=1).to_broadcast([P, DIM])),
            ):
                sp.dma_start(dst, src).then_inc(const_in, 16)
            counts = [sp.alloc_register("counts_as")]
            with sp.Fori(0, CHUNKS) as i:
                sp.wait_ge(xn_done, i * PER)
                sp.dma_start(xc[:], x[bass.ds(i * CHUNK, CHUNK), :].rearrange("(j p) d -> p j d", p=P)).then_inc(x_in, 16)
                wait_apart(sp, counts, (const_in, 16 * 7), (split_done, i * 8 + 8))
                for p in range(3):
                    sp.dma_start(q_pieces[p, :, bass.ds(i * CHUNK, CHUNK)], pieces[0][:, p, :]).then_inc(stored, 16)
                    sp.dma_start(k_pieces[p, :, bass.ds(i * CHUNK, CHUNK)], pieces[1][:, p, :]).then_inc(stored, 16)
                sp.wait_ge(v_done, i + 1)
                sp.dma_start(v_padded[:, bass.ds(i * PER, PER), :],
                             vst[:].rearrange("p j h c -> p j (h c)")).then_inc(stored, 16)
            sp.wait_ge(stored, CHUNKS * 7 * 16)

        @block.vector
        def _(dve):
            counts = [dve.alloc_register(f"counts_a{k}") for k in range(1)]
            nc.vector.memset(vst[:], 0.0).then_inc(pads_done, 1)
            dve.wait_ge(pads_done, 1)
            nc.vector.memset(vst[:, :, :, HD:HD + 1], 1.0).then_inc(pads_done, 1)
            dve.wait_ge(const_in, 16 * 7)
            nc.vector.tensor_scalar(bqcol[:], bqcol[:], SCALE, None, ALU.mult).then_inc(scaled_b, 1)
            with dve.Fori(0, CHUNKS) as i:
                dve.wait_ge(x_in, i * 16 + 16)
                for j in range(PER):
                    nc.vector.bn_stats(stats[:, j, :], xc[:, j, :]).then_inc(stats_done, 1)
                for j in range(PER):
                    wait_apart(dve, counts, (const_in, 16 * 7), (stats_done, i * PER + j + 1))
                    nc.vector.bn_aggr(mv[:, j, :], stats[:, j, :]).then_inc(aggr_done, 1)
                dve.wait_ge(aggr_done, i * PER + PER)
                nc.vector.tensor_scalar(var2[:], mv[:, :, 1], 1.0 + EPS, EPS * EPS, ALU.mult, ALU.add).then_inc(var_done, 1)
                dve.wait_ge(std_done, i + 1)
                nc.vector.reciprocal(rstd[:], std[:]).then_inc(rstd_done, 1)
                dve.wait_ge(rstd_done, i + 1)
                dve.wait_ge(turned, i)
                for j in range(PER):
                    nc.vector.tensor_scalar(xn[:, j, :], xc[:, j, :], mv[:, j, 0:1], rstd[:, j:j + 1],
                                            ALU.subtract, ALU.mult).then_inc(xn_done, 1)
                dve.wait_ge(stored, i * (7 * 16))
                for a in range(2):
                    dve.wait_ge(full_done, i * 2 + a + 1)
                    exact_pieces(dve, nc, full[a][:], rest[a][:], [pieces[a][:, p, :] for p in range(3)],
                                 split_done, i * 8 + 4 * a)
                dve.wait_ge(v_ready, i + 1)
                nc.vector.tensor_tensor(
                    vst[:, :, :, 0:HD], psV[:].rearrange("p (j h d) -> p j h d", j=PER, h=H),
                    bv[:].rearrange("p (o h d) -> p o h d", o=1, h=H).to_broadcast([P, PER, H, HD]),
                    ALU.add).then_inc(v_done, 1)

        @block.scalar
        def _(act):
            act.wait_ge(const_in, 16 * 7)
            act.wait_ge(scaled_b, 1)
            with act.Fori(0, CHUNKS) as i:
                act.wait_ge(var_done, i + 1)
                nc.scalar.activation(std[:], var2[:], ACT.Sqrt).then_inc(std_done, 1)
                act.wait_ge(turned, i + 1)
                act.wait_ge(v_ready, i)
                nc.scalar.activation(xnT[:], psT[:], ACT.Identity, bias=bcol[:], scale=gcol[:]).then_inc(xnT_done, 1)
                act.wait_ge(qk_ready, i * 2 + 1)
                act.wait_ge(split_done, i * 8)
                nc.scalar.activation(full[0][:], psQ[:], ACT.Identity, bias=bqcol[:], scale=SCALE).then_inc(full_done, 1)
                act.wait_ge(qk_ready, i * 2 + 2)
                nc.scalar.activation(full[1][:], psK[:], ACT.Identity, bias=bkcol[:]).then_inc(full_done, 1)

        @block.tensor
        def _(pe):
            pe.wait_ge(const_in, 16 * 7)
            with pe.Fori(0, CHUNKS) as i:
                pe.wait_ge(xn_done, i * PER + PER)
                pe.wait_ge(xnT_done, i)
                for j in range(PER):
                    mm = nc.tensor.transpose(psT[:, j * P:(j + 1) * P], xn[:, j, :], ident[:])
                mm.then_inc(turned, 1)
                pe.wait_ge(xnT_done, i + 1)
                pe.wait_ge(full_done, i * 2)
                nc.tensor.matmul(psQ[:], w[:, 0:DIM], xnT[:], start=True, stop=True).then_inc(qk_ready, 1)
                nc.tensor.matmul(psK[:], w[:, DIM:2 * DIM], xnT[:], start=True, stop=True).then_inc(qk_ready, 1)
                pe.wait_ge(v_done, i)
                for j in range(PER):
                    mm = nc.tensor.matmul(psV[:, j * P:(j + 1) * P], xnT[:, j * P:(j + 1) * P],
                                          w[:, 2 * DIM:3 * DIM], start=True, stop=True)
                mm.then_inc(v_ready, 1)


UNITS = 2 * GROUPS
STEPS = 32
BATCH_STEPS = UNITS * STEPS
LEAD = 48
ST_BANKS = 3
S_BANKS = 3
P_SLOTS = 16
PV_LAG = 6
J_UOUT, J_OTURN, J_OCOPY = 9, 12, 14
J_MTURN, J_MCOPY = 21, 22
LOADS = 2 * len(TERMS) + 1


def attend(nc, w_rel, q_table, k_table, ident_in, q_pieces, k_pieces, v_padded, att):
    with ExitStack() as ctx:
        sb = lambda name, shape, dt=F32: ctx.enter_context(nc.sbuf_tensor(name, shape, dt))
        ps = lambda name: ctx.enter_context(nc.psum_tensor(name, [P, CHUNK], F32))
        sem = lambda name: ctx.enter_context(nc.semaphore(name))

        q_stack = [sb(f"q_stack{g}", [STACK_ROWS, 2, HG, CHUNK], BF16) for g in range(GROUPS)]
        k_stack = [sb(f"k_stack{g}", [STACK_ROWS, 2, HG, CHUNK], BF16) for g in range(GROUPS)]
        values = [sb(f"values{g}", [P, T // P, HG, VW]) for g in range(GROUPS)]
        probs = sb("probs", [P, P_SLOTS, CHUNK])
        half_max = [sb(f"half_max{v}", [P, STEPS]) for v in range(2)]
        minus_max = sb("minus_max", [P, STEPS // 2])
        shift_rest = sb("shift_rest", [P, STEPS // 2])
        shift = sb("shift", [P, 3, STEPS // 2], BF16)
        shiftT = sb("shiftT", [3 * STEPS // 2, P], BF16)
        unit_out = sb("unit_out", [P, CHUNK])
        unit_rows = sb("unit_rows", [P, PER, HG, HD + 1])
        ident = sb("identB", [P, P])
        ident16 = sb("ident16", [P, P], BF16)
        wrow = sb("wrow", [16, P])
        tabq = sb("tabq", [16, T])
        bias_q = sb("bias_q", [P, T])
        bias_rest = sb("bias_rest", [P, T])
        bias_qp = sb("bias_qp", [P, 3, T], BF16)
        tabk = sb("tabk", [HD, T])
        tabk_rest = sb("tabk_rest", [HD, T])
        tabk_p = sb("tabk_p", [HD, 3, T], BF16)

        st_bank = [ps(f"st_bank{v}") for v in range(ST_BANKS)]
        s_bank = [ps(f"s_bank{v}") for v in range(S_BANKS)]
        pv_bank = ps("pv_bank")
        misc = ps("misc")

        tables_in = sem("tables_in")
        w_clear = sem("w_clear")
        w_in = sem("w_in")
        bias_ready = sem("bias_ready")
        bias_read = sem("bias_read")
        setup = sem("setup")
        ones_done = sem("ones_done")
        bias_rows_in = sem("bias_rows_in")
        loaded = [sem(f"loaded{g}") for g in range(GROUPS)]
        s_ready = sem("s_ready")
        max_done = sem("max_done")
        row_max_done = sem("row_max_done")
        shift_done = sem("shift_done")
        shift_turned = sem("shift_turned")
        shiftT_done = sem("shiftT_done")
        shift_in = sem("shift_in")
        st_ready = sem("st_ready")
        exp_done = sem("exp_done")
        pv_done = sem("pv_done")
        unit_out_done = sem("unit_out_done")
        out_turned = sem("out_turned")
        rows_done = sem("rows_done")
        rows_stored = sem("rows_stored")

        block = ctx.enter_context(nc.Block())

        MAX0, EXP0, PV0 = S_BANKS, ST_BANKS, P_SLOTS // HG

        def before(s, ring):
            if s >= ring:
                return s - ring
            last = BATCH_STEPS - 1
            while last % ring != s:
                last -= 1
            return last - BATCH_STEPS

        def split(s):
            return s // STEPS, s % STEPS

        def load(sp, b, g):
            rows = slice(HG * HD * g, HG * HD * (g + 1))
            for which, (stack, src) in enumerate(((q_stack[g], q_pieces), (k_stack[g], k_pieces))):
                for t, term in enumerate(TERMS):
                    for half in range(2):
                        sp.dma_start(
                            stack[HD * t:HD * (t + 1), half],
                            src[term[which], rows, bass.ds(b * T + half * CHUNK, CHUNK)].rearrange("(h d) i -> d h i", d=HD),
                        ).then_inc(loaded[g], 16)
            sp.dma_start(values[g][:].rearrange("p k h c -> p k (h c)"),
                         v_padded[:, bass.ds(b * (T // P), T // P), HG * VW * g:HG * VW * (g + 1)]).then_inc(loaded[g], 16)

        LOAD = 16 * (4 * len(TERMS) + 1)

        def put_shift(sp, unit, n):
            g, half = unit // 2, unit % 2
            sp.wait_ge(shiftT_done, n + 1)
            for p in range(3):
                r = SCORE_ROWS + p
                sp.dma_start(q_stack[g][r:r + 1, half].rearrange("o h i -> o (h i)"),
                             shiftT[16 * p:16 * (p + 1), :]).then_inc(shift_in, 16)

        def store_rows(sp, b, unit, n):
            g, half = unit // 2, unit % 2
            sp.wait_ge(rows_done, n + 1)
            sp.dma_start(att[bass.ds(b * T + half * CHUNK, CHUNK), HG * g:HG * (g + 1), :].rearrange("(t p) h c -> p t (h c)", p=P),
                         unit_rows[:].rearrange("p t h c -> p t (h c)")).then_inc(rows_stored, 16)

        @block.sync
        def _(sp):
            counts = [sp.alloc_register(f"counts_bs{k}") for k in range(2)]
            sp.dma_start(ident[:], ident_in).then_inc(tables_in, 16)
            sp.dma_start(tabq[:], q_table).then_inc(tables_in, 16)
            sp.dma_start(tabk[:], k_table).then_inc(tables_in, 16)
            sp.wait_ge(w_clear, 1)
            wv = wrow[:].rearrange("r (h e) -> r h e", e=HD)
            for f in range(HD // 2):
                for par in range(2):
                    for s in range(2):
                        r = 4 * f + 2 * par + s
                        sp.dma_start(wv[r:r + 1, :, 2 * f + par:2 * f + par + 1],
                                     w_rel[2 * f + s:2 * f + s + 1, :].rearrange("o (h e) -> o h e", e=1),
                                     allow_slow_non_contiguous=True).then_inc(w_in, 16)
            for g in range(GROUPS):
                load(sp, 0, g)
            sp.wait_ge(setup, 12)
            for g in range(GROUPS):
                for t, (pq, pk) in enumerate(TERMS):
                    r = QK_ROWS + HD * t
                    for h in range(HG):
                        at = HD * (HG * g + h)
                        sp.dma_start(q_stack[g][r:r + HD, :, h, :],
                                     bias_qp[at:at + HD, pq, :].rearrange("e (u i) -> e u i", u=2)).then_inc(bias_rows_in, 16)
                        sp.dma_start(k_stack[g][r:r + HD, :, h, :],
                                     tabk_p[:, pk, :].rearrange("e (u i) -> e u i", u=2)).then_inc(bias_rows_in, 16)
            put_shift(sp, 0, 0)

            def batch(b, last):
                for u in range(UNITS):
                    if u % 2 == 0 and u >= 2 and not last:
                        g = u // 2 - 1
                        wait_apart(sp, counts, (tables_in, 48), (st_ready, b * BATCH_STEPS + 2 * STEPS * (g + 1)),
                                   (pv_done, b * (BATCH_STEPS // HG) + 2 * STEPS // HG * (g + 1) + PV0))
                        load(sp, b + 1, g)
                    if u >= 1:
                        store_rows(sp, b, u - 1, b * UNITS + u - 1)
                    if u < UNITS - 1 or not last:
                        put_shift(sp, (u + 1) % UNITS, b * UNITS + u + 1)
                if not last:
                    wait_apart(sp, counts, (tables_in, 48), (st_ready, b * BATCH_STEPS + BATCH_STEPS),
                               (pv_done, b * (BATCH_STEPS // HG) + BATCH_STEPS // HG + PV0))
                    load(sp, b + 1, GROUPS - 1)
                store_rows(sp, b, UNITS - 1, b * UNITS + UNITS - 1)

            with sp.Fori(0, B - 1) as b:
                batch(b, False)
            batch(B - 1, True)
            sp.wait_ge(rows_stored, 16 * B * UNITS)

        @block.vector
        def _(dve):
            nc.vector.memset(wrow[:], 0.0).then_inc(w_clear, 1)
            n = 0
            for g in range(GROUPS):
                nc.vector.memset(k_stack[g][SCORE_ROWS:STACK_ROWS], 1.0).then_inc(setup, 1)
                n += 1
            dve.wait_ge(tables_in, 48)
            n += exact_pieces(dve, nc, tabk[:], tabk_rest[:], [tabk_p[:, p, :] for p in range(3)], setup, n)
            dve.wait_ge(bias_read, 2)
            n += exact_pieces(dve, nc, bias_q[:], bias_rest[:], [bias_qp[:, p, :] for p in range(3)], setup, n)
            nc.vector.tensor_copy(ident16[:], ident[:]).then_inc(setup, 1)
            nc.vector.memset(minus_max[:], 0.0).then_inc(max_done, MAX0)

            def step(b, s):
                unit, j = split(s)
                dve.wait_ge(s_ready, b * BATCH_STEPS + s + 1)
                nc.vector.tensor_reduce(half_max[unit % 2][:, j:j + 1], s_bank[s % S_BANKS][:], AX.X, ALU.max).then_inc(max_done, 1)
                if j == STEPS - 1:
                    dve.wait_ge(max_done, b * BATCH_STEPS + s + 1 + MAX0)
                    dve.wait_ge(shift_done, b * (4 * UNITS) + 4 * unit)
                    nc.vector.tensor_reduce(minus_max[:], half_max[unit % 2][:].rearrange("p (r k) -> p r k", k=2),
                                            AX.X, ALU.max, negate=True).then_inc(row_max_done, 1)

            for s in range(LEAD):
                step(0, s)
            with dve.Fori(0, B - 1) as b:
                for s in range(LEAD, BATCH_STEPS):
                    step(b, s)
                for s in range(LEAD):
                    step(b + 1, s)
            for s in range(LEAD, BATCH_STEPS):
                step(B - 1, s)

        @block.gpsimd
        def _(pool):
            counts = [pool.alloc_register(f"counts_b{k}") for k in range(2)]
            with pool.Fori(0, B * UNITS) as n:
                wait_apart(pool, counts, (setup, 13), (row_max_done, n + 1), (shift_turned, n))
                nc.gpsimd.tensor_copy(shift[:, 0, :], minus_max[:]).then_inc(shift_done, 1)
                pool.wait_ge(shift_done, n * 4 + 1)
                nc.gpsimd.tensor_tensor(shift_rest[:], minus_max[:], shift[:, 0, :], ALU.subtract).then_inc(shift_done, 1)
                wait_apart(pool, counts, (setup, 13), (shift_done, n * 4 + 2))
                nc.gpsimd.tensor_copy(shift[:, 1, :], shift_rest[:]).then_inc(shift_done, 1)
                pool.wait_ge(shift_done, n * 4 + 3)
                nc.gpsimd.tensor_tensor(shift[:, 2, :], shift_rest[:], shift[:, 1, :], ALU.subtract).then_inc(shift_done, 1)

        @block.scalar
        def _(act):
            for half in range(2):
                act.wait_ge(bias_ready, half + 1)
                nc.scalar.copy(bias_q[:, half * CHUNK:(half + 1) * CHUNK], [misc, pv_bank][half][:]).then_inc(bias_read, 1)
            act.wait_ge(tables_in, 48)
            nc.scalar.copy(unit_out[:, 0:1], ident[:, 0:1]).then_inc(exp_done, EXP0)

            def shift_copy(n):
                act.wait_ge(shift_turned, n + 1)
                act.wait_ge(shift_in, n * 48)
                nc.scalar.copy(shiftT[:], misc[0:48, 0:P]).then_inc(shiftT_done, 1)

            def out_copy(n):
                act.wait_ge(pv_done, n * (STEPS // HG) + STEPS // HG + PV0)
                act.wait_ge(out_turned, n)
                nc.scalar.copy(unit_out[:], pv_bank[:]).then_inc(unit_out_done, 1)

            def rows_copy(n):
                act.wait_ge(out_turned, n + 1)
                act.wait_ge(rows_stored, n * 16)
                nc.scalar.copy(unit_rows[:], misc[:].rearrange("p (t h c) -> p t h c", t=PER, h=HG)[:, :, :, 0:HD + 1]).then_inc(rows_done, 1)

            shift_copy(0)

            def batch(b, last):
                for u in range(UNITS):
                    n = b * UNITS + u
                    for j in range(STEPS):
                        s = STEPS * u + j
                        act.wait_ge(st_ready, b * BATCH_STEPS + s + 1)
                        if j % HG == 0:
                            act.wait_ge(pv_done, b * (BATCH_STEPS // HG) + s // HG + 1)
                        nc.scalar.activation(probs[:, s % P_SLOTS, :], st_bank[s % ST_BANKS][:], ACT.Exp).then_inc(exp_done, 1)
                        if u >= 1 and j == J_UOUT:
                            out_copy(n - 1)
                        if u >= 1 and j == J_OCOPY:
                            rows_copy(n - 1)
                        if j == J_MCOPY and (u < UNITS - 1 or not last):
                            shift_copy(n + 1)
                out_copy(b * UNITS + UNITS - 1)
                rows_copy(b * UNITS + UNITS - 1)

            with act.Fori(0, B - 1) as b:
                batch(b, False)
            batch(B - 1, True)

        @block.tensor
        def _(pe):
            pe.wait_ge(w_in, 16 * 16)
            pe.wait_ge(tables_in, 48)
            for half in range(2):
                nc.tensor.matmul([misc, pv_bank][half][:], wrow[:], tabq[:, half * CHUNK:(half + 1) * CHUNK],
                                 start=True, stop=True).then_inc(bias_ready, 1)
            pe.wait_ge(setup, 13)
            pe.wait_ge(bias_rows_in, 16 * 2 * GROUPS * len(TERMS) * HG)
            pe.wait_ge(bias_read, 2)
            nc.tensor.matmul(misc[0:32, 0:P], ident16[:, 0:32], ident16[:], start=True, stop=True).then_inc(pv_done, PV0)

            def score(b, base, s):
                unit, j = split(s)
                g, half = unit // 2, unit % 2
                h, tile, keys = j // 8, j // 2 % 4, j % 2
                if j == 0 and half == 0:
                    pe.wait_ge(loaded[g], b * LOAD + LOAD)
                pe.wait_ge(max_done, base + before(s, S_BANKS) + 1 + MAX0)
                nc.tensor.matmul(s_bank[s % S_BANKS][:], q_stack[g][0:SCORE_ROWS, half, h, tile * P:(tile + 1) * P],
                                 k_stack[g][0:SCORE_ROWS, keys, h, :], start=True, stop=True).then_inc(s_ready, 1)

            def score_t(b, s):
                unit, j = split(s)
                g, half = unit // 2, unit % 2
                tile, h = j // HG, j % HG
                if j == 0:
                    pe.wait_ge(shift_in, b * (UNITS * 48) + (unit + 1) * 48)
                pe.wait_ge(exp_done, b * BATCH_STEPS + before(s, ST_BANKS) + 1 + EXP0)
                nc.tensor.matmul(st_bank[s % ST_BANKS][:], k_stack[g][:, tile // 4, h, tile % 4 * P:(tile % 4 + 1) * P],
                                 q_stack[g][:, half, h, :], start=True, stop=True).then_inc(st_ready, 1)

            def times_values(b, unit, tile):
                s = STEPS * unit + HG * tile
                pe.wait_ge(exp_done, b * BATCH_STEPS + s + HG + EXP0)
                if tile == 0:
                    pe.wait_ge(unit_out_done, b * UNITS + unit)
                for h in range(HG):
                    mm = nc.tensor.matmul(pv_bank[VW * h:VW * (h + 1), :], values[unit // 2][:, tile, h, :],
                                          probs[:, (s + h) % P_SLOTS, :], start=(tile == 0), stop=(tile == T // P - 1),
                                          tile_position=(0, VW * h))
                mm.then_inc(pv_done, 1)

            def turn_out(n, shifts):
                pe.wait_ge(unit_out_done, n + 1)
                pe.wait_ge(shiftT_done, shifts)
                for t in range(PER):
                    mm = nc.tensor.transpose(misc[:, t * P:(t + 1) * P], unit_out[:, t * P:(t + 1) * P], ident[:])
                mm.then_inc(out_turned, 1)

            def turn_shift(n, rows):
                pe.wait_ge(shift_done, n * 4 + 4)
                pe.wait_ge(rows_done, rows)
                nc.tensor.matmul(misc[0:48, 0:P], shift[:].rearrange("p c r -> p (c r)"), ident16[:],
                                 start=True, stop=True).then_inc(shift_turned, 1)

            for s in range(LEAD):
                score(0, 0, s)
            turn_shift(0, 0)

            def batch(b, last):
                base = b * BATCH_STEPS if last else pe.snap(score_count, min_val=0, max_val=B * BATCH_STEPS)
                for u in range(UNITS + 1):
                    for j in range(STEPS):
                        s = STEPS * u + j
                        if u < UNITS:
                            score_t(b, s)
                            if s + LEAD < BATCH_STEPS:
                                score(b, base, s + LEAD)
                            elif not last:
                                score(b + 1, base + BATCH_STEPS, s + LEAD - BATCH_STEPS)
                        done = s - PV_LAG
                        if done >= 0 and done % HG == HG - 1 and done < BATCH_STEPS:
                            unit, jj = split(done)
                            times_values(b, unit, jj // HG)
                        if u >= 1 and j == J_OTURN:
                            turn_out(b * UNITS + u - 1, b * UNITS + (u if last and u == UNITS else u + 1))
                        if u < UNITS and j == J_MTURN and (u < UNITS - 1 or not last):
                            turn_shift(b * UNITS + u + 1, b * UNITS + u)

            score_count = pe.alloc_register("score_count")
            pe.reg_mov(score_count, 0)
            with pe.Fori(0, B - 1) as b:
                batch(b, False)
                pe.reg_add(score_count, score_count, BATCH_STEPS)
            batch(B - 1, True)


E, TOPK, NGROUPS, TOPG = 64, 8, 8, 4
GE = E // NGROUPS
CAP = 128
F = 64
ROUTE_SCALE = 2.5
ROW = DIM + E
ROWS = N + CAP
BIG = 1e30
STEPS_C = 97


def inverse_std(pool, nc, out, var, minus_half, tmp, done, count):
    nc.gpsimd.tensor_scalar(tmp, var, EPS, None, ALU.add).then_inc(done, 1)
    pool.wait_ge(done, count + 1)
    nc.gpsimd.tensor_tensor(out, tmp, minus_half, ALU.pow).then_inc(done, 1)


def route(nc, x, att, w_out, b_out, gate_t, e_bias, shared_gate_t, shared_up_t, shared_down_t,
          ident_in, before_in, iota_in, x1, table, sums, slot_ids):
    with ExitStack() as ctx:
        sb = lambda name, shape, dt=F32: ctx.enter_context(nc.sbuf_tensor(name, shape, dt))
        ps = lambda name: ctx.enter_context(nc.psum_tensor(name, [P, CHUNK], F32))
        sem = lambda name: ctx.enter_context(nc.semaphore(name))

        ident = sb("identC", [P, P])
        before_f = sb("before_f", [P, P])
        before = sb("before", [P, P], BF16)
        ones = sb("ones", [P, P], BF16)
        iota = sb("iota", [P, P])
        w_o = sb("w_o", [P, DIM])
        b_o = sb("b_o", [P, DIM])
        gate = sb("gate", [P, E])
        bias = sb("bias", [P, E])
        s_gate = sb("s_gate", [P, P])
        s_up = sb("s_up", [P, P])
        s_down = sb("s_down", [P, P])
        minus_half = sb("minus_half", [P, PER])
        earlier = sb("earlier", [P, NGROUPS, NGROUPS])
        token_lo = sb("token_lo", [P, 1])
        tile_no = sb("tile_no", [P, PER])
        expert_1 = sb("expert_1", [P, E])

        attc = sb("attc", [P, PER, H, HD + 1])
        xc = sb("xcC", [P, PER, DIM])
        recip = sb("recip", [P, PER, H])
        normed = sb("normed", [P, PER, DIM])
        turned_sb = sb("turned_sb", [P, CHUNK])
        y = sb("y", [P, PER, DIM])
        stats = sb("statsC", [P, PER, 6])
        mv = sb("mvC", [P, PER, 2])
        veps = sb("veps", [P, PER])
        rstd = sb("rstdC", [P, PER])
        x1c = sb("x1c", [P, PER, DIM])
        rows = sb("rows", [P, PER, ROW])
        xfT = sb("xfT", [P, CHUNK])
        scores = sb("scores", [P, PER, E])
        sg = sb("sg", [P, CHUNK])
        sh = sb("sh", [P, CHUNK])
        shared = sb("shared", [P, PER, DIM])
        sfc = sb("sfc", [P, PER, E])
        top1 = sb("top1", [P, PER * NGROUPS])
        is_top = sb("is_top", [P, PER, E])
        count = sb("count", [P, PER * NGROUPS])
        second = sb("second", [P, PER * NGROUPS])
        gsum = sb("gsum", [P, PER, NGROUPS])
        above = sb("above", [P, PER, NGROUPS, NGROUPS])
        same = sb("same", [P, PER, NGROUPS, NGROUPS])
        grank = sb("grank", [P, PER * NGROUPS])
        tmp = sb("tmp", [P, PER, E])
        best = sb("best", [P, PER, TOPK])
        marked = sb("marked", [P, PER, E])
        chosen = sb("chosen", [P, PER, E])
        chosen16 = sb("chosen16", [P, PER, E], BF16)
        picked = sb("picked", [P, PER, E])
        wsum = sb("wsum", [P, PER])
        wrec = sb("wrec", [P, PER])
        sofar = sb("sofar", [P, E], BF16)
        key = sb("key", [P, PER, E])
        keys = sb("keys", [P, PER * TOPK])
        keys_i = sb("keys_i", [P, PER * TOPK], U32)
        part_i = sb("part_i", [P, 2, PER * TOPK], U32)
        part = sb("part", [P, 2, PER * TOPK])
        hot_e = sb("hot_e", [P, PER * TOPK, E], BF16)
        id_parts = sb("id_parts", [P, PER * TOPK, 2, E], BF16)
        hot_s = sb("hot_s", [P, PER * TOPK, CAP], BF16)
        ids = sb("ids", [P, 2, E])
        zeros = sb("zeros", [P, DIM * (ROWS // P)])
        free_id = sb("free_id", [P, 1])
        is_free = sb("is_free", [P, E])
        ids_u = sb("ids_u", [P, E], U32)

        psA, psB, psC, psD, psE, psF, psG = [ps(f"psC{i}") for i in range(7)]

        v = sem("dve_steps")
        consts_in = sem("consts_inC")
        loaded = sem("loadedC")
        attT_turned, attT_done = sem("attT_turned"), sem("attT_done")
        projected = sem("projected")
        var_ready, rstd_ready = sem("var_ready"), sem("rstd_ready")
        xf_turned, xfT_ready = sem("xf_turned"), sem("xfT_ready")
        logits_ready, scores_ready = sem("logits_ready"), sem("scores_ready")
        shared_gu, shared_sig = sem("shared_gu"), sem("shared_sig")
        shared_ready, shared_copied = sem("shared_ready"), sem("shared_copied")
        ranks_ready = sem("ranks_ready")
        ids_ready = sem("ids_ready")
        stored = sem("storedC")
        cleared = sem("cleared")
        init_p = sem("init_p")

        block = ctx.enter_context(nc.Block())
        NCONST = 12
        at = {}

        def vector(dve):
            base = [0]
            n = [0]

            def step(ins, name=None, plain_next=False):
                ins.then_inc(v, 1)
                n[0] += 1
                if name:
                    at[name] = n[0]
                if plain_next:
                    wait_apart(dve, counts, (init_p, 1), (v, base[0] + n[0]))
                else:
                    dve.wait_ge(v, base[0] + n[0])

            V = nc.vector
            counts = [dve.alloc_register(f"counts_c{k}") for k in range(1)]
            dve.wait_ge(consts_in, 16 * NCONST)
            step(V.memset(ones[:], 1.0))
            step(V.tensor_copy(before[:], before_f[:]))
            step(V.memset(sofar[:], 0.0))
            step(V.memset(ids[:], 0.0))
            step(V.memset(zeros[:], 0.0))
            step(V.tensor_scalar(expert_1[:], iota[:, 0:E], 1.0, None, ALU.add))
            for g in range(NGROUPS):
                step(V.tensor_scalar(earlier[:, g, :], iota[:, 0:NGROUPS], float(g), None, ALU.is_lt))
            at["setup"] = setup = n[0]
            dve.wait_ge(init_p, 1 + PER)

            def norm(x_, names):
                for j in range(PER):
                    step(V.bn_stats(stats[:, j, :], x_[:, j, :]), plain_next=(j == PER - 1))
                for j in range(PER):
                    step(V.bn_aggr(mv[:, j, :], stats[:, j, :]), names if j == PER - 1 else None, plain_next=(j < PER - 1))

            with dve.Fori(0, CHUNKS) as i:
                n[0] = 0
                per = STEPS_C
                base[0] = i * per + setup
                dve.wait_ge(loaded, i * 32 + 32)
                step(V.reciprocal(recip[:], attc[:, :, :, HD]))
                step(V.tensor_tensor(normed[:].rearrange("p j (h d) -> p (j h) d", h=H),
                                     attc[:].rearrange("p j h c -> p (j h) c")[:, :, 0:HD],
                                     recip[:].rearrange("p j (h o) -> p (j h) o", o=1).to_broadcast([P, PER * H, HD]),
                                     ALU.mult), "normed")
                dve.wait_ge(projected, i + 1)
                step(V.tensor_tensor(y[:], psB[:].rearrange("p (j d) -> p j d", j=PER),
                                     b_o[:].rearrange("p (o d) -> p o d", o=1).to_broadcast([P, PER, DIM]), ALU.add), "y")
                norm(y, "var_y")
                dve.wait_ge(rstd_ready, i * 4 + 2)
                for j in range(PER):
                    step(V.tensor_scalar(y[:, j, :], y[:, j, :], mv[:, j, 0:1], rstd[:, j:j + 1], ALU.subtract, ALU.mult))
                dve.wait_ge(stored, i * 48)
                step(V.tensor_tensor(x1c[:], xc[:], y[:], ALU.add), "x1")
                norm(x1c, "var_x1")
                dve.wait_ge(rstd_ready, i * 4 + 4)
                for j in range(PER):
                    step(V.tensor_scalar(rows[:, j, 0:DIM], x1c[:, j, :], mv[:, j, 0:1], rstd[:, j:j + 1],
                                         ALU.subtract, ALU.mult), "xf")
                dve.wait_ge(shared_sig, i + 1)
                step(V.tensor_tensor(sh[:], psD[:], sg[:], ALU.mult))
                step(V.tensor_tensor(sh[:], psE[:], sh[:], ALU.mult), "shared_h")
                dve.wait_ge(scores_ready, i + 1)
                by_group = lambda a: a.rearrange("p j (g e) -> p (j g) e", e=GE)
                spread = lambda a: a.rearrange("p (g o) -> p g o", o=1).to_broadcast([P, PER * NGROUPS, GE])
                step(V.tensor_tensor(sfc[:], scores[:], bias[:].rearrange("p (o e) -> p o e", o=1).to_broadcast([P, PER, E]), ALU.add))
                step(V.tensor_reduce(top1[:], by_group(sfc[:]), AX.X, ALU.max))
                step(V.tensor_tensor(by_group(is_top[:]), by_group(sfc[:]), spread(top1[:]), ALU.is_equal))
                step(V.tensor_reduce(count[:], by_group(is_top[:]), AX.X, ALU.add))
                step(V.scalar_tensor_tensor(out=tmp[:], in0=is_top[:], scalar=-BIG, in1=sfc[:], op0=ALU.mult, op1=ALU.add))
                step(V.tensor_reduce(second[:], by_group(tmp[:]), AX.X, ALU.max))
                step(V.tensor_scalar(count[:], count[:], 2.0, -BIG, ALU.is_lt, ALU.mult))
                step(V.tensor_tensor(count[:], count[:], top1[:], ALU.add))
                step(V.tensor_tensor(second[:], second[:], count[:], ALU.max))
                flat = gsum[:].rearrange("p j g -> p (j g)")
                step(V.tensor_tensor(flat, top1[:], second[:], ALU.add))
                for j in range(PER):
                    mine = gsum[:, j, :].rearrange("p (g o) -> p g o", o=1).to_broadcast([P, NGROUPS, NGROUPS])
                    other = gsum[:, j, :].rearrange("p (o g) -> p o g", o=1).to_broadcast([P, NGROUPS, NGROUPS])
                    step(V.tensor_tensor(above[:, j], other, mine, ALU.is_gt))
                    step(V.tensor_tensor(same[:, j], other, mine, ALU.is_equal))
                    step(V.tensor_tensor(same[:, j], same[:, j], earlier[:], ALU.mult))
                step(V.tensor_tensor(above[:], above[:], same[:], ALU.add))
                step(V.tensor_reduce(grank[:], above[:].rearrange("p j g o -> p (j g) o"), AX.X, ALU.add))
                step(V.tensor_scalar(grank[:], grank[:], float(TOPG), None, ALU.is_lt))
                step(V.tensor_tensor(by_group(tmp[:]), by_group(sfc[:]), spread(grank[:]), ALU.mult), plain_next=True)
                for j in range(PER):
                    step(V.max(best[:, j, :], tmp[:, j, :]), plain_next=True)
                for j in range(PER):
                    step(V.match_replace(marked[:, j, :], best[:, j, :], tmp[:, j, :], -BIG), plain_next=(j < PER - 1))
                step(V.tensor_scalar(chosen[:], marked[:], -0.5 * BIG, None, ALU.is_lt))
                step(V.tensor_copy(chosen16[:], chosen[:]), "chosen")
                step(V.tensor_tensor(picked[:], scores[:], chosen[:], ALU.mult))
                step(V.tensor_reduce(wsum[:], picked[:], AX.X, ALU.add))
                step(V.tensor_scalar(wsum[:], wsum[:], 1e-20, None, ALU.add))
                step(V.reciprocal(wrec[:], wsum[:]))
                for j in range(PER):
                    step(V.tensor_scalar(rows[:, j, DIM:ROW], picked[:, j, :], wrec[:, j:j + 1], ROUTE_SCALE,
                                         ALU.mult, ALU.mult), "weights")
                dve.wait_ge(ranks_ready, i + 1)
                step(V.scalar_tensor_tensor(out=key[:], in0=psC[:, 0:PER * E].rearrange("p (j e) -> p j e", j=PER), scalar=float(E),
                                            in1=expert_1[:].rearrange("p (o e) -> p o e", o=1).to_broadcast([P, PER, E]),
                                            op0=ALU.mult, op1=ALU.add))
                for j in range(PER):
                    step(V.tensor_tensor(sofar[:], sofar[:], chosen16[:, j, :], ALU.add))
                step(V.tensor_tensor(key[:], key[:], chosen[:], ALU.mult), plain_next=True)
                for j in range(PER):
                    step(V.max(keys[:, j * TOPK:(j + 1) * TOPK], key[:, j, :]), plain_next=(j < PER - 1))
                step(V.tensor_scalar(keys_i[:], keys[:], -1.0, None, ALU.add))
                step(V.tensor_scalar(part_i[:, 0, :], keys_i[:], E - 1, None, ALU.bitwise_and))
                step(V.tensor_scalar(part_i[:, 1, :], keys_i[:], E.bit_length() - 1, None, ALU.logical_shift_right))
                step(V.tensor_copy(part[:], part_i[:]), "part")
                step(V.tensor_tensor(hot_e[:], iota[:, 0:E].rearrange("p (o e) -> p o e", o=1).to_broadcast([P, PER * TOPK, E]),
                                     part[:, 0, :].rearrange("p (k o) -> p k o", o=1).to_broadcast([P, PER * TOPK, E]), ALU.is_equal))
                step(V.tensor_scalar(id_parts[:, :, 0, :], hot_e[:], token_lo[:], None, ALU.mult))
                for j in range(PER):
                    ks = slice(j * TOPK, (j + 1) * TOPK)
                    step(V.tensor_scalar(id_parts[:, ks, 1, :], hot_e[:, ks, :], tile_no[:, j:j + 1], None, ALU.mult), "id_parts")
                step(V.tensor_tensor(hot_s[:], iota[:].rearrange("p (o s) -> p o s", o=1).to_broadcast([P, PER * TOPK, CAP]),
                                     part[:, 1, :].rearrange("p (k o) -> p k o", o=1).to_broadcast([P, PER * TOPK, CAP]), ALU.is_equal), "hot")
                step(V.tensor_scalar(tile_no[:], tile_no[:], float(PER), None, ALU.add))
                dve.wait_ge(ids_ready, i + 1)
                step(V.tensor_tensor(ids[:].rearrange("p a e -> p (a e)"), psF[:, 0:2 * E], ids[:].rearrange("p a e -> p (a e)"), ALU.add), "ids")
                at["per"] = n[0]
                assert n[0] == STEPS_C, n[0]
            n[0] = 0
            base[0] = setup + CHUNKS * STEPS_C
            step(V.tensor_scalar(is_free[:], ids[:, 0, :], 0.0, None, ALU.is_equal))
            step(V.tensor_scalar(is_free[:], is_free[:], free_id[:], None, ALU.mult))
            step(V.scalar_tensor_tensor(out=ids[:, 1, :], in0=ids[:, 1, :], scalar=float(P), in1=ids[:, 0, :], op0=ALU.mult, op1=ALU.add))
            step(V.tensor_tensor(ids[:, 1, :], ids[:, 1, :], is_free[:], ALU.add))
            step(V.tensor_scalar(ids_u[:], ids[:, 1, :], -1.0, None, ALU.add), "ids_u")

        block.vector(vector)

        def v_at(i, name):
            return i * STEPS_C + at["setup"] + at[name]

        @block.sync
        def _(sp):
            row = lambda a, n_: a.rearrange("(o d) -> o d", o=1).to_broadcast([P, n_])
            for dst, src in ((ident[:], ident_in), (before_f[:], before_in), (iota[:], iota_in[0:1, :].to_broadcast([P, P])),
                             (token_lo[:], iota_in[1:2, :].rearrange("o p -> p o")), (free_id[:], iota_in[2:3, :].rearrange("o p -> p o")),
                             (w_o[:], w_out), (b_o[:], row(b_out, DIM)), (gate[:], gate_t), (bias[:], row(e_bias, E)),
                             (s_gate[:], shared_gate_t), (s_up[:], shared_up_t), (s_down[:], shared_down_t)):
                sp.dma_start(dst, src, allow_slow_non_contiguous=True).then_inc(consts_in, 16)
            sp.wait_ge(v, at["setup"])
            for k in range(1, 4):
                sp.dma_start(sums[k].rearrange("(p r) d -> p (r d)", p=P), zeros[:]).then_inc(cleared, 16)
            sp.dma_start(sums[0][N:ROWS, :], zeros[:, 0:DIM]).then_inc(cleared, 16)
            sp.dma_start(table[N:ROWS, :], zeros[:, 0:ROW]).then_inc(cleared, 16)
            with sp.Fori(0, CHUNKS) as i:
                tok = bass.ds(i * CHUNK, CHUNK)
                sp.dma_start(attc[:].rearrange("p j h c -> p j (h c)"), att[tok].rearrange("(j p) h c -> p j (h c)", p=P)).then_inc(loaded, 16)
                sp.dma_start(xc[:], x[tok, :].rearrange("(j p) d -> p j d", p=P)).then_inc(loaded, 16)
                sp.wait_ge(v, v_at(i, "x1"))
                sp.dma_start(x1[tok, :].rearrange("(j p) d -> p j d", p=P), x1c[:]).then_inc(stored, 16)
                sp.wait_ge(shared_copied, i + 1)
                sp.dma_start(sums[0][tok, :].rearrange("(j p) d -> p j d", p=P), shared[:]).then_inc(stored, 16)
                sp.wait_ge(v, v_at(i, "weights"))
                sp.dma_start(table[tok, :].rearrange("(j p) d -> p j d", p=P), rows[:]).then_inc(stored, 16)
            sp.wait_ge(v, STEPS_C * CHUNKS + at["setup"] + at["ids_u"])
            sp.dma_start(slot_ids, ids_u[:]).then_inc(stored, 16)
            sp.wait_ge(stored, CHUNKS * 48 + 16)
            sp.wait_ge(cleared, 16 * 5)

        @block.gpsimd
        def _(pool):
            G = nc.gpsimd
            counts = [pool.alloc_register(f"counts_cp{k}") for k in range(1)]
            G.memset(minus_half[:], -0.5).then_inc(init_p, 1)
            pool.wait_ge(init_p, 1)
            for j in range(PER):
                G.memset(tile_no[:, j:j + 1], float(j)).then_inc(init_p, 1)
            with pool.Fori(0, CHUNKS) as i:
                wait_apart(pool, counts, (init_p, 1), (v, v_at(i, "var_y")))
                inverse_std(pool, nc, rstd[:], mv[:, :, 1], minus_half[:], veps[:], rstd_ready, i * 4)
                wait_apart(pool, counts, (init_p, 1), (v, v_at(i, "var_x1")))
                inverse_std(pool, nc, rstd[:], mv[:, :, 1], minus_half[:], veps[:], rstd_ready, i * 4 + 2)

        @block.scalar
        def _(act):
            act.wait_ge(consts_in, 16 * NCONST)
            with act.Fori(0, CHUNKS) as i:
                act.wait_ge(attT_turned, i + 1)
                nc.scalar.copy(turned_sb[:], psA[:]).then_inc(attT_done, 1)
                act.wait_ge(xf_turned, i + 1)
                nc.scalar.copy(xfT[:], psA[:]).then_inc(xfT_ready, 1)
                act.wait_ge(logits_ready, i + 1)
                nc.scalar.activation(scores[:].rearrange("p j e -> p (j e)"), psG[:, 0:PER * E], ACT.Sigmoid).then_inc(scores_ready, 1)
                act.wait_ge(shared_gu, i + 1)
                nc.scalar.activation(sg[:], psD[:], ACT.Sigmoid).then_inc(shared_sig, 1)
                act.wait_ge(shared_ready, i + 1)
                act.wait_ge(stored, i * 48)
                nc.scalar.copy(shared[:].rearrange("p j d -> p (j d)"), psB[:]).then_inc(shared_copied, 1)

        @block.tensor
        def _(pe):
            pe.wait_ge(consts_in, 16 * NCONST)
            M = nc.tensor.matmul

            def turn(src, done):
                for j in range(PER):
                    mm = nc.tensor.transpose(psA[:, j * P:(j + 1) * P], src(j), ident[:])
                mm.then_inc(done, 1)

            def by_tile(bank, src, w, done, width=P):
                for j in range(PER):
                    mm = M(bank[:, j * width:(j + 1) * width], src[:, j * P:(j + 1) * P], w, start=True, stop=True)
                mm.then_inc(done, 1)

            with pe.Fori(0, CHUNKS) as i:
                pe.wait_ge(v, v_at(i, "normed"))
                pe.wait_ge(xfT_ready, i)
                turn(lambda j: normed[:, j, :], attT_turned)
                pe.wait_ge(attT_done, i + 1)
                pe.wait_ge(shared_copied, i)
                by_tile(psB, turned_sb, w_o[:], projected)
                pe.wait_ge(v, v_at(i, "xf"))
                turn(lambda j: rows[:, j, 0:DIM], xf_turned)
                pe.wait_ge(xfT_ready, i + 1)
                by_tile(psG, xfT, gate[:], logits_ready, E)
                M(psD[:], s_gate[:], xfT[:], start=True, stop=True)
                M(psE[:], s_up[:], xfT[:], start=True, stop=True).then_inc(shared_gu, 1)
                pe.wait_ge(v, v_at(i, "shared_h"))
                by_tile(psB, sh, s_down[:], shared_ready)
                pe.wait_ge(v, v_at(i, "chosen"))
                for j in range(PER):
                    out = psC[:, j * E:(j + 1) * E]
                    M(out, before[:], chosen16[:, j, :], start=True, stop=False)
                    for jj in range(j):
                        M(out, ones[:], chosen16[:, jj, :], start=False, stop=False)
                    mm = M(out, ones[:], sofar[:], start=False, stop=True)
                mm.then_inc(ranks_ready, 1)
                pe.wait_ge(v, v_at(i, "hot"))
                for k in range(PER * TOPK):
                    mm = M(psF[:, 0:2 * E], hot_s[:, k, :], id_parts[:, k].rearrange("p a e -> p (a e)"),
                           start=(k == 0), stop=(k == PER * TOPK - 1))
                mm.then_inc(ids_ready, 1)


def run_experts(nc, table, slot_ids, w1_t, w3_t, w2_t, ident_in, sums):
    Q = 4
    with ExitStack() as ctx:
        sb = lambda name, shape, dt=F32: ctx.enter_context(nc.sbuf_tensor(name, shape, dt))
        ps = lambda name: ctx.enter_context(nc.psum_tensor(name, [P, CHUNK], F32))
        sem = lambda name: ctx.enter_context(nc.semaphore(name))
        ident = sb("identD", [P, P])
        ids = sb("idsD", [P, E], U32)
        ids_g = sb("ids_g", [P, Q], U32)
        ids_s = sb("ids_s", [P, Q], U32)
        xe = sb("xe", [P, Q, ROW])
        w_cur = sb("w_cur", [P, Q])
        xeT = sb("xeT", [P, Q * P])
        w1 = sb("w1", [P, Q * F])
        w3 = sb("w3", [P, Q * F])
        w2 = sb("w2", [P, Q // 2, DIM])
        gsig = sb("gsig", [P, 2 * P])
        h = sb("h", [P, 2 * P])
        out = sb("out", [P, Q, DIM])
        psX, psH1, psH3, psY0, psY1 = [ps(f"psD{i}") for i in range(5)]
        c_in, w_in, g_in = sem("c_inD"), sem("w_inD"), sem("g_inD")
        ids_g_ready, ids_s_ready, w_ready = sem("ids_g_ready"), sem("ids_s_ready"), sem("w_ready")
        turned, xeT_ready, up_ready, sig_ready = sem("turnedD"), sem("xeT_ready"), sem("up_ready"), sem("sig_ready")
        half_ready, h_ready, y_ready, out_ready = sem("half_ready"), sem("h_ready"), sem("y_ready"), sem("out_ready")
        added = [sem(f"added{k}") for k in range(Q)]
        block = ctx.enter_context(nc.Block())
        ROUNDS = E // Q

        @block.sync
        def _(sp):
            sp.dma_start(ident[:], ident_in).then_inc(c_in, 16)
            sp.dma_start(ids[:], slot_ids).then_inc(c_in, 16)
            with sp.Fori(0, ROUNDS) as i:
                sp.wait_ge(y_ready, i)
                sp.dma_start(w1[:], w1_t[:, bass.ds(i * Q * F, Q * F)]).then_inc(w_in, 16)
                sp.dma_start(w3[:], w3_t[:, bass.ds(i * Q * F, Q * F)]).then_inc(w_in, 16)
                sp.dma_start(w2[:], w2_t[bass.ds(i * Q * F, Q * F), :].rearrange("(m p) d -> p m d", p=P)).then_inc(w_in, 16)

        @block.gpsimd
        def _(pool):
            counts = [pool.alloc_register(f"counts_d{k}") for k in range(3)]
            with pool.Fori(0, ROUNDS) as i:
                wait_apart(pool, counts, (c_in, 32), (ids_g_ready, i + 1), (turned, i), (w_ready, i * Q))
                for k in range(Q):
                    pool.indirect_dma_start(out=xe[:, k, :], out_offset=None, in_=table,
                                            in_offset=bass.IndirectOffsetOnAxis(ap=ids_g[:, k:k + 1], axis=0)).then_inc(g_in, 16)
                for k in range(Q):
                    wait_apart(pool, counts, (c_in, 32), (ids_s_ready, i + 1), (out_ready, i * Q + k + 1), (added[k], i * 16))
                    pool.indirect_dma_start(out=sums[k], out_offset=bass.IndirectOffsetOnAxis(ap=ids_s[:, k:k + 1], axis=0),
                                            in_=out[:, k, :], in_offset=None, compute_op=ALU.add).then_inc(added[k], 16)
            for k in range(Q):
                pool.wait_ge(added[k], ROUNDS * 16)

        @block.vector
        def _(dve):
            dve.wait_ge(c_in, 32)
            counts = [dve.alloc_register(f"counts_dv{k}") for k in range(4)]
            with dve.Fori(0, ROUNDS) as i:
                wait_apart(dve, counts, (c_in, 32), (g_in, i * 64))
                nc.vector.tensor_copy(ids_g[:], ids[:, bass.ds(i * Q, Q)]).then_inc(ids_g_ready, 1)
                wait_apart(dve, counts, (c_in, 32), *((added[k], i * 16) for k in range(Q)))
                nc.vector.tensor_copy(ids_s[:], ids[:, bass.ds(i * Q, Q)]).then_inc(ids_s_ready, 1)
                wait_apart(dve, counts, (c_in, 32), (g_in, i * 64 + 64), (out_ready, i * Q))
                for k in range(Q):
                    nc.vector.tensor_copy(w_cur[:, k:k + 1], xe[:, k, bass.ds(i * Q + (DIM + k), 1)]).then_inc(w_ready, 1)
                dve.wait_ge(sig_ready, i + 1)
                dve.wait_ge(y_ready, i)
                nc.vector.tensor_tensor(h[:], psH1[:, 0:2 * P], gsig[:], ALU.mult).then_inc(half_ready, 1)
                dve.wait_ge(half_ready, i + 1)
                nc.vector.tensor_tensor(h[:], psH3[:, 0:2 * P], h[:], ALU.mult).then_inc(h_ready, 1)

        @block.scalar
        def _(act):
            with act.Fori(0, ROUNDS) as i:
                act.wait_ge(turned, i + 1)
                act.wait_ge(up_ready, i)
                nc.scalar.copy(xeT[:], psX[:]).then_inc(xeT_ready, 1)
                act.wait_ge(up_ready, i + 1)
                act.wait_ge(half_ready, i)
                nc.scalar.activation(gsig[:], psH1[:, 0:2 * P], ACT.Sigmoid).then_inc(sig_ready, 1)
                act.wait_ge(y_ready, i + 1)
                act.wait_ge(w_ready, i * Q + Q)
                for k in range(Q):
                    act.wait_ge(added[k], i * 16)
                    nc.scalar.activation(out[:, k, :], [psY0, psY1][k % 2][:, k // 2 * P:(k // 2 + 1) * P], ACT.Identity,
                                         scale=w_cur[:, k:k + 1]).then_inc(out_ready, 1)

        @block.tensor
        def _(pe):
            M = nc.tensor.matmul
            pe.wait_ge(c_in, 32)
            with pe.Fori(0, ROUNDS) as i:
                pe.wait_ge(g_in, i * 64 + 64)
                pe.wait_ge(xeT_ready, i)
                for k in range(Q):
                    mm = nc.tensor.transpose(psX[:, k * P:(k + 1) * P], xe[:, k, 0:DIM], ident[:])
                mm.then_inc(turned, 1)
                pe.wait_ge(xeT_ready, i + 1)
                pe.wait_ge(w_in, i * 48 + 48)
                pe.wait_ge(h_ready, i)
                for bank, w in ((psH1, w1), (psH3, w3)):
                    for k in range(Q):
                        a = F * (k % 2)
                        mm = M(bank[a:a + F, k // 2 * P:(k // 2 + 1) * P], w[:, k * F:(k + 1) * F], xeT[:, k * P:(k + 1) * P],
                               start=True, stop=True)
                mm.then_inc(up_ready, 1)
                pe.wait_ge(h_ready, i + 1)
                pe.wait_ge(out_ready, i * Q)
                for k in range(Q):
                    a = F * (k % 2)
                    m = k // 2
                    mm = M([psY0, psY1][k % 2][:, m * P:(m + 1) * P], h[a:a + F, m * P:(m + 1) * P], w2[a:a + F, m, :],
                           start=True, stop=True)
                mm.then_inc(y_ready, 1)


def finish(nc, x1, sums, out):
    with ExitStack() as ctx:
        sb = lambda name, shape, dt=F32: ctx.enter_context(nc.sbuf_tensor(name, shape, dt))
        sem = lambda name: ctx.enter_context(nc.semaphore(name))
        s = [[sb(f"s{k}_{a}", [P, PER, DIM]) for k in range(4)] for a in range(2)]
        x1c = [sb(f"x1f{a}", [P, PER, DIM]) for a in range(2)]
        res = [sb(f"res{a}", [P, PER, DIM]) for a in range(2)]
        stats = sb("statsE", [P, PER, 6])
        mv = sb("mvE", [P, PER, 2])
        veps = sb("vepsE", [P, PER])
        rstd = sb("rstdE", [P, PER])
        minus_half = sb("minus_halfE", [P, PER])
        v, rstd_ready, init_p = sem("vE"), sem("rstdE_ready"), sem("init_pE")
        loaded = [sem(f"loadedE{a}") for a in range(2)]
        stored = [sem(f"storedE{a}") for a in range(2)]
        block = ctx.enter_context(nc.Block())
        PERV = 3 + 3 * PER + 1

        @block.sync
        def _(sp):
            with sp.Fori(0, CHUNKS // 2) as i:
                for a in range(2):
                    tok = bass.ds(i * (2 * CHUNK) + a * CHUNK, CHUNK)
                    sp.wait_ge(v, i * (2 * PERV))
                    for k in range(4):
                        sp.dma_start(s[a][k][:], sums[k][tok, :].rearrange("(j p) d -> p j d", p=P)).then_inc(loaded[a], 16)
                    sp.dma_start(x1c[a][:], x1[tok, :].rearrange("(j p) d -> p j d", p=P)).then_inc(loaded[a], 16)

        @block.scalar
        def _(act):
            with act.Fori(0, CHUNKS // 2) as i:
                for a in range(2):
                    act.wait_ge(v, i * (2 * PERV) + (a + 1) * PERV)
                    tok = bass.ds(i * (2 * CHUNK) + a * CHUNK, CHUNK)
                    act.dma_start(out[tok, :].rearrange("(j p) d -> p j d", p=P), res[a][:]).then_inc(stored[a], 16)
            for a in range(2):
                act.wait_ge(stored[a], 16 * CHUNKS // 2)

        @block.gpsimd
        def _(pool):
            counts = [pool.alloc_register(f"counts_e{k}") for k in range(1)]
            nc.gpsimd.memset(minus_half[:], -0.5).then_inc(init_p, 1)
            pool.wait_ge(init_p, 1)
            with pool.Fori(0, CHUNKS) as c:
                wait_apart(pool, counts, (init_p, 1), (v, c * PERV + (3 + 2 * PER)))
                inverse_std(pool, nc, rstd[:], mv[:, :, 1], minus_half[:], veps[:], rstd_ready, c * 2)

        @block.vector
        def _(dve):
            V = nc.vector
            counts = [dve.alloc_register(f"counts_ev{k}") for k in range(1)]
            with dve.Fori(0, CHUNKS // 2) as i:
                n = [0]

                def step(ins, plain_next=False):
                    ins.then_inc(v, 1)
                    n[0] += 1
                    if plain_next:
                        wait_apart(dve, counts, (init_p, 1), (v, i * (2 * PERV) + n[0]))
                    else:
                        dve.wait_ge(v, i * (2 * PERV) + n[0])

                for a in range(2):
                    dve.wait_ge(loaded[a], i * 80 + 80)
                    step(V.tensor_tensor(s[a][0][:], s[a][0][:], s[a][1][:], ALU.add))
                    step(V.tensor_tensor(s[a][2][:], s[a][2][:], s[a][3][:], ALU.add))
                    step(V.tensor_tensor(s[a][0][:], s[a][0][:], s[a][2][:], ALU.add))
                    for j in range(PER):
                        step(V.bn_stats(stats[:, j, :], s[a][0][:, j, :]), plain_next=(j == PER - 1))
                    for j in range(PER):
                        step(V.bn_aggr(mv[:, j, :], stats[:, j, :]), plain_next=(j < PER - 1))
                    dve.wait_ge(rstd_ready, i * 4 + 2 * a + 2)
                    for j in range(PER):
                        step(V.tensor_scalar(s[a][0][:, j, :], s[a][0][:, j, :], mv[:, j, 0:1], rstd[:, j:j + 1], ALU.subtract, ALU.mult))
                    dve.wait_ge(stored[a], i * 16)
                    step(V.tensor_tensor(res[a][:], s[a][0][:], x1c[a][:], ALU.add))


def program(nc, x, ln_g, ln_b, w_qkv, b_qkv, w_rel, w_out, b_out, gate_t, e_bias, w1_t, w2_t, w3_t,
            shared_gate_t, shared_up_t, shared_down_t, q_table, k_table, ident, before, iota, out):
    dram = lambda name, shape, dt=F32: nc.dram_tensor(name, shape, dt).ap()
    q_pieces = dram("q_pieces", [3, P, N], BF16)
    k_pieces = dram("k_pieces", [3, P, N], BF16)
    v_padded = dram("v_padded", [P, TILES, H * VW])
    att = dram("att", [N, H, HD + 1])
    x1 = dram("x1", [N, DIM])
    table = dram("table", [ROWS, ROW])
    sums = [dram(f"sums{k}", [ROWS, DIM]) for k in range(4)]
    slot_ids = dram("slot_ids", [P, E], U32)
    project_tokens(nc, x, ln_g, ln_b, w_qkv, b_qkv, ident, q_pieces, k_pieces, v_padded)
    attend(nc, w_rel, q_table, k_table, ident, q_pieces, k_pieces, v_padded, att)
    route(nc, x, att, w_out, b_out, gate_t, e_bias, shared_gate_t, shared_up_t, shared_down_t,
          ident, before, iota, x1, table, sums, slot_ids)
    run_experts(nc, table, slot_ids, w1_t, w3_t, w2_t, ident, sums)
    finish(nc, x1, sums, out)


def shape_constants():
    freq = np.exp(np.arange(0, HD, 2) * (-np.log(10000.0) / HD))
    angle = np.arange(T)[None, :] * freq[:, None]
    sin, cos = np.sin(angle), np.cos(angle)
    q_table = np.stack([sin, cos, -cos, sin], axis=1).reshape(2 * HD, T)
    k_table = np.stack([cos, sin], axis=1).reshape(HD, T)
    n = np.arange(P)
    iota = np.stack([n, n + 1, N + n + 1])
    f = lambda a: np.ascontiguousarray(a, dtype=np.float32)
    return {"q_table": f(q_table), "k_table": f(k_table), "ident": f(np.eye(P)),
            "before": f(n[:, None] < n[None, :]), "iota": f(iota)}


def kernel(**inputs):
    import concourse.bacc as bacc
    from concourse.bass_utils import run_bass_kernel_spmd

    a = {k: np.asarray(v) for k, v in inputs.items()}
    arrays = {
        "x": a["L0_attn_x"].reshape(N, DIM),
        "ln_g": a["L0_attn_ln_g"], "ln_b": a["L0_attn_ln_b"],
        "w_qkv": a["L0_attn_w_qkv"], "b_qkv": a["L0_attn_b_qkv"], "w_rel": a["L0_attn_w_rel"],
        "w_out": a["L0_attn_w_out"], "b_out": a["L0_attn_b_out"],
        "gate_t": a["L0_ffn_gate_weight"].T, "e_bias": a["L0_ffn_e_bias"],
        "w1_t": a["L0_ffn_w1"].transpose(2, 0, 1).reshape(DIM, E * F),
        "w2_t": a["L0_ffn_w2"].transpose(0, 2, 1).reshape(E * F, DIM),
        "w3_t": a["L0_ffn_w3"].transpose(2, 0, 1).reshape(DIM, E * F),
        "shared_gate_t": a["L0_ffn_shared_gate"].T, "shared_up_t": a["L0_ffn_shared_up"].T,
        "shared_down_t": a["L0_ffn_shared_down"].T,
        **shape_constants(),
    }
    nc = bacc.Bacc("TRN2", target_bir_lowering=False, num_devices=1)
    sent, args = {}, []
    for name, v in arrays.items():
        v = np.ascontiguousarray(v)
        sent[f"in_{name}"] = v
        args.append(nc.dram_tensor(f"in_{name}", v.shape, mybir.dt.from_np(v.dtype), kind="ExternalInput").ap())
    out = nc.dram_tensor("result", (N, DIM), F32, kind="ExternalOutput").ap()
    program(nc, *args, out)
    r = run_bass_kernel_spmd(nc, [sent], core_ids=[0])
    return r.results[0]["result"].reshape(B, T, DIM)
```

```python
from contextlib import ExitStack

import numpy as np

import concourse.bass as bass
from concourse import mybir

F32 = mybir.dt.float32
BF16 = mybir.dt.bfloat16
U32 = mybir.dt.uint32
ALU = mybir.AluOpType
ACT = mybir.ActivationFunctionType
AX = mybir.AxisListType

P = 128
B, T, DIM = 4, 1024, 128
H, HD = 16, 8
N = B * T
TILES = N // P
CHUNK = 512
CHUNKS = N // CHUNK
PER = CHUNK // P
EPS = 1e-5
SCALE = float(HD) ** -0.5
HG = 4
GROUPS = H // HG
VW = 32

TERMS = [(0, 0), (0, 1), (0, 2), (1, 0), (1, 1), (2, 0)]
K_RUNS = [(0, 3), (3, 2), (5, 1)]
QK_ROWS = HD * len(TERMS)
SCORE_ROWS = 2 * QK_ROWS
SHIFT_ROWS = 3
STACK_ROWS = SCORE_ROWS + SHIFT_ROWS


def wait_apart(engine, registers, met, *waits):
    for register, (_, count) in zip(registers, waits):
        engine.reg_mov(register, count)
    engine.wait_ge(*met)
    for register, (semaphore, _) in zip(registers, waits):
        engine.wait_ge(semaphore, register)


def exact_pieces(dve, nc, src, rest, pieces, done, count):
    nc.vector.tensor_copy(pieces[0], src).then_inc(done, 1)
    dve.wait_ge(done, count + 1)
    nc.vector.tensor_tensor(rest, src, pieces[0], ALU.subtract).then_inc(done, 1)
    dve.wait_ge(done, count + 2)
    nc.vector.tensor_copy(pieces[1], rest).then_inc(done, 1)
    dve.wait_ge(done, count + 3)
    nc.vector.tensor_tensor(pieces[2], rest, pieces[1], ALU.subtract).then_inc(done, 1)
    return 4


def project_tokens(nc, x, ln_g, ln_b, w_qkv, b_qkv, w_rel_rows, q_table, k_table, ident_in,
                   q_image, k_image, v_padded, bias_q_image, bias_k_image):
    with ExitStack() as ctx:
        sb = lambda name, shape, dt=F32: ctx.enter_context(nc.sbuf_tensor(name, shape, dt))
        ps = lambda name: ctx.enter_context(nc.psum_tensor(name, [P, CHUNK], F32))
        sem = lambda name: ctx.enter_context(nc.semaphore(name))
        two = lambda make, name, *args: [make(f"{name}{a}", *args) for a in range(2)]

        xc = two(sb, "xc", [P, PER, DIM])
        stats = sb("stats", [P, PER, 6])
        mv = two(sb, "mv", [P, PER, 2])
        var2 = two(sb, "var2", [P, PER])
        rstd = two(sb, "rstd", [P, PER])
        minus_half = sb("minus_halfA", [P, PER])
        xn = two(sb, "xn", [P, PER, DIM])
        xnT = two(sb, "xnT", [P, CHUNK])
        w = sb("w", [P, 3 * DIM])
        ident = sb("ident", [P, P])
        gcol = sb("gcol", [P, 1])
        bcol = sb("bcol", [P, 1])
        bqcol = sb("bqcol", [P, 1])
        bkcol = sb("bkcol", [P, 1])
        bv = sb("bv", [P, DIM])
        q_full, k_full = two(sb, "q_full", [P, CHUNK]), two(sb, "k_full", [P, CHUNK])
        q_rest, k_rest = sb("q_rest", [P, CHUNK]), sb("k_rest", [P, CHUNK])
        q_piece, k_piece = two(sb, "q_piece", [P, 3, CHUNK], BF16), two(sb, "k_piece", [P, 3, CHUNK], BF16)
        vst = two(sb, "vst", [P, PER, H, VW])
        wrow = sb("wrow", [2 * HD, P])
        tabq = sb("tabq", [2 * HD, T])
        bias_q = sb("bias_q", [P, T])
        bias_rest = sb("bias_rest", [P, T])
        bias_p = sb("bias_p", [P, 3, T], BF16)
        tabk = sb("tabk", [HD, T])
        tabk_rest = sb("tabk_rest", [HD, T])
        tabk_p = sb("tabk_p", [HD, 3, T], BF16)

        psT, psQ, psK, psV = two(ps, "psT"), two(ps, "psQ"), two(ps, "psK"), two(ps, "psV")

        const_in, bias_in = sem("const_in"), sem("bias_in")
        x_in = two(sem, "x_in")
        stats_done, aggr_done = sem("stats_done"), sem("aggr_done")
        var_done, rstd_done, xn_done = two(sem, "var_done"), two(sem, "rstd_done"), two(sem, "xn_done")
        turned, xnT_done = two(sem, "turned"), two(sem, "xnT_done")
        q_ready, k_ready, v_ready = two(sem, "q_ready"), two(sem, "k_ready"), two(sem, "v_ready")
        q_full_done, k_full_done = two(sem, "q_full_done"), two(sem, "k_full_done")
        q_split, k_split, v_done = two(sem, "q_split"), two(sem, "k_split"), two(sem, "v_done")
        stored = two(sem, "stored")
        pads_done, scaled_b, half_made = sem("pads_done"), sem("scaled_b"), sem("half_made")
        bias_ready, bias_read = sem("bias_ready"), sem("bias_read")
        bias_split, table_split, bias_stored = sem("bias_split"), sem("table_split"), sem("bias_stored")

        CONSTS, BIAS_CONSTS = 8 * 16, 3 * 16
        PAIRS = CHUNKS // 2
        STORES = 7 * 16
        block = ctx.enter_context(nc.Block())

        @block.sync
        def _(sp):
            counts = [sp.alloc_register("counts_as")]

            def load(chunk, a):
                sp.dma_start(xc[a][:], x[bass.ds(chunk * CHUNK, CHUNK), :].rearrange("(j p) d -> p j d", p=P)).then_inc(x_in[a], 16)

            def store(pair, a):
                for done, image, piece in ((q_split, q_image, q_piece), (k_split, k_image, k_piece)):
                    wait_apart(sp, counts, (const_in, CONSTS), (done[a], pair * 4 + 8))
                    for p in range(3):
                        sp.dma_start(image[p, :, bass.ds(pair * 2 + a, 1)].rearrange("d o h i -> o h d i")[0], piece[a][:, p, :]).then_inc(stored[a], 16)
                wait_apart(sp, counts, (const_in, CONSTS), (v_done[a], pair + 2))
                sp.dma_start(v_padded[:, bass.ds(pair * (2 * PER) + a * PER, PER), :],
                             vst[a][:].rearrange("p j h c -> p j (h c)")).then_inc(stored[a], 16)

            for a in range(2):
                sp.sem_inc(stored[a], STORES)
            load(0, 0)
            for dst, src in (
                (gcol[:], ln_g.rearrange("(p o) -> p o", o=1)),
                (bcol[:], ln_b.rearrange("(p o) -> p o", o=1)),
                (bqcol[:], b_qkv[0:DIM].rearrange("(p o) -> p o", o=1)),
                (bkcol[:], b_qkv[DIM:2 * DIM].rearrange("(p o) -> p o", o=1)),
                (bv[:], b_qkv[2 * DIM:3 * DIM].rearrange("(o d) -> o d", o=1).to_broadcast([P, DIM])),
            ):
                sp.dma_start(dst, src).then_inc(const_in, 16)
            load(1, 1)
            for a in range(2):
                sp.wait_ge(xn_done[a], 2)
                load(2 + a, a)
            sp.wait_ge(bias_split, 4)
            for p in range(3):
                for half in range(2):
                    sp.dma_start(bias_q_image[p, :, half].rearrange("e h i -> h e i"),
                                 bias_p[:, p, half * CHUNK:(half + 1) * CHUNK]).then_inc(bias_stored, 16)
            with sp.Fori(0, PAIRS - 2) as i:
                for a in range(2):
                    store(i, a)
                    sp.wait_ge(xn_done[a], i + 3)
                    load(i * 2 + (4 + a), a)
            for pair in (PAIRS - 2, PAIRS - 1):
                for a in range(2):
                    store(pair, a)
            sp.wait_ge(bias_stored, (6 + 2 * HG) * 16)
            for a in range(2):
                sp.wait_ge(stored[a], (PAIRS + 1) * STORES)

        @block.vector
        def _(dve):
            counts = [dve.alloc_register("counts_av")]
            for a in range(2):
                dve.sem_inc(v_done[a], 1)
                dve.sem_inc(q_split[a], 4)
                dve.sem_inc(xn_done[a], 1)

            def norm_stats(pair, a, count):
                dve.wait_ge(x_in[a], pair * 16 + 16)
                for j in range(PER):
                    nc.vector.bn_stats(stats[:, j, :], xc[a][:, j, :]).then_inc(stats_done, 1)
                for j in range(PER):
                    wait_apart(dve, counts, (scaled_b, 1), (stats_done, count + (j + 1)))
                    nc.vector.bn_aggr(mv[a][:, j, :], stats[:, j, :]).then_inc(aggr_done, 1)
                dve.wait_ge(aggr_done, count + PER)
                nc.vector.tensor_scalar(var2[a][:], mv[a][:, :, 1], 1.0 + EPS, EPS * EPS, ALU.mult, ALU.add).then_inc(var_done[a], 1)

            def norm_rows(pair, a):
                dve.wait_ge(rstd_done[a], pair + 1)
                dve.wait_ge(turned[a], pair + 1)
                for j in range(PER):
                    ins = nc.vector.tensor_scalar(xn[a][:, j, :], xc[a][:, j, :], mv[a][:, j, 0:1], rstd[a][:, j:j + 1],
                                                  ALU.subtract, ALU.mult)
                ins.then_inc(xn_done[a], 1)

            def split_q_add_v(pair, a):
                dve.wait_ge(q_full_done[a], pair + 1)
                dve.wait_ge(stored[a], (pair + 1) * STORES)
                exact_pieces(dve, nc, q_full[a][:], q_rest[:], [q_piece[a][:, p, :] for p in range(3)],
                             q_split[a], pair * 4 + 4)
                dve.wait_ge(v_ready[a], pair + 2)
                nc.vector.tensor_tensor(
                    vst[a][:, :, :, 0:HD], psV[a][:].rearrange("p (j h d) -> p j h d", j=PER, h=H),
                    bv[:].rearrange("p (o h d) -> p o h d", o=1, h=H).to_broadcast([P, PER, H, HD]),
                    ALU.add).then_inc(v_done[a], 1)

            dve.wait_ge(const_in, CONSTS)
            nc.vector.tensor_scalar(bqcol[:], bqcol[:], SCALE, None, ALU.mult).then_inc(scaled_b, 1)
            for a in range(2):
                norm_stats(0, a, PER * a)
                norm_rows(0, a)
            for half in range(2):
                dve.wait_ge(bias_read, half + 1)
            exact_pieces(dve, nc, bias_q[:], bias_rest[:], [bias_p[:, p, :] for p in range(3)], bias_split, 0)
            dve.wait_ge(pads_done, 4)
            with dve.Fori(0, PAIRS - 1) as i:
                for a in range(2):
                    norm_stats(i + 1, a, i * (2 * PER) + (2 + a) * PER)
                    split_q_add_v(i, a)
                    norm_rows(i + 1, a)
            for a in range(2):
                split_q_add_v(PAIRS - 1, a)

        @block.gpsimd
        def _(pool):
            counts = [pool.alloc_register("counts_ap"), pool.alloc_register("counts_ap1")]
            nc.gpsimd.memset(minus_half[:], -0.5).then_inc(half_made, 1)
            for a in range(2):
                pool.sem_inc(k_split[a], 4)

            def inverse(pair, a):
                pool.wait_ge(var_done[a], pair + 1)
                nc.gpsimd.tensor_tensor(rstd[a][:], var2[a][:], minus_half[:], ALU.pow).then_inc(rstd_done[a], 1)

            def split_k(pair, a):
                wait_apart(pool, counts, (half_made, 1), (k_full_done[a], pair + 1), (stored[a], (pair + 1) * STORES))
                pieces = [k_piece[a][:, p, :] for p in range(3)]
                nc.gpsimd.tensor_copy(pieces[0], k_full[a][:]).then_inc(k_split[a], 1)
                pool.wait_ge(k_split[a], pair * 4 + 5)
                nc.gpsimd.tensor_tensor(k_rest[:], k_full[a][:], pieces[0], ALU.subtract).then_inc(k_split[a], 1)
                wait_apart(pool, counts, (half_made, 1), (k_split[a], pair * 4 + 6))
                nc.gpsimd.tensor_copy(pieces[1], k_rest[:]).then_inc(k_split[a], 1)
                pool.wait_ge(k_split[a], pair * 4 + 7)
                nc.gpsimd.tensor_tensor(pieces[2], k_rest[:], pieces[1], ALU.subtract).then_inc(k_split[a], 1)

            pool.wait_ge(half_made, 1)
            for a in range(2):
                inverse(0, a)
            for a in range(2):
                nc.gpsimd.memset(vst[a][:], 0.0).then_inc(pads_done, 1)
            pool.wait_ge(pads_done, 2)
            for a in range(2):
                nc.gpsimd.memset(vst[a][:, :, :, HD:HD + 1], 1.0).then_inc(pads_done, 1)
            pool.wait_ge(bias_in, BIAS_CONSTS)
            nc.gpsimd.tensor_copy(tabk_p[:, 0, :], tabk[:]).then_inc(table_split, 1)
            pool.wait_ge(table_split, 1)
            nc.gpsimd.tensor_tensor(tabk_rest[:], tabk[:], tabk_p[:, 0, :], ALU.subtract).then_inc(table_split, 1)
            pool.wait_ge(table_split, 2)
            nc.gpsimd.tensor_copy(tabk_p[:, 1, :], tabk_rest[:]).then_inc(table_split, 1)
            pool.wait_ge(table_split, 3)
            nc.gpsimd.tensor_tensor(tabk_p[:, 2, :], tabk_rest[:], tabk_p[:, 1, :], ALU.subtract).then_inc(table_split, 1)
            with pool.Fori(0, PAIRS - 1) as i:
                for a in range(2):
                    inverse(i + 1, a)
                    split_k(i, a)
            for a in range(2):
                split_k(PAIRS - 1, a)

        @block.scalar
        def _(act):
            for dst, src in ((wrow[:], w_rel_rows), (tabq[:], q_table), (tabk[:], k_table)):
                act.dma_start(dst, src).then_inc(bias_in, 16)
            for dst, src in ((ident[:], ident_in), (w[:, 0:DIM], w_qkv[:, 0:DIM]), (w[:, DIM:3 * DIM], w_qkv[:, DIM:3 * DIM])):
                act.dma_start(dst, src).then_inc(const_in, 16)
            for half in range(2):
                act.wait_ge(bias_ready, half + 1)
                nc.scalar.copy(bias_q[:, half * CHUNK:(half + 1) * CHUNK], [psQ, psK][half][0][:]).then_inc(bias_read, 1)
            act.wait_ge(const_in, CONSTS)
            act.wait_ge(scaled_b, 1)
            act.wait_ge(table_split, 4)
            for half in range(2):
                for h in range(HG):
                    act.dma_start(bias_k_image[:, :, half, h, :].rearrange("p e i -> e p i"),
                                  tabk_p[:, :, half * CHUNK:(half + 1) * CHUNK]).then_inc(bias_stored, 16)
            with act.Fori(0, PAIRS) as i:
                for a in range(2):
                    act.wait_ge(turned[a], i + 2)
                    act.wait_ge(v_ready[a], i + 1)
                    nc.scalar.activation(xnT[a][:], psT[a][:], ACT.Identity, bias=bcol[:], scale=gcol[:]).then_inc(xnT_done[a], 1)
                    act.wait_ge(q_ready[a], i + 1)
                    act.wait_ge(q_split[a], i * 4 + 4)
                    nc.scalar.activation(q_full[a][:], psQ[a][:], ACT.Identity, bias=bqcol[:], scale=SCALE).then_inc(q_full_done[a], 1)
                    act.wait_ge(k_ready[a], i + 1)
                    act.wait_ge(k_split[a], i * 4 + 4)
                    nc.scalar.activation(k_full[a][:], psK[a][:], ACT.Identity, bias=bkcol[:]).then_inc(k_full_done[a], 1)

        @block.tensor
        def _(pe):
            for a in range(2):
                pe.sem_inc(turned[a], 1)
                pe.sem_inc(v_ready[a], 1)
            pe.wait_ge(bias_in, BIAS_CONSTS)
            for half in range(2):
                nc.tensor.matmul([psQ, psK][half][0][:], wrow[:], tabq[:, half * CHUNK:(half + 1) * CHUNK],
                                 start=True, stop=True).then_inc(bias_ready, 1)
            pe.wait_ge(const_in, CONSTS)
            pe.wait_ge(bias_read, 2)
            with pe.Fori(0, PAIRS) as i:
                for a in range(2):
                    pe.wait_ge(xn_done[a], i + 2)
                    for j in range(PER):
                        mm = nc.tensor.transpose(psT[a][:, j * P:(j + 1) * P], xn[a][:, j, :], ident[:])
                    mm.then_inc(turned[a], 1)
                    pe.wait_ge(xnT_done[a], i + 1)
                    nc.tensor.matmul(psQ[a][:], w[:, 0:DIM], xnT[a][:], start=True, stop=True).then_inc(q_ready[a], 1)
                    nc.tensor.matmul(psK[a][:], w[:, DIM:2 * DIM], xnT[a][:], start=True, stop=True).then_inc(k_ready[a], 1)
                    pe.wait_ge(v_done[a], i + 1)
                    for j in range(PER):
                        mm = nc.tensor.matmul(psV[a][:, j * P:(j + 1) * P], xnT[a][:, j * P:(j + 1) * P],
                                              w[:, 2 * DIM:3 * DIM], start=True, stop=True)
                    mm.then_inc(v_ready[a], 1)


UNITS = 2 * GROUPS
STEPS = 32
BATCH_STEPS = UNITS * STEPS
LEAD = 48
ST_BANKS = 3
S_BANKS = 3
P_SLOTS = 16
PV_LAG = 6
J_UOUT, J_OTURN, J_OCOPY = 9, 12, 14
J_MTURN, J_MCOPY = 21, 22
LOADS = 2 * len(TERMS) + 1


def attend(nc, ident_in, q_image, k_image, v_padded, bias_q_image, bias_k_image, att, later, cleared_dram, spare_rows):
    with ExitStack() as ctx:
        sb = lambda name, shape, dt=F32: ctx.enter_context(nc.sbuf_tensor(name, shape, dt))
        ps = lambda name: ctx.enter_context(nc.psum_tensor(name, [P, CHUNK], F32))
        sem = lambda name: ctx.enter_context(nc.semaphore(name))

        q_stack = [sb(f"q_stack{g}", [STACK_ROWS, 2, HG, CHUNK], BF16) for g in range(GROUPS)]
        k_stack = [sb(f"k_stack{g}", [STACK_ROWS, 2, HG, CHUNK], BF16) for g in range(GROUPS)]
        values = [sb(f"values{g}", [P, T // P, HG, VW]) for g in range(GROUPS)]
        probs = sb("probs", [P, P_SLOTS, CHUNK])
        half_max = [sb(f"half_max{v}", [P, STEPS]) for v in range(2)]
        minus_max = sb("minus_max", [P, STEPS // 2])
        shift_rest = sb("shift_rest", [P, STEPS // 2])
        shift = sb("shift", [P, 3, STEPS // 2], BF16)
        shiftT = sb("shiftT", [3 * STEPS // 2, P], BF16)
        unit_out = sb("unit_out", [P, CHUNK])
        unit_rows = sb("unit_rows", [P, PER, HG, HD + 1])
        ident = sb("identB", [P, P])
        ident16 = sb("ident16", [P, P], BF16)

        st_bank = [ps(f"st_bank{v}") for v in range(ST_BANKS)]
        s_bank = [ps(f"s_bank{v}") for v in range(S_BANKS)]
        pv_bank = ps("pv_bank")
        misc = ps("misc")

        zeros = sb("zeros", [P, ROW])
        ident_ready = sem("ident_ready")
        later_in, zeros_done, cleared = sem("later_in"), sem("zeros_done"), sem("cleared")
        ident16_done = sem("ident16_done")
        ones_done = sem("ones_done")
        bias_rows_in = [sem(f"bias_rows_in{g}") for g in range(GROUPS)]
        loaded = [sem(f"loaded{g}") for g in range(GROUPS)]
        s_ready = sem("s_ready")
        max_done = sem("max_done")
        row_max_done = sem("row_max_done")
        shift_done = sem("shift_done")
        shift_turned = sem("shift_turned")
        shiftT_done = sem("shiftT_done")
        shift_in = sem("shift_in")
        st_ready = sem("st_ready")
        exp_done = sem("exp_done")
        pv_done = sem("pv_done")
        unit_out_done = sem("unit_out_done")
        out_turned = sem("out_turned")
        rows_done = sem("rows_done")
        rows_stored = sem("rows_stored")

        block = ctx.enter_context(nc.Block())

        MAX0, EXP0, PV0 = S_BANKS, ST_BANKS, P_SLOTS // HG

        def before(s, ring):
            if s >= ring:
                return s - ring
            last = BATCH_STEPS - 1
            while last % ring != s:
                last -= 1
            return last - BATCH_STEPS

        def split(s):
            return s // STEPS, s % STEPS

        def load(sp, b, g):
            heads, chunks = slice(HG * g, HG * (g + 1)), bass.ds(b * 2, 2)
            for t, (piece, _) in enumerate(TERMS):
                sp.dma_start(q_stack[g][HD * t:HD * (t + 1)].rearrange("r c h i -> r c (h i)"), q_image[piece, :, chunks, heads, :]
                             .rearrange("d c h i -> d c (h i)")).then_inc(loaded[g], 16)
            for first, n in K_RUNS:
                rows = slice(HD * first, HD * (first + n))
                sp.dma_start(k_stack[g][rows].rearrange("r c h i -> r c (h i)"), k_image[0:n, :, chunks, heads, :]
                             .rearrange("p d c h i -> (p d) c (h i)")).then_inc(loaded[g], 16)
            sp.dma_start(values[g][:].rearrange("p k h c -> p k (h c)"),
                         v_padded[:, bass.ds(b * (T // P), T // P), HG * VW * g:HG * VW * (g + 1)]).then_inc(loaded[g], 16)

        LOAD = 16 * (len(TERMS) + len(K_RUNS) + 1)

        def load_bias(sp, g):
            for t, (piece, _) in enumerate(TERMS):
                r = QK_ROWS + HD * t
                sp.dma_start(q_stack[g][r:r + HD].rearrange("r c h i -> r c (h i)"),
                             bias_q_image[piece, :, :, HG * g:HG * (g + 1), :].rearrange("e c h i -> e c (h i)")).then_inc(bias_rows_in[g], 16)
            for first, n in K_RUNS:
                rows = slice(QK_ROWS + HD * first, QK_ROWS + HD * (first + n))
                sp.dma_start(k_stack[g][rows].rearrange("r c h i -> r (c h i)"),
                             bias_k_image[0:n].rearrange("p e c h i -> (p e) (c h i)")).then_inc(bias_rows_in[g], 16)

        LOAD_BIAS = 16 * (len(TERMS) + len(K_RUNS))

        def put_shift(sp, unit, n):
            g, half = unit // 2, unit % 2
            sp.wait_ge(shiftT_done, n + 1)
            for p in range(3):
                r = SCORE_ROWS + p
                sp.dma_start(q_stack[g][r:r + 1, half].rearrange("o h i -> o (h i)"),
                             shiftT[16 * p:16 * (p + 1), :]).then_inc(shift_in, 16)

        def store_rows(sp, b, unit, n):
            g, half = unit // 2, unit % 2
            sp.wait_ge(rows_done, n + 1)
            sp.dma_start(att[bass.ds(b * T + half * CHUNK, CHUNK), HG * g:HG * (g + 1), :].rearrange("(t p) h c -> p t (h c)", p=P),
                         unit_rows[:].rearrange("p t h c -> p t (h c)")).then_inc(rows_stored, 16)

        @block.sync
        def _(sp):
            counts = [sp.alloc_register(f"counts_bs{k}") for k in range(2)]
            sp.dma_start(ident[:], ident_in).then_inc(ident_ready, 16)
            for g in range(GROUPS):
                load(sp, 0, g)
                load_bias(sp, g)
            put_shift(sp, 0, 0)
            for dst, src in later:
                sp.dma_start(dst, src, allow_slow_non_contiguous=True).then_inc(later_in, 16)

            def batch(b, last):
                for u in range(UNITS):
                    if u % 2 == 0 and u >= 2 and not last:
                        g = u // 2 - 1
                        wait_apart(sp, counts, (ident_ready, 16), (st_ready, b * BATCH_STEPS + 2 * STEPS * (g + 1)),
                                   (pv_done, b * (BATCH_STEPS // HG) + 2 * STEPS // HG * (g + 1) + PV0))
                        load(sp, b + 1, g)
                    if u >= 1:
                        store_rows(sp, b, u - 1, b * UNITS + u - 1)
                    if u < UNITS - 1 or not last:
                        put_shift(sp, (u + 1) % UNITS, b * UNITS + u + 1)
                if not last:
                    wait_apart(sp, counts, (ident_ready, 16), (st_ready, b * BATCH_STEPS + BATCH_STEPS),
                               (pv_done, b * (BATCH_STEPS // HG) + BATCH_STEPS // HG + PV0))
                    load(sp, b + 1, GROUPS - 1)
                store_rows(sp, b, UNITS - 1, b * UNITS + UNITS - 1)

            with sp.Fori(0, B - 1) as b:
                batch(b, False)
            batch(B - 1, True)
            sp.wait_ge(rows_stored, 16 * B * UNITS)
            sp.wait_ge(later_in, 16 * len(later))
            sp.wait_ge(cleared, 16 * (len(spare_rows) + B * UNITS * len(cleared_dram)))

        @block.vector
        def _(dve):
            dve.sem_inc(max_done, MAX0)
            nc.vector.memset(minus_max[:], 0.0).then_inc(ident16_done, 1)
            dve.wait_ge(ident_ready, 16)
            nc.vector.tensor_copy(ident16[:], ident[:]).then_inc(ident16_done, 1)

            def step(b, s):
                unit, j = split(s)
                dve.wait_ge(s_ready, b * BATCH_STEPS + s + 1)
                nc.vector.tensor_reduce(half_max[unit % 2][:, j:j + 1], s_bank[s % S_BANKS][:], AX.X, ALU.max).then_inc(max_done, 1)
                if j == STEPS - 1:
                    dve.wait_ge(max_done, b * BATCH_STEPS + s + 1 + MAX0)
                    dve.wait_ge(shift_done, b * (4 * UNITS) + 4 * unit)
                    nc.vector.tensor_reduce(minus_max[:], half_max[unit % 2][:].rearrange("p (r k) -> p r k", k=2),
                                            AX.X, ALU.max, negate=True).then_inc(row_max_done, 1)

            for s in range(LEAD):
                step(0, s)
            with dve.Fori(0, B - 1) as b:
                for s in range(LEAD, BATCH_STEPS):
                    step(b, s)
                for s in range(LEAD):
                    step(b + 1, s)
            for s in range(LEAD, BATCH_STEPS):
                step(B - 1, s)

        @block.gpsimd
        def _(pool):
            counts = [pool.alloc_register(f"counts_b{k}") for k in range(2)]
            for g in range(GROUPS):
                nc.gpsimd.memset(k_stack[g][SCORE_ROWS:STACK_ROWS], 1.0).then_inc(ones_done, 1)
            pool.wait_ge(ones_done, GROUPS)
            nc.gpsimd.memset(zeros[:], 0.0).then_inc(zeros_done, 1)
            pool.wait_ge(zeros_done, 1)
            for rows in spare_rows:
                pool.dma_start(rows, zeros[:, 0:rows.shape[1]]).then_inc(cleared, 16)
            with pool.Fori(0, B * UNITS) as n:
                wait_apart(pool, counts, (ones_done, GROUPS), (row_max_done, n + 1), (shift_turned, n))
                nc.gpsimd.tensor_copy(shift[:, 0, :], minus_max[:]).then_inc(shift_done, 1)
                pool.wait_ge(shift_done, n * 4 + 1)
                nc.gpsimd.tensor_tensor(shift_rest[:], minus_max[:], shift[:, 0, :], ALU.subtract).then_inc(shift_done, 1)
                wait_apart(pool, counts, (ones_done, GROUPS), (shift_done, n * 4 + 2))
                nc.gpsimd.tensor_copy(shift[:, 1, :], shift_rest[:]).then_inc(shift_done, 1)
                pool.wait_ge(shift_done, n * 4 + 3)
                nc.gpsimd.tensor_tensor(shift[:, 2, :], shift_rest[:], shift[:, 1, :], ALU.subtract).then_inc(shift_done, 1)
                for table in cleared_dram:
                    pool.dma_start(table[bass.ds(n * P, P), :], zeros[:, 0:DIM]).then_inc(cleared, 16)

        @block.scalar
        def _(act):
            act.sem_inc(exp_done, EXP0)

            def shift_copy(n):
                act.wait_ge(shift_turned, n + 1)
                act.wait_ge(shift_in, n * 48)
                nc.scalar.copy(shiftT[:], misc[0:48, 0:P]).then_inc(shiftT_done, 1)

            def out_copy(n):
                act.wait_ge(pv_done, n * (STEPS // HG) + STEPS // HG + PV0)
                act.wait_ge(out_turned, n)
                nc.scalar.copy(unit_out[:], pv_bank[:]).then_inc(unit_out_done, 1)

            def rows_copy(n):
                act.wait_ge(out_turned, n + 1)
                act.wait_ge(rows_stored, n * 16)
                nc.scalar.copy(unit_rows[:], misc[:].rearrange("p (t h c) -> p t h c", t=PER, h=HG)[:, :, :, 0:HD + 1]).then_inc(rows_done, 1)

            shift_copy(0)

            def batch(b, last):
                for u in range(UNITS):
                    n = b * UNITS + u
                    for j in range(STEPS):
                        s = STEPS * u + j
                        act.wait_ge(st_ready, b * BATCH_STEPS + s + 1)
                        if j % HG == 0:
                            act.wait_ge(pv_done, b * (BATCH_STEPS // HG) + s // HG + 1)
                        nc.scalar.activation(probs[:, s % P_SLOTS, :], st_bank[s % ST_BANKS][:], ACT.Exp).then_inc(exp_done, 1)
                        if u >= 1 and j == J_UOUT:
                            out_copy(n - 1)
                        if u >= 1 and j == J_OCOPY:
                            rows_copy(n - 1)
                        if j == J_MCOPY and (u < UNITS - 1 or not last):
                            shift_copy(n + 1)
                out_copy(b * UNITS + UNITS - 1)
                rows_copy(b * UNITS + UNITS - 1)

            with act.Fori(0, B - 1) as b:
                batch(b, False)
            batch(B - 1, True)

        @block.tensor
        def _(pe):
            pe.wait_ge(ident_ready, 16)
            pe.wait_ge(ident16_done, 2)
            pe.sem_inc(pv_done, PV0)

            def score(b, base, s):
                unit, j = split(s)
                g, half = unit // 2, unit % 2
                h, tile, keys = j // 8, j // 2 % 4, j % 2
                if j == 0 and half == 0:
                    pe.wait_ge(loaded[g], b * LOAD + LOAD)
                    pe.wait_ge(bias_rows_in[g], LOAD_BIAS)
                pe.wait_ge(max_done, base + before(s, S_BANKS) + 1 + MAX0)
                nc.tensor.matmul(s_bank[s % S_BANKS][:], q_stack[g][0:SCORE_ROWS, half, h, tile * P:(tile + 1) * P],
                                 k_stack[g][0:SCORE_ROWS, keys, h, :], start=True, stop=True).then_inc(s_ready, 1)

            def score_t(b, s):
                unit, j = split(s)
                g, half = unit // 2, unit % 2
                tile, h = j // HG, j % HG
                if j == 0:
                    pe.wait_ge(shift_in, b * (UNITS * 48) + (unit + 1) * 48)
                pe.wait_ge(exp_done, b * BATCH_STEPS + before(s, ST_BANKS) + 1 + EXP0)
                nc.tensor.matmul(st_bank[s % ST_BANKS][:], k_stack[g][:, tile // PER, h, tile % PER * P:(tile % PER + 1) * P],
                                 q_stack[g][:, half, h, :], start=True, stop=True).then_inc(st_ready, 1)

            def times_values(b, unit, tile):
                s = STEPS * unit + HG * tile
                pe.wait_ge(exp_done, b * BATCH_STEPS + s + HG + EXP0)
                if tile == 0:
                    pe.wait_ge(unit_out_done, b * UNITS + unit)
                for h in range(HG):
                    mm = nc.tensor.matmul(pv_bank[VW * h:VW * (h + 1), :], values[unit // 2][:, tile, h, :],
                                          probs[:, (s + h) % P_SLOTS, :], start=(tile == 0), stop=(tile == T // P - 1),
                                          tile_position=(0, VW * h))
                mm.then_inc(pv_done, 1)

            def turn_out(n, shifts):
                pe.wait_ge(unit_out_done, n + 1)
                pe.wait_ge(shiftT_done, shifts)
                for t in range(PER):
                    mm = nc.tensor.transpose(misc[:, t * P:(t + 1) * P], unit_out[:, t * P:(t + 1) * P], ident[:])
                mm.then_inc(out_turned, 1)

            def turn_shift(n, rows):
                pe.wait_ge(shift_done, n * 4 + 4)
                pe.wait_ge(rows_done, rows)
                nc.tensor.matmul(misc[0:48, 0:P], shift[:].rearrange("p c r -> p (c r)"), ident16[:],
                                 start=True, stop=True).then_inc(shift_turned, 1)

            for s in range(LEAD):
                score(0, 0, s)
            pe.wait_ge(ones_done, GROUPS)
            turn_shift(0, 0)

            def batch(b, last):
                base = b * BATCH_STEPS if last else pe.snap(score_count, min_val=0, max_val=B * BATCH_STEPS)
                for u in range(UNITS + 1):
                    for j in range(STEPS):
                        s = STEPS * u + j
                        if u < UNITS:
                            score_t(b, s)
                            if s + LEAD < BATCH_STEPS:
                                score(b, base, s + LEAD)
                            elif not last:
                                score(b + 1, base + BATCH_STEPS, s + LEAD - BATCH_STEPS)
                        done = s - PV_LAG
                        if done >= 0 and done % HG == HG - 1 and done < BATCH_STEPS:
                            unit, jj = split(done)
                            times_values(b, unit, jj // HG)
                        if u >= 1 and j == J_OTURN:
                            turn_out(b * UNITS + u - 1, b * UNITS + (u if last and u == UNITS else u + 1))
                        if u < UNITS and j == J_MTURN and (u < UNITS - 1 or not last):
                            turn_shift(b * UNITS + u + 1, b * UNITS + u)

            score_count = pe.alloc_register("score_count")
            pe.reg_mov(score_count, 0)
            with pe.Fori(0, B - 1) as b:
                batch(b, False)
                pe.reg_add(score_count, score_count, BATCH_STEPS)
            batch(B - 1, True)


E, TOPK, NGROUPS, TOPG = 64, 8, 8, 4
GE = E // NGROUPS
CAP = 128
F = 64
ROUTE_SCALE = 2.5
ROW = DIM + E
ROWS = N + CAP
BIG = 1e30
STEPS_1, STEPS_2 = 5, 25


def inverse_std(pool, nc, out, var, minus_half, tmp, tmp_ready, tmp_count, done):
    nc.gpsimd.tensor_scalar(tmp, var, EPS, None, ALU.add).then_inc(tmp_ready, 1)
    pool.wait_ge(tmp_ready, tmp_count)
    nc.gpsimd.tensor_tensor(out, tmp, minus_half, ALU.pow).then_inc(done, 1)


def route(nc, x, att, consts, table, shared_sums, slot_ids):
    with ExitStack() as ctx:
        sb = lambda name, shape, dt=F32: ctx.enter_context(nc.sbuf_tensor(name, shape, dt))
        ps = lambda name: ctx.enter_context(nc.psum_tensor(name, [P, CHUNK], F32))
        sem = lambda name: ctx.enter_context(nc.semaphore(name))

        k = consts
        ones = sb("ones", [P, P], BF16)
        before = sb("before", [P, P], BF16)
        minus_half = sb("minus_half", [P, PER])
        tile_no = sb("tile_no", [P, PER])

        attc = sb("attc", [P, PER, H, HD + 1])
        xc = sb("xcC", [P, PER, DIM])
        recip = sb("recip", [P, PER, H])
        normed = sb("normed", [P, PER, DIM])
        turned_sb = sb("turned_sb", [P, CHUNK])
        y = sb("y", [P, PER, DIM])
        stats = sb("statsC", [P, PER, 6])
        mv = sb("mvC", [P, PER, 2])
        veps = sb("veps", [P, PER])
        rstd = sb("rstdC", [P, PER])
        x1c = sb("x1c", [P, PER, DIM])
        xf = sb("xf", [P, PER, DIM])
        weights = sb("weights", [P, PER, E])
        xfT = sb("xfT", [P, CHUNK])
        scores = sb("scores", [P, PER, E])
        sg = sb("sg", [P, CHUNK])
        sh = sb("sh", [P, CHUNK])
        shared = sb("shared", [P, PER, DIM])
        sfc = sb("sfc", [P, PER, E])
        top1 = sb("top1", [P, PER * NGROUPS])
        is_top = sb("is_top", [P, PER, E])
        count = sb("count", [P, PER * NGROUPS])
        second = sb("second", [P, PER * NGROUPS])
        gsum = sb("gsum", [P, PER, NGROUPS])
        above = sb("above", [P, PER, NGROUPS, NGROUPS])
        same = sb("same", [P, PER, NGROUPS, NGROUPS])
        grank = sb("grank", [P, PER * NGROUPS])
        tmp = sb("tmp", [P, PER, E])
        best = sb("best", [P, PER, TOPK])
        marked = sb("marked", [P, PER, E])
        chosen = sb("chosen", [P, PER, E], BF16)
        picked = sb("picked", [P, PER, E])
        wsum = sb("wsum", [P, PER])
        wrec = sb("wrec", [P, PER])
        sofar = sb("sofar", [P, E], BF16)
        key = sb("key", [P, PER, E])
        keys = sb("keys", [P, PER * TOPK])
        keys_i = sb("keys_i", [P, PER * TOPK], U32)
        part_i = sb("part_i", [P, 2, PER * TOPK], U32)
        part = sb("part", [P, 2, PER * TOPK])
        hot_e = sb("hot_e", [P, PER * TOPK, E], BF16)
        id_parts = sb("id_parts", [P, PER * TOPK, 2, E], BF16)
        hot_s = sb("hot_s", [P, PER * TOPK, CAP], BF16)
        nothing = sb("nothing", [P, P], BF16)
        lo = sb("lo", [P, E])
        token = sb("token", [P, E])
        is_free = sb("is_free", [P, E])
        ids_u = sb("ids_u", [P, E], U32)

        psA, psB, psC, psD, psE, psF, psG = [ps(f"psC{i}") for i in range(7)]

        own = {1: sem("stage1_steps"), 2: sem("stage2_steps")}
        setup_v, setup_p, final_steps = sem("setup_v"), sem("setup_p"), sem("final_steps")
        att_in, x_in = sem("att_inC"), sem("x_inC")
        signals = {}
        for name in ("normed_done", "attT_turned", "attT_done", "projected", "var_y", "rstd_y", "x1_done",
                     "var_x1", "rstd_x1", "xf_done", "xf_turned", "xfT_done", "logits_ready", "scores_done",
                     "gate_up_ready", "shared_sig", "shared_h", "down_ready", "shared_done", "picked_done",
                     "chosen_done", "ranks_ready", "sofar_done", "weights_done", "hot_e_done",
                     "ids_parts_done", "hot_s_done", "x1_kept", "ids_ready", "veps_y", "veps_x1"):
            signals[name] = sem(name)
        S = signals
        tile_no_steps = sem("tile_no_steps")
        sofar_steps, recip_done = sem("sofar_steps"), sem("recip_done")
        xf_stored, shared_stored, weights_stored = sem("xf_stored"), sem("shared_stored"), sem("weights_stored")
        ids_stored = sem("ids_stored")

        def this(c):
            return c + 2

        def last(c):
            return c + 1

        def credit(engine, *names):
            for name in names:
                engine.sem_inc(S[name], 1)

        block = ctx.enter_context(nc.Block())

        @block.sync
        def _(sp):
            def rows(a, c):
                return a[bass.ds(c * CHUNK, CHUNK)].rearrange("(j p) d -> p j d", p=P)

            def load_att(c):
                sp.dma_start(attc[:].rearrange("p j h c -> p j (h c)"),
                             att[bass.ds(c * CHUNK, CHUNK)].rearrange("(j p) h c -> p j (h c)", p=P)).then_inc(att_in, 16)

            def load_x(c):
                sp.dma_start(xc[:], rows(x, c)).then_inc(x_in, 16)

            def next_att(c):
                wait_apart(sp, counts, (setup_v, 3), (S["normed_done"], this(c)))
                load_att(c + 1)

            def stage1(c, more):
                if more:
                    wait_apart(sp, counts, (setup_v, 3), (S["x1_done"], this(c)))
                    load_x(c + 1)

            def stage1_end(c):
                wait_apart(sp, counts, (setup_v, 3), (S["xf_done"], this(c)))
                sp.dma_start(rows(table, c)[:, :, 0:DIM], xf[:]).then_inc(xf_stored, 16)
                wait_apart(sp, counts, (setup_v, 3), (S["shared_done"], this(c)))
                sp.dma_start(rows(shared_sums, c), shared[:]).then_inc(shared_stored, 16)

            def stage2(c):
                wait_apart(sp, counts, (setup_v, 3), (S["weights_done"], this(c)))
                sp.dma_start(rows(table, c)[:, :, DIM:ROW], weights[:]).then_inc(weights_stored, 16)

            counts = [sp.alloc_register("counts_cs")]
            load_att(0)
            load_x(0)
            for stored in (xf_stored, shared_stored, weights_stored):
                sp.sem_inc(stored, 16)
            sp.wait_ge(setup_v, 3)
            next_att(0)
            stage1(0, True)
            stage1_end(0)
            next_att(1)
            with sp.Fori(0, CHUNKS - 3) as i:
                stage1(i + 1, True)
                stage2(i)
                stage1_end(i + 1)
                next_att(i + 2)
            stage1(CHUNKS - 2, True)
            stage2(CHUNKS - 3)
            stage1_end(CHUNKS - 2)
            stage1(CHUNKS - 1, False)
            stage2(CHUNKS - 2)
            stage1_end(CHUNKS - 1)
            stage2(CHUNKS - 1)
            sp.wait_ge(final_steps, 6)
            sp.dma_start(slot_ids, ids_u[:]).then_inc(ids_stored, 16)
            for stored in (xf_stored, shared_stored, weights_stored):
                sp.wait_ge(stored, (CHUNKS + 1) * 16)
            sp.wait_ge(ids_stored, 16)

        @block.vector
        def _(dve):
            V = nc.vector
            counts = [dve.alloc_register("counts_cv")]
            credit(dve, "normed_done", "var_y", "x1_done", "var_x1", "xf_done", "shared_h", "picked_done",
                   "chosen_done", "weights_done", "hot_e_done", "hot_s_done")
            V.memset(ones[:], 1.0).then_inc(setup_v, 1)
            V.memset(nothing[:], 0.0).then_inc(setup_v, 1)
            V.tensor_copy(before[:], k["before"][:]).then_inc(setup_v, 1)

            n = {1: 0, 2: 0}
            base = {1: 0, 2: 0}
            latest = {}

            def chunk(stage, c, steps):
                n[stage] = 0
                base[stage] = c * steps

            def step(stage, ins):
                ins.then_inc(own[stage], 1)
                n[stage] += 1
                latest[stage] = (own[stage], base[stage] + n[stage])

            def signal(stage, ins, name, c):
                ins.then_inc(S[name], 1)
                latest[stage] = (S[name], this(c))

            def settle(stage, plain=False):
                if plain:
                    wait_apart(dve, counts, (setup_v, 3), latest[stage])
                else:
                    dve.wait_ge(*latest[stage])

            by_tile = lambda a, width: a.rearrange("p (o d) -> p o d", o=1).to_broadcast([P, PER, width])

            def norm(c, src, name):
                settle(1)
                for j in range(PER):
                    ins = V.bn_stats(stats[:, j, :], src[:, j, :])
                step(1, ins)
                settle(1, plain=True)
                for j in range(PER):
                    ins = V.bn_aggr(mv[:, j, :], stats[:, j, :])
                signal(1, ins, name, c)

            def normalise(c):
                dve.wait_ge(att_in, c * 16 + 16)
                V.reciprocal(recip[:], attc[:, :, :, HD]).then_inc(recip_done, 1)
                dve.wait_ge(recip_done, c + 1)
                dve.wait_ge(S["attT_turned"], last(c))
                V.tensor_tensor(normed[:].rearrange("p j (h d) -> p (j h) d", h=H),
                                attc[:].rearrange("p j h c -> p (j h) c")[:, :, 0:HD],
                                recip[:].rearrange("p j (h o) -> p (j h) o", o=1).to_broadcast([P, PER * H, HD]),
                                ALU.mult).then_inc(S["normed_done"], 1)

            def add_bias(c):
                chunk(1, c, STEPS_1)
                dve.wait_ge(S["projected"], this(c))
                step(1, V.tensor_tensor(y[:], psB[:].rearrange("p (j d) -> p j d", j=PER), by_tile(k["b_o"][:], DIM), ALU.add))
                norm(c, y, "var_y")

            def residual(c):
                dve.wait_ge(S["rstd_y"], this(c))
                for j in range(PER):
                    ins = V.tensor_scalar(y[:, j, :], y[:, j, :], mv[:, j, 0:1], rstd[:, j:j + 1], ALU.subtract, ALU.mult)
                step(1, ins)
                settle(1)
                dve.wait_ge(x_in, c * 16 + 16)
                dve.wait_ge(S["x1_kept"], last(c))
                signal(1, V.tensor_tensor(x1c[:], xc[:], y[:], ALU.add), "x1_done", c)
                norm(c, x1c, "var_x1")

            def expert_input(c):
                dve.wait_ge(S["rstd_x1"], this(c))
                dve.wait_ge(xf_stored, c * 16 + 16)
                dve.wait_ge(S["xf_turned"], last(c))
                for j in range(PER):
                    ins = V.tensor_scalar(xf[:, j, :], x1c[:, j, :], mv[:, j, 0:1], rstd[:, j:j + 1], ALU.subtract, ALU.mult)
                signal(1, ins, "xf_done", c)

            def shared_expert(c):
                dve.wait_ge(S["shared_sig"], this(c))
                dve.wait_ge(S["down_ready"], last(c))
                step(1, V.tensor_tensor(sh[:], psD[:], sg[:], ALU.mult))
                settle(1)
                signal(1, V.tensor_tensor(sh[:], psE[:], sh[:], ALU.mult), "shared_h", c)

            by_group = lambda a: a.rearrange("p j (g e) -> p (j g) e", e=GE)
            spread = lambda a: a.rearrange("p (g o) -> p g o", o=1).to_broadcast([P, PER * NGROUPS, GE])

            def then(ins, plain=False):
                step(2, ins)
                settle(2, plain)

            def two_best(c):
                chunk(2, c, STEPS_2)
                dve.wait_ge(S["scores_done"], this(c))
                then(V.tensor_tensor(sfc[:], scores[:], by_tile(k["e_bias"][:], E), ALU.add))
                then(V.tensor_reduce(top1[:], by_group(sfc[:]), AX.X, ALU.max))
                then(V.tensor_tensor(by_group(is_top[:]), by_group(sfc[:]), spread(top1[:]), ALU.is_equal))
                V.tensor_reduce(count[:], by_group(is_top[:]), AX.X, ALU.add)
                then(V.scalar_tensor_tensor(out=tmp[:], in0=is_top[:], scalar=-BIG, in1=sfc[:], op0=ALU.mult, op1=ALU.add))
                V.tensor_reduce(second[:], by_group(tmp[:]), AX.X, ALU.max)
                then(V.tensor_scalar(count[:], count[:], 2.0, -BIG, ALU.is_lt, ALU.mult))
                then(V.tensor_tensor(count[:], count[:], top1[:], ALU.add))
                then(V.tensor_tensor(second[:], second[:], count[:], ALU.max))
                then(V.tensor_tensor(gsum[:].rearrange("p j g -> p (j g)"), top1[:], second[:], ALU.add))

            def group_choice(c):
                settle(2)
                shape = [P, PER, NGROUPS, NGROUPS]
                mine = gsum[:].rearrange("p j (g o) -> p j g o", o=1).to_broadcast(shape)
                other = gsum[:].rearrange("p j (o g) -> p j o g", o=1).to_broadcast(shape)
                V.tensor_tensor(above[:], other, mine, ALU.is_gt)
                then(V.tensor_tensor(same[:], other, mine, ALU.is_equal))
                then(V.tensor_tensor(same[:], same[:], k["earlier"][:].rearrange("p (o g h) -> p o g h", o=1, g=NGROUPS).to_broadcast(shape), ALU.mult))
                then(V.tensor_tensor(above[:], above[:], same[:], ALU.add))
                then(V.tensor_reduce(grank[:], above[:].rearrange("p j g o -> p (j g) o"), AX.X, ALU.add))
                then(V.tensor_scalar(grank[:], grank[:], float(TOPG), None, ALU.is_lt))
                then(V.tensor_tensor(by_group(tmp[:]), by_group(sfc[:]), spread(grank[:]), ALU.mult), plain=True)
                for j in range(PER):
                    ins = V.max(best[:, j, :], tmp[:, j, :])
                then(ins, plain=True)
                for j in range(PER):
                    ins = V.match_replace(marked[:, j, :], best[:, j, :], tmp[:, j, :], -BIG)
                step(2, ins)

            def choice(c):
                settle(2)
                dve.wait_ge(S["sofar_done"], last(c))
                signal(2, V.tensor_scalar(chosen[:], marked[:], -0.5 * BIG, None, ALU.is_lt), "chosen_done", c)
                settle(2)
                signal(2, V.tensor_tensor(picked[:], scores[:], chosen[:], ALU.mult), "picked_done", c)
                settle(2)
                then(V.tensor_reduce(wsum[:], picked[:], AX.X, ALU.add))
                then(V.tensor_scalar(wsum[:], wsum[:], 1e-20, None, ALU.add))
                then(V.reciprocal(wrec[:], wsum[:]))
                dve.wait_ge(weights_stored, c * 16 + 16)
                for j in range(PER):
                    ins = V.tensor_scalar(weights[:, j, :], picked[:, j, :], wrec[:, j:j + 1], ROUTE_SCALE, ALU.mult, ALU.mult)
                signal(2, ins, "weights_done", c)

            def rank_and_expert(c):
                dve.wait_ge(S["ranks_ready"], this(c))
                then(V.scalar_tensor_tensor(out=key[:], in0=psC[:, 0:PER * E].rearrange("p (j e) -> p j e", j=PER), scalar=float(E),
                                            in1=by_tile(k["expert_1"][:], E), op0=ALU.mult, op1=ALU.add))
                then(V.tensor_tensor(key[:], key[:], chosen[:], ALU.mult), plain=True)
                for j in range(PER):
                    ins = V.max(keys[:, j * TOPK:(j + 1) * TOPK], key[:, j, :])
                then(ins)
                then(V.tensor_scalar(keys_i[:], keys[:], -1.0, None, ALU.add))
                V.tensor_scalar(part_i[:, 0, :], keys_i[:], E - 1, None, ALU.bitwise_and)
                then(V.tensor_scalar(part_i[:, 1, :], keys_i[:], E.bit_length() - 1, None, ALU.logical_shift_right))
                then(V.tensor_copy(part[:], part_i[:]))
                dve.wait_ge(S["ids_parts_done"], last(c))
                signal(2, V.tensor_tensor(hot_e[:], k["iota"][:, 0:E].rearrange("p (o e) -> p o e", o=1).to_broadcast([P, PER * TOPK, E]),
                                          part[:, 0, :].rearrange("p (k o) -> p k o", o=1).to_broadcast([P, PER * TOPK, E]),
                                          ALU.is_equal), "hot_e_done", c)

            def slot_hot(c):
                dve.wait_ge(S["ids_ready"], last(c))
                signal(2, V.tensor_tensor(hot_s[:], k["iota"][:].rearrange("p (o s) -> p o s", o=1).to_broadcast([P, PER * TOPK, CAP]),
                                          part[:, 1, :].rearrange("p (k o) -> p k o", o=1).to_broadcast([P, PER * TOPK, CAP]),
                                          ALU.is_equal), "hot_s_done", c)

            def stage2(c, ahead, far):
                two_best(c)
                if ahead:
                    add_bias(c + 1)
                group_choice(c)
                if ahead:
                    residual(c + 1)
                choice(c)
                if ahead:
                    expert_input(c + 1)
                rank_and_expert(c)
                if ahead:
                    shared_expert(c + 1)
                if far:
                    normalise(c + 2)
                slot_hot(c)

            dve.wait_ge(setup_p, 1)
            normalise(0)
            add_bias(0)
            residual(0)
            expert_input(0)
            shared_expert(0)
            assert n[1] == STEPS_1
            normalise(1)
            with dve.Fori(0, CHUNKS - 2) as i:
                stage2(i, True, True)
                assert n[2] == STEPS_2
            stage2(CHUNKS - 2, True, False)
            stage2(CHUNKS - 1, False, False)

            dve.wait_ge(S["ids_ready"], this(CHUNKS - 1))
            V.tensor_copy(lo[:], psF[:, 0:E]).then_inc(final_steps, 1)
            dve.wait_ge(final_steps, 1)
            V.scalar_tensor_tensor(out=token[:], in0=psF[:, E:2 * E], scalar=float(P), in1=lo[:], op0=ALU.mult, op1=ALU.add).then_inc(final_steps, 1)
            V.tensor_scalar(is_free[:], lo[:], 0.0, None, ALU.is_equal).then_inc(final_steps, 1)
            dve.wait_ge(final_steps, 3)
            V.tensor_scalar(is_free[:], is_free[:], k["free_id"][:], None, ALU.mult).then_inc(final_steps, 1)
            dve.wait_ge(final_steps, 4)
            V.tensor_tensor(token[:], token[:], is_free[:], ALU.add).then_inc(final_steps, 1)
            dve.wait_ge(final_steps, 5)
            V.tensor_scalar(ids_u[:], token[:], -1.0, None, ALU.add).then_inc(final_steps, 1)

        @block.gpsimd
        def _(pool):
            G = nc.gpsimd
            counts = [pool.alloc_register("counts_cp"), pool.alloc_register("counts_cp1")]
            credit(pool, "rstd_y", "rstd_x1", "sofar_done")
            G.memset(sofar[:], 0.0).then_inc(setup_p, 1)
            G.memset(minus_half[:], -0.5).then_inc(setup_p, 1)
            for j in range(PER):
                G.memset(tile_no[:, j:j + 1], float(j)).then_inc(setup_p, 1)
            pool.wait_ge(setup_p, 2 + PER)
            pool.sem_inc(tile_no_steps, 1)

            def stage1(c):
                for var, eps_done, done in (("var_y", "veps_y", "rstd_y"), ("var_x1", "veps_x1", "rstd_x1")):
                    wait_apart(pool, counts, (setup_p, 2 + PER), (S[var], this(c)))
                    inverse_std(pool, nc, rstd[:], mv[:, :, 1], minus_half[:], veps[:], S[eps_done], c + 1, S[done])

            def stage2(c):
                pool.wait_ge(S["ranks_ready"], this(c))
                for j in range(PER):
                    ins = G.tensor_tensor(sofar[:], sofar[:], chosen[:, j, :], ALU.add)
                    if j < PER - 1:
                        ins.then_inc(sofar_steps, 1)
                        pool.wait_ge(sofar_steps, c * (PER - 1) + (j + 1))
                ins.then_inc(S["sofar_done"], 1)
                wait_apart(pool, counts, (setup_p, 2 + PER), (S["ids_parts_done"], this(c)))
                G.tensor_scalar(tile_no[:], tile_no[:], float(PER), None, ALU.add).then_inc(tile_no_steps, 1)

            stage1(0)
            with pool.Fori(0, CHUNKS - 1) as i:
                stage1(i + 1)
                stage2(i)
            stage2(CHUNKS - 1)

        @block.scalar
        def _(act):
            credit(act, "attT_done", "xfT_done", "scores_done", "shared_sig", "shared_done", "ids_parts_done", "x1_kept")

            def copy_attT(c):
                act.wait_ge(S["attT_turned"], this(c))
                nc.scalar.copy(turned_sb[:], psA[:]).then_inc(S["attT_done"], 1)

            def stage1(c):
                act.wait_ge(S["x1_done"], this(c))
                nc.scalar.copy(k["x1"][:, bass.ds(c * PER, PER), :], x1c[:]).then_inc(S["x1_kept"], 1)
                act.wait_ge(S["xf_turned"], this(c))
                nc.scalar.copy(xfT[:], psA[:]).then_inc(S["xfT_done"], 1)
                act.wait_ge(S["logits_ready"], this(c))
                act.wait_ge(S["picked_done"], last(c))
                nc.scalar.activation(scores[:].rearrange("p j e -> p (j e)"), psG[:, 0:PER * E], ACT.Sigmoid).then_inc(S["scores_done"], 1)
                act.wait_ge(S["gate_up_ready"], this(c))
                nc.scalar.activation(sg[:], psD[:], ACT.Sigmoid).then_inc(S["shared_sig"], 1)
                act.wait_ge(S["down_ready"], this(c))
                act.wait_ge(shared_stored, c * 16 + 16)
                nc.scalar.copy(shared[:].rearrange("p j d -> p (j d)"), psB[:]).then_inc(S["shared_done"], 1)

            def number(c):
                act.wait_ge(S["hot_e_done"], this(c))
                act.wait_ge(tile_no_steps, c + 1)
                act.wait_ge(S["ids_ready"], last(c))
                nc.scalar.activation(id_parts[:, :, 0, :], hot_e[:], ACT.Copy, scale=k["token_lo"][:])
                for j in range(PER):
                    ks = slice(j * TOPK, (j + 1) * TOPK)
                    ins = nc.scalar.activation(id_parts[:, ks, 1, :], hot_e[:, ks, :], ACT.Copy, scale=tile_no[:, j:j + 1])
                ins.then_inc(S["ids_parts_done"], 1)

            act.wait_ge(setup_p, 2)
            nc.scalar.activation(sg[:, 0:PER], minus_half[:], ACT.Sigmoid)
            copy_attT(0)
            stage1(0)
            copy_attT(1)
            with act.Fori(0, CHUNKS - 2) as i:
                stage1(i + 1)
                copy_attT(i + 2)
                number(i)
            stage1(CHUNKS - 1)
            number(CHUNKS - 2)
            number(CHUNKS - 1)

        @block.tensor
        def _(pe):
            M = nc.tensor.matmul
            credit(pe, "attT_turned", "projected", "xf_turned", "logits_ready", "gate_up_ready", "down_ready",
                   "ranks_ready", "ids_ready")
            pe.wait_ge(setup_v, 3)
            pe.wait_ge(setup_p, 1)
            M(psF[:, 0:2 * E], nothing[:], nothing[:], start=True, stop=False)

            def by_tile(bank, src, w, done, width=P):
                for j in range(PER):
                    mm = M(bank[:, j * width:(j + 1) * width], src[:, j * P:(j + 1) * P], w, start=True, stop=True)
                mm.then_inc(S[done], 1)

            def project(c):
                pe.wait_ge(S["normed_done"], this(c))
                pe.wait_ge(S["xfT_done"], last(c))
                for j in range(PER):
                    mm = nc.tensor.transpose(psA[:, j * P:(j + 1) * P], normed[:, j, :], k["ident"][:])
                mm.then_inc(S["attT_turned"], 1)
                pe.wait_ge(S["attT_done"], this(c))
                pe.wait_ge(S["shared_done"], last(c))
                by_tile(psB, turned_sb, k["w_o"][:], "projected")

            def experts_input(c):
                pe.wait_ge(S["xf_done"], this(c))
                for j in range(PER):
                    mm = nc.tensor.transpose(psA[:, j * P:(j + 1) * P], xf[:, j, :], k["ident"][:])
                mm.then_inc(S["xf_turned"], 1)
                pe.wait_ge(S["xfT_done"], this(c))
                pe.wait_ge(S["scores_done"], last(c))
                by_tile(psG, xfT, k["gate"][:], "logits_ready", E)
                pe.wait_ge(S["shared_h"], last(c))
                M(psD[:], k["s_gate"][:], xfT[:], start=True, stop=True)
                M(psE[:], k["s_up"][:], xfT[:], start=True, stop=True).then_inc(S["gate_up_ready"], 1)
                pe.wait_ge(S["shared_h"], this(c))
                by_tile(psB, sh, k["s_down"][:], "down_ready")

            def ranks(c):
                pe.wait_ge(S["chosen_done"], this(c))
                pe.wait_ge(S["sofar_done"], last(c))
                for j in range(PER):
                    out = psC[:, j * E:(j + 1) * E]
                    M(out, before[:], chosen[:, j, :], start=True, stop=False)
                    for jj in range(j):
                        M(out, ones[:], chosen[:, jj, :], start=False, stop=False)
                    mm = M(out, ones[:], sofar[:], start=False, stop=True)
                mm.then_inc(S["ranks_ready"], 1)

            def slots(c, final):
                pe.wait_ge(S["ids_parts_done"], this(c))
                pe.wait_ge(S["hot_s_done"], this(c))
                for n_ in range(PER * TOPK):
                    mm = M(psF[:, 0:2 * E], hot_s[:, n_, :], id_parts[:, n_].rearrange("p a e -> p (a e)"),
                           start=False, stop=(final and n_ == PER * TOPK - 1))
                mm.then_inc(S["ids_ready"], 1)

            project(0)
            experts_input(0)
            project(1)
            with pe.Fori(0, CHUNKS - 2) as i:
                ranks(i)
                experts_input(i + 1)
                project(i + 2)
                slots(i, False)
            ranks(CHUNKS - 2)
            experts_input(CHUNKS - 1)
            slots(CHUNKS - 2, False)
            ranks(CHUNKS - 1)
            slots(CHUNKS - 1, True)


def run_experts(nc, table, slot_ids, w13, w2_t, consts, sums):
    Q = 4
    PAIRS = E // (2 * Q)
    with ExitStack() as ctx:
        sb = lambda name, shape, dt=F32: ctx.enter_context(nc.sbuf_tensor(name, shape, dt))
        ps = lambda name: ctx.enter_context(nc.psum_tensor(name, [P, CHUNK], F32))
        sem = lambda name: ctx.enter_context(nc.semaphore(name))
        two = lambda make, name, *args: [make(f"{name}{a}", *args) for a in range(2)]
        ident = consts["ident"]
        up_w, down_w = two(sb, "up_w", [P, 2 * Q * F]), two(sb, "down_w", [P, Q // 2 * DIM])
        ids = sb("idsD", [P, E], U32)
        ids_g, ids_s = two(sb, "ids_g", [P, Q], U32), two(sb, "ids_s", [P, Q], U32)
        xe = two(sb, "xe", [P, Q, ROW])
        xeT = two(sb, "xeT", [P, Q * P])
        gsig = two(sb, "gsig", [P, 2 * P])
        h = two(sb, "h", [P, 2 * P])
        out = two(sb, "out", [P, Q, DIM])
        psX, psH1, psH3, psY = two(ps, "psX"), two(ps, "psH1"), two(ps, "psH3"), two(ps, "psY")
        ids_in = sem("ids_in")
        gathered, w_in = two(sem, "gathered"), two(sem, "w_in")
        ids_g_ready, ids_s_ready = two(sem, "ids_g_ready"), two(sem, "ids_s_ready")
        turned, xeT_ready, up_ready = two(sem, "turnedD"), two(sem, "xeT_ready"), two(sem, "up_ready")
        sig_ready, half_ready, h_ready, y_ready = two(sem, "sig_ready"), two(sem, "half_ready"), two(sem, "h_ready"), two(sem, "y_ready")
        out_ready = sem("out_ready")
        added = [sem(f"added{k}") for k in range(Q)]

        def adds_before(pair, a, rounds):
            if isinstance(pair, int) and pair * 2 + a < rounds:
                return [[] for k in range(Q)]
            return [[(added[k], (pair * 2 + a) * 16 + 16 * (1 - rounds))] for k in range(Q)]

        block = ctx.enter_context(nc.Block())

        @block.sync
        def _(sp):
            sp.dma_start(ids[:], slot_ids).then_inc(ids_in, 16)
            with sp.Fori(0, PAIRS) as i:
                for a in range(2):
                    sp.wait_ge(y_ready[a], i + 1)
                    for dst, src in ((up_w[a], w13), (down_w[a], w2_t)):
                        width = dst.shape[1]
                        sp.dma_start(dst[:], src[:, bass.ds(i * (2 * width) + a * width, width)]).then_inc(w_in[a], 16)

        @block.gpsimd
        def _(pool):
            counts = [pool.alloc_register(f"counts_d{k}") for k in range(3)]

            def gather(pair, a):
                wait_apart(pool, counts, (ids_in, 16), (ids_g_ready[a], pair + 1))
                for k in range(Q):
                    pool.indirect_dma_start(out=xe[a][:, k, :], out_offset=None, in_=table,
                                            in_offset=bass.IndirectOffsetOnAxis(ap=ids_g[a][:, k:k + 1], axis=0)).then_inc(gathered[a], 16)

            def add(pair, a):
                n = pair * 2 + a
                for k in range(Q):
                    wait_apart(pool, counts, (ids_in, 16), (ids_s_ready[a], pair + 1), (out_ready, n * Q + (Q + k + 1)),
                               *adds_before(pair, a, 1)[k])
                    pool.indirect_dma_start(out=sums[k], out_offset=bass.IndirectOffsetOnAxis(ap=ids_s[a][:, k:k + 1], axis=0),
                                            in_=out[a][:, k, :], in_offset=None, compute_op=ALU.add).then_inc(added[k], 16)

            def rounds(pair):
                gather(pair, 1)
                add(pair, 0)
                gather(pair + 1, 0)
                add(pair, 1)

            gather(0, 0)
            rounds(0)
            with pool.Fori(1, PAIRS - 1) as i:
                rounds(i)
            gather(PAIRS - 1, 1)
            for a in range(2):
                add(PAIRS - 1, a)
            for k in range(Q):
                pool.wait_ge(added[k], 2 * PAIRS * 16)

        @block.vector
        def _(dve):
            counts = [dve.alloc_register(f"counts_dv{k}") for k in range(4)]
            V = nc.vector

            def gather_ids(pair, a):
                V.tensor_copy(ids_g[a][:], ids[:, bass.ds(pair * (2 * Q) + a * Q, Q)]).then_inc(ids_g_ready[a], 1)

            def hidden(pair, a):
                wait_apart(dve, counts, (ids_in, 16), *sum(adds_before(pair, a, 2), []))
                V.tensor_copy(ids_s[a][:], ids[:, bass.ds(pair * (2 * Q) + a * Q, Q)]).then_inc(ids_s_ready[a], 1)
                dve.wait_ge(sig_ready[a], pair + 1)
                V.tensor_tensor(h[a][:], psH1[a][:, 0:2 * P], gsig[a][:], ALU.mult).then_inc(half_ready[a], 1)
                dve.wait_ge(half_ready[a], pair + 1)
                V.tensor_tensor(h[a][:], psH3[a][:, 0:2 * P], h[a][:], ALU.mult).then_inc(h_ready[a], 1)

            dve.wait_ge(ids_in, 16)
            for a in range(2):
                gather_ids(0, a)

            def rounds(pair):
                for a in range(2):
                    hidden(pair, a)
                    wait_apart(dve, counts, (ids_in, 16), (gathered[a], pair * 64 + 64))
                    gather_ids(pair + 1, a)

            rounds(0)
            with dve.Fori(1, PAIRS - 1) as i:
                rounds(i)
            for a in range(2):
                hidden(PAIRS - 1, a)

        @block.scalar
        def _(act):
            def rounds(pair):
                for a in range(2):
                    n = pair * 2 + a
                    act.wait_ge(turned[a], pair + 1)
                    act.wait_ge(up_ready[a], pair + 1)
                    nc.scalar.copy(xeT[a][:], psX[a][:]).then_inc(xeT_ready[a], 1)
                    act.wait_ge(up_ready[a], pair + 2)
                    nc.scalar.activation(gsig[a][:], psH1[a][:, 0:2 * P], ACT.Sigmoid).then_inc(sig_ready[a], 1)
                    act.wait_ge(y_ready[a], pair + 2)
                    for k in range(Q):
                        for buffer_free in adds_before(pair, a, 2)[k]:
                            act.wait_ge(*buffer_free)
                        nc.scalar.activation(out[a][:, k, :], psY[k % 2][:, k // 2 * P:(k // 2 + 1) * P], ACT.Copy,
                                             scale=xe[a][:, k, bass.ds(n * Q + (DIM + k), 1)]).then_inc(out_ready, 1)

            rounds(0)
            with act.Fori(1, PAIRS) as i:
                rounds(i)

        @block.tensor
        def _(pe):
            M = nc.tensor.matmul
            for a in range(2):
                pe.sem_inc(up_ready[a], 1)
                pe.sem_inc(y_ready[a], 1)
            pe.sem_inc(out_ready, Q)
            with pe.Fori(0, PAIRS) as i:
                for a in range(2):
                    n = i * 2 + a
                    pe.wait_ge(gathered[a], i * 64 + 64)
                    for k in range(Q):
                        mm = nc.tensor.transpose(psX[a][:, k * P:(k + 1) * P], xe[a][:, k, 0:DIM], ident[:])
                    mm.then_inc(turned[a], 1)
                    pe.wait_ge(xeT_ready[a], i + 1)
                    pe.wait_ge(w_in[a], i * 32 + 32)
                    for which, bank in enumerate((psH1[a], psH3[a])):
                        for k in range(Q):
                            half = F * (k % 2)
                            mm = M(bank[half:half + F, k // 2 * P:(k // 2 + 1) * P], up_w[a][:, (which * Q + k) * F:(which * Q + k + 1) * F],
                                   xeT[a][:, k * P:(k + 1) * P], start=True, stop=True)
                    mm.then_inc(up_ready[a], 1)
                    pe.wait_ge(h_ready[a], i + 1)
                    pe.wait_ge(out_ready, n * Q + Q)
                    for k in range(Q):
                        half, m = F * (k % 2), k // 2
                        mm = M(psY[k % 2][:, m * P:(m + 1) * P], h[a][half:half + F, m * P:(m + 1) * P],
                               down_w[a][half:half + F, m * DIM:(m + 1) * DIM], start=True, stop=True)
                    mm.then_inc(y_ready[a], 1)


def finish(nc, x1, sums, out):
    with ExitStack() as ctx:
        sb = lambda name, shape, dt=F32: ctx.enter_context(nc.sbuf_tensor(name, shape, dt))
        sem = lambda name: ctx.enter_context(nc.semaphore(name))
        two = lambda make, name, *args: [make(f"{name}{a}", *args) for a in range(2)]
        s = [two(sb, f"s{k}_", [P, PER, DIM]) for k in range(4)]
        res = two(sb, "res", [P, PER, DIM])
        stats = sb("statsE", [P, PER, 6])
        mv, veps, rstd = two(sb, "mvE", [P, PER, 2]), two(sb, "vepsE", [P, PER]), two(sb, "rstdE", [P, PER])
        minus_half = sb("minus_halfE", [P, PER])
        loaded, stored = two(sem, "loadedE"), two(sem, "storedE")
        pool_sum, first_sum, whole_sum = sem("pool_sum"), sem("first_sum"), sem("whole_sum")
        stats_done, var_done, veps_done, rstd_done = sem("stats_doneE"), sem("var_doneE"), sem("veps_doneE"), sem("rstd_doneE")
        norm_done, res_done = sem("norm_doneE"), sem("res_doneE")
        half_made = sem("half_madeE")
        PAIRS = CHUNKS // 2
        block = ctx.enter_context(nc.Block())

        def rows(a_, pair, a):
            return a_[bass.ds(pair * (2 * CHUNK) + a * CHUNK, CHUNK), :].rearrange("(j p) d -> p j d", p=P)

        @block.sync
        def _(sp):
            for a in range(2):
                sp.sem_inc(stored[a], 16)
            with sp.Fori(0, PAIRS) as i:
                for a in range(2):
                    sp.wait_ge(res_done, i * 2 + (a + 1))
                    for k in range(4):
                        sp.dma_start(s[k][a][:], rows(sums[k], i, a)).then_inc(loaded[a], 16)

        @block.scalar
        def _(act):
            with act.Fori(0, PAIRS) as i:
                for a in range(2):
                    act.wait_ge(res_done, i * 2 + (a + 3))
                    act.dma_start(rows(out, i, a), res[a][:]).then_inc(stored[a], 16)
            for a in range(2):
                act.wait_ge(stored[a], 16 * (PAIRS + 1))

        @block.gpsimd
        def _(pool):
            counts = [pool.alloc_register("counts_e")]
            nc.gpsimd.memset(minus_half[:], -0.5).then_inc(half_made, 1)
            pool.wait_ge(half_made, 1)

            def sum_two(pair, a):
                pool.wait_ge(loaded[a], pair * 64 + 64)
                nc.gpsimd.tensor_tensor(s[2][a][:], s[2][a][:], s[3][a][:], ALU.add).then_inc(pool_sum, 1)

            def inverse(pair, a):
                wait_apart(pool, counts, (half_made, 1), (var_done, pair * 2 + (a + 1)))
                inverse_std(pool, nc, rstd[a][:], mv[a][:, :, 1], minus_half[:], veps[a][:], veps_done, pair * 2 + (a + 1), rstd_done)

            sum_two(0, 0)
            with pool.Fori(0, PAIRS - 1) as i:
                sum_two(i, 1)
                inverse(i, 0)
                sum_two(i + 1, 0)
                inverse(i, 1)
            sum_two(PAIRS - 1, 1)
            for a in range(2):
                inverse(PAIRS - 1, a)

        @block.vector
        def _(dve):
            counts = [dve.alloc_register("counts_ev")]
            V = nc.vector
            dve.sem_inc(res_done, 2)

            def sum_and_stats(pair, a):
                dve.wait_ge(loaded[a], pair * 64 + 64)
                V.tensor_tensor(s[0][a][:], s[0][a][:], s[1][a][:], ALU.add).then_inc(first_sum, 1)
                dve.wait_ge(first_sum, pair * 2 + (a + 1))
                dve.wait_ge(pool_sum, pair * 2 + (a + 1))
                V.tensor_tensor(s[0][a][:], s[0][a][:], s[2][a][:], ALU.add).then_inc(whole_sum, 1)
                dve.wait_ge(whole_sum, pair * 2 + (a + 1))
                for j in range(PER):
                    ins = V.bn_stats(stats[:, j, :], s[0][a][:, j, :])
                ins.then_inc(stats_done, 1)
                wait_apart(dve, counts, (half_made, 1), (stats_done, pair * 2 + (a + 1)))
                for j in range(PER):
                    ins = V.bn_aggr(mv[a][:, j, :], stats[:, j, :])
                ins.then_inc(var_done, 1)

            def norm_and_residual(pair, a):
                dve.wait_ge(rstd_done, pair * 2 + (a + 1))
                for j in range(PER):
                    ins = V.tensor_scalar(s[0][a][:, j, :], s[0][a][:, j, :], mv[a][:, j, 0:1], rstd[a][:, j:j + 1], ALU.subtract, ALU.mult)
                ins.then_inc(norm_done, 1)
                dve.wait_ge(norm_done, pair * 2 + (a + 1))
                dve.wait_ge(stored[a], pair * 16 + 16)
                V.tensor_tensor(res[a][:], s[0][a][:], x1[:, bass.ds(pair * (2 * PER) + a * PER, PER), :], ALU.add).then_inc(res_done, 1)

            sum_and_stats(0, 0)
            with dve.Fori(0, PAIRS - 1) as i:
                sum_and_stats(i, 1)
                norm_and_residual(i, 0)
                sum_and_stats(i + 1, 0)
                norm_and_residual(i, 1)
            sum_and_stats(PAIRS - 1, 1)
            for a in range(2):
                norm_and_residual(PAIRS - 1, a)


def program(nc, x, ln_g, ln_b, w_qkv, b_qkv, w_rel_rows, w_out, b_out, gate_t, e_bias, w13, w2_t,
            shared_gate_t, shared_up_t, shared_down_t, q_table, k_table, ident, before, iota, out):
    dram = lambda name, shape, dt=F32: nc.dram_tensor(name, shape, dt).ap()
    q_image = dram("q_image", [3, HD, CHUNKS, H, CHUNK], BF16)
    k_image = dram("k_image", [3, HD, CHUNKS, H, CHUNK], BF16)
    bias_q_image = dram("bias_q_image", [3, HD, 2, H, CHUNK], BF16)
    bias_k_image = dram("bias_k_image", [3, HD, 2, HG, CHUNK], BF16)
    v_padded = dram("v_padded", [P, TILES, H * VW])
    att = dram("att", [N, H, HD + 1])
    table = dram("table", [ROWS, ROW])
    sums = [dram(f"sums{k}", [ROWS, DIM]) for k in range(4)]
    slot_ids = dram("slot_ids", [P, E], U32)
    project_tokens(nc, x, ln_g, ln_b, w_qkv, b_qkv, w_rel_rows, q_table, k_table, ident,
                   q_image, k_image, v_padded, bias_q_image, bias_k_image)
    row = lambda a, n: a.rearrange("(o d) -> o d", o=1).to_broadcast([P, n])
    with ExitStack() as ctx:
        consts, later = {}, []
        for name, shape, src in (
            ("ident", [P, P], ident), ("before", [P, P], before), ("iota", [P, P], iota[0:1, :].to_broadcast([P, P])),
            ("token_lo", [P, 1], iota[1:2, :].rearrange("o p -> p o")), ("free_id", [P, 1], iota[2:3, :].rearrange("o p -> p o")),
            ("expert_1", [P, E], iota[1:2, 0:E].to_broadcast([P, E])), ("earlier", [P, E], iota[3:4, 0:E].to_broadcast([P, E])),
            ("w_o", [P, DIM], w_out), ("b_o", [P, DIM], row(b_out, DIM)), ("gate", [P, E], gate_t), ("e_bias", [P, E], row(e_bias, E)),
            ("s_gate", [P, P], shared_gate_t), ("s_up", [P, P], shared_up_t), ("s_down", [P, P], shared_down_t),
            ("x1", [P, TILES, DIM], None),
        ):
            consts[name] = ctx.enter_context(nc.sbuf_tensor(f"const_{name}", shape, F32))
            if src is not None:
                later.append((consts[name][:], src))
        attend(nc, ident, q_image, k_image, v_padded, bias_q_image, bias_k_image, att, later, sums[1:],
               [a[N:ROWS, :] for a in (*sums, table)])
        route(nc, x, att, consts, table, sums[0], slot_ids)
        run_experts(nc, table, slot_ids, w13, w2_t, consts, sums)
        finish(nc, consts["x1"], sums, out)


def shape_constants():
    freq = np.exp(np.arange(0, HD, 2) * (-np.log(10000.0) / HD))
    angle = np.arange(T)[None, :] * freq[:, None]
    sin, cos = np.sin(angle), np.cos(angle)
    q_table = np.stack([sin, cos, -cos, sin], axis=1).reshape(2 * HD, T)
    k_table = np.stack([cos, sin], axis=1).reshape(HD, T)
    n = np.arange(P)
    earlier = np.arange(NGROUPS)[:, None] > np.arange(NGROUPS)[None, :]
    iota = np.stack([n, n + 1, N + n + 1, np.pad(earlier.reshape(-1), (0, P - E))])
    f = lambda a: np.ascontiguousarray(a, dtype=np.float32)
    return {"q_table": f(q_table), "k_table": f(k_table), "ident": f(np.eye(P)),
            "before": f(n[:, None] < n[None, :]), "iota": f(iota)}


def place_w_rel(w_rel):
    rows = np.zeros((2 * HD, H * HD), w_rel.dtype)
    for f in range(HD // 2):
        for par in range(2):
            for s in range(2):
                rows[4 * f + 2 * par + s, 2 * f + par::HD] = w_rel[2 * f + s]
    return rows


def kernel(**inputs):
    import concourse.bacc as bacc
    from concourse.bass_utils import run_bass_kernel_spmd

    a = {k: np.asarray(v) for k, v in inputs.items()}
    by_round = lambda w: w.transpose(2, 0, 1).reshape(DIM, E // 4, 4 * F)
    arrays = {
        "x": a["L0_attn_x"].reshape(N, DIM),
        "ln_g": a["L0_attn_ln_g"], "ln_b": a["L0_attn_ln_b"],
        "w_qkv": a["L0_attn_w_qkv"], "b_qkv": a["L0_attn_b_qkv"], "w_rel_rows": place_w_rel(a["L0_attn_w_rel"]),
        "w_out": a["L0_attn_w_out"], "b_out": a["L0_attn_b_out"],
        "gate_t": a["L0_ffn_gate_weight"].T, "e_bias": a["L0_ffn_e_bias"],
        "w13": np.stack([by_round(a["L0_ffn_w1"]), by_round(a["L0_ffn_w3"])], axis=2).reshape(DIM, -1),
        "w2_t": a["L0_ffn_w2"].transpose(0, 2, 1).reshape(E * F // P, P, DIM).transpose(1, 0, 2).reshape(P, -1),
        "shared_gate_t": a["L0_ffn_shared_gate"].T, "shared_up_t": a["L0_ffn_shared_up"].T,
        "shared_down_t": a["L0_ffn_shared_down"].T,
        **shape_constants(),
    }
    nc = bacc.Bacc("TRN2", target_bir_lowering=False, num_devices=1)
    sent, args = {}, []
    for name, v in arrays.items():
        v = np.ascontiguousarray(v)
        sent[f"in_{name}"] = v
        args.append(nc.dram_tensor(f"in_{name}", v.shape, mybir.dt.from_np(v.dtype), kind="ExternalInput").ap())
    out = nc.dram_tensor("result", (N, DIM), F32, kind="ExternalOutput").ap()
    program(nc, *args, out)
    r = run_bass_kernel_spmd(nc, [sent], core_ids=[0])
    return r.results[0]["result"].reshape(B, T, DIM)
```

```python
from contextlib import ExitStack

import numpy as np

import concourse.bass as bass
from concourse import mybir

F32 = mybir.dt.float32
BF16 = mybir.dt.bfloat16
U32 = mybir.dt.uint32
ALU = mybir.AluOpType
ACT = mybir.ActivationFunctionType
AX = mybir.AxisListType

P = 128
B, T, DIM = 4, 1024, 128
H, HD = 16, 8
N = B * T
TILES = N // P
CHUNK = 512
CHUNKS = N // CHUNK
PER = CHUNK // P
EPS = 1e-5
SCALE = float(HD) ** -0.5
HG = 4
GROUPS = H // HG
VW = HD + 1
PART = P // HG

TERMS = [(0, 0), (0, 1), (0, 2), (1, 0), (1, 1), (2, 0)]
K_RUNS = [(0, 3), (3, 2), (5, 1)]
QK_ROWS = HD * len(TERMS)
SCORE_ROWS = 2 * QK_ROWS
SHIFT_ROWS = 3
STACK_ROWS = SCORE_ROWS + SHIFT_ROWS


def wait_apart(engine, registers, met, *waits):
    for register, (_, count) in zip(registers, waits):
        engine.reg_mov(register, count)
    engine.wait_ge(*met)
    for register, (semaphore, _) in zip(registers, waits):
        engine.wait_ge(semaphore, register)


def exact_pieces(dve, nc, src, rest, pieces, done, count):
    nc.vector.tensor_tensor(rest, src, pieces[0], ALU.subtract).then_inc(done, 1)
    dve.wait_ge(done, count + 1)
    nc.vector.tensor_copy(pieces[1], rest).then_inc(done, 1)
    dve.wait_ge(done, count + 2)
    nc.vector.tensor_tensor(pieces[2], rest, pieces[1], ALU.subtract).then_inc(done, 1)


def project_tokens(nc, x, ln_g, ln_b, w_qkv, b_qkv, w_rel_rows, q_table, k_table, ident_in,
                   q_image, k_image, v_columns, bias_q_image, bias_k_image):
    with ExitStack() as ctx:
        sb = lambda name, shape, dt=F32: ctx.enter_context(nc.sbuf_tensor(name, shape, dt))
        ps = lambda name: ctx.enter_context(nc.psum_tensor(name, [P, CHUNK], F32))
        sem = lambda name: ctx.enter_context(nc.semaphore(name))
        two = lambda make, name, *args: [make(f"{name}{a}", *args) for a in range(2)]

        xc = two(sb, "xc", [P, PER, DIM])
        stats = sb("stats", [P, PER, 6])
        mv = two(sb, "mv", [P, PER, 2])
        var2 = two(sb, "var2", [P, PER])
        rstd = two(sb, "rstd", [P, PER])
        minus_half = sb("minus_halfA", [P, PER])
        xn = two(sb, "xn", [P, PER, DIM])
        xnT = two(sb, "xnT", [P, CHUNK])
        w = sb("w", [P, 3 * DIM])
        ident = sb("ident", [P, P])
        gcol = sb("gcol", [P, 1])
        bcol = sb("bcol", [P, 1])
        bqcol = sb("bqcol", [P, 1])
        bkcol = sb("bkcol", [P, 1])
        bv = sb("bv", [P, DIM])
        q_full, k_full = two(sb, "q_full", [P, CHUNK]), two(sb, "k_full", [P, CHUNK])
        q_rest, k_rest = two(sb, "q_rest", [P, CHUNK]), two(sb, "k_rest", [P, CHUNK])
        q_piece, k_piece = two(sb, "q_piece", [P, 3, CHUNK], BF16), two(sb, "k_piece", [P, 3, CHUNK], BF16)
        vst = two(sb, "vst", [P, PER, H, VW])
        wrow = sb("wrow", [2 * HD, P])
        tabq = sb("tabq", [2 * HD, T])
        bias_q = sb("bias_q", [P, T])
        bias_rest = sb("bias_rest", [P, T])
        bias_p = sb("bias_p", [P, 3, T], BF16)
        tabk = sb("tabk", [HD, T])
        tabk_rest = sb("tabk_rest", [HD, T])
        tabk_p = sb("tabk_p", [HD, 3, T], BF16)

        psT, psQ, psK, psV = two(ps, "psT"), two(ps, "psQ"), two(ps, "psK"), two(ps, "psV")

        const_in, bias_in = sem("const_in"), sem("bias_in")
        x_in = two(sem, "x_in")
        stats_done, aggr_done = sem("stats_done"), sem("aggr_done")
        var_done, rstd_done, xn_done = two(sem, "var_done"), two(sem, "rstd_done"), two(sem, "xn_done")
        turned, xnT_done = two(sem, "turned"), two(sem, "xnT_done")
        q_ready, k_ready, v_ready = two(sem, "q_ready"), two(sem, "k_ready"), two(sem, "v_ready")
        q_full_done, k_full_done = two(sem, "q_full_done"), two(sem, "k_full_done")
        q_split, k_split, v_done = two(sem, "q_split"), two(sem, "k_split"), two(sem, "v_done")
        stored = two(sem, "stored")
        scaled_b = sem("scaled_b")
        half_made = sem("constants_made")
        bias_ready, bias_read = sem("bias_ready"), sem("bias_read")
        bias_split, table_split, bias_stored = sem("bias_split"), sem("table_split"), sem("bias_stored")

        CONSTS, BIAS_CONSTS = 8 * 16, 3 * 16
        PAIRS = CHUNKS // 2
        STORES = 3 * 16
        block = ctx.enter_context(nc.Block())

        @block.sync
        def _(sp):
            counts = [sp.alloc_register("counts_as")]

            def load(chunk, a):
                sp.dma_start(xc[a][:], x[bass.ds(chunk * CHUNK, CHUNK), :].rearrange("(j p) d -> p j d", p=P)).then_inc(x_in[a], 16)

            def store(pair, a):
                for done, image, piece in ((q_split, q_image, q_piece), (k_split, k_image, k_piece)):
                    wait_apart(sp, counts, (const_in, CONSTS), (done[a], pair * 3 + 6))
                    sp.dma_start(image[bass.ds(pair * 2 + a, 1)].rearrange("o p d h i -> (o d h) p i"), piece[a][:]).then_inc(stored[a], 16)
                wait_apart(sp, counts, (const_in, CONSTS), (v_done[a], pair + 2))
                sp.dma_start(v_columns[:, bass.ds(pair * (2 * PER) + a * PER, PER), :],
                             vst[a][:].rearrange("p j h c -> p j (h c)")).then_inc(stored[a], 16)

            for a in range(2):
                sp.sem_inc(stored[a], STORES)
            load(0, 0)
            for dst, src in (
                (gcol[:], ln_g.rearrange("(p o) -> p o", o=1)),
                (bcol[:], ln_b.rearrange("(p o) -> p o", o=1)),
                (bqcol[:], b_qkv[0:DIM].rearrange("(p o) -> p o", o=1)),
                (bkcol[:], b_qkv[DIM:2 * DIM].rearrange("(p o) -> p o", o=1)),
                (bv[:], b_qkv[2 * DIM:3 * DIM].rearrange("(o d) -> o d", o=1).to_broadcast([P, DIM])),
            ):
                sp.dma_start(dst, src).then_inc(const_in, 16)
            load(1, 1)
            for a in range(2):
                sp.wait_ge(xn_done[a], 2)
                load(2 + a, a)
            sp.wait_ge(bias_split, 3)
            for half in range(2):
                sp.dma_start(bias_q_image[half].rearrange("p e h i -> (e h) p i"),
                             bias_p[:, :, half * CHUNK:(half + 1) * CHUNK]).then_inc(bias_stored, 16)
            sp.wait_ge(table_split, 4)
            for half in range(2):
                for h in range(HG):
                    sp.dma_start(bias_k_image[half, :, :, h, :].rearrange("p e i -> e p i"),
                                 tabk_p[:, :, half * CHUNK:(half + 1) * CHUNK]).then_inc(bias_stored, 16)
            with sp.Fori(0, PAIRS - 2) as i:
                for a in range(2):
                    store(i, a)
                    sp.wait_ge(xn_done[a], i + 3)
                    load(i * 2 + (4 + a), a)
            for pair in (PAIRS - 2, PAIRS - 1):
                for a in range(2):
                    store(pair, a)
            sp.wait_ge(bias_stored, (2 + 2 * HG) * 16)
            for a in range(2):
                sp.wait_ge(stored[a], (PAIRS + 1) * STORES)

        @block.vector
        def _(dve):
            counts = [dve.alloc_register("counts_av")]
            for a in range(2):
                dve.sem_inc(v_done[a], 1)
                dve.sem_inc(q_split[a], 3)
                dve.sem_inc(xn_done[a], 1)

            def norm_stats(pair, a, count):
                dve.wait_ge(x_in[a], pair * 16 + 16)
                for j in range(PER):
                    nc.vector.bn_stats(stats[:, j, :], xc[a][:, j, :]).then_inc(stats_done, 1)
                for j in range(PER):
                    wait_apart(dve, counts, (scaled_b, 1), (stats_done, count + (j + 1)))
                    nc.vector.bn_aggr(mv[a][:, j, :], stats[:, j, :]).then_inc(aggr_done, 1)
                dve.wait_ge(aggr_done, count + PER)
                nc.vector.tensor_scalar(var2[a][:], mv[a][:, :, 1], 1.0 + EPS, EPS * EPS, ALU.mult, ALU.add).then_inc(var_done[a], 1)

            def norm_rows(pair, a):
                dve.wait_ge(rstd_done[a], pair + 1)
                dve.wait_ge(turned[a], pair + 1)
                for j in range(PER):
                    ins = nc.vector.tensor_scalar(xn[a][:, j, :], xc[a][:, j, :], mv[a][:, j, 0:1], rstd[a][:, j:j + 1],
                                                  ALU.subtract, ALU.mult)
                ins.then_inc(xn_done[a], 1)

            def split_q_add_v(pair, a):
                dve.wait_ge(q_full_done[a], pair * 2 + 2)
                exact_pieces(dve, nc, q_full[a][:], q_rest[a][:], [q_piece[a][:, p, :] for p in range(3)],
                             q_split[a], pair * 3 + 3)
                dve.wait_ge(v_ready[a], pair + 2)
                dve.wait_ge(stored[a], (pair + 1) * STORES)
                nc.vector.tensor_tensor(
                    vst[a][:, :, :, 0:HD], psV[a][:].rearrange("p (j h d) -> p j h d", j=PER, h=H),
                    bv[:].rearrange("p (o h d) -> p o h d", o=1, h=H).to_broadcast([P, PER, H, HD]),
                    ALU.add).then_inc(v_done[a], 1)

            dve.wait_ge(const_in, CONSTS)
            nc.vector.tensor_scalar(bqcol[:], bqcol[:], SCALE, None, ALU.mult).then_inc(scaled_b, 1)
            for a in range(2):
                norm_stats(0, a, PER * a)
                norm_rows(0, a)
            dve.wait_ge(bias_read, 4)
            exact_pieces(dve, nc, bias_q[:], bias_rest[:], [bias_p[:, p, :] for p in range(3)], bias_split, 0)
            dve.wait_ge(table_split, 1)
            exact_pieces(dve, nc, tabk[:], tabk_rest[:], [tabk_p[:, p, :] for p in range(3)], table_split, 1)
            dve.wait_ge(half_made, 3)
            with dve.Fori(0, PAIRS - 1) as i:
                for a in range(2):
                    norm_stats(i + 1, a, i * (2 * PER) + (2 + a) * PER)
                    split_q_add_v(i, a)
                    norm_rows(i + 1, a)
            for a in range(2):
                split_q_add_v(PAIRS - 1, a)

        @block.gpsimd
        def _(pool):
            counts = [pool.alloc_register("counts_ap"), pool.alloc_register("counts_ap1")]
            nc.gpsimd.memset(minus_half[:], -0.5).then_inc(half_made, 1)
            for a in range(2):
                pool.sem_inc(k_split[a], 3)

            def inverse(pair, a):
                pool.wait_ge(var_done[a], pair + 1)
                nc.gpsimd.tensor_tensor(rstd[a][:], var2[a][:], minus_half[:], ALU.pow).then_inc(rstd_done[a], 1)

            def split_k(pair, a):
                pool.wait_ge(k_full_done[a], pair * 2 + 2)
                pieces = [k_piece[a][:, p, :] for p in range(3)]
                nc.gpsimd.tensor_tensor(k_rest[a][:], k_full[a][:], pieces[0], ALU.subtract).then_inc(k_split[a], 1)
                wait_apart(pool, counts, (half_made, 1), (k_split[a], pair * 3 + 4))
                nc.gpsimd.tensor_copy(pieces[1], k_rest[a][:]).then_inc(k_split[a], 1)
                pool.wait_ge(k_split[a], pair * 3 + 5)
                nc.gpsimd.tensor_tensor(pieces[2], k_rest[a][:], pieces[1], ALU.subtract).then_inc(k_split[a], 1)

            pool.wait_ge(half_made, 1)
            for a in range(2):
                inverse(0, a)
            for a in range(2):
                nc.gpsimd.memset(vst[a][:, :, :, HD:VW], 1.0).then_inc(half_made, 1)
            with pool.Fori(0, PAIRS - 1) as i:
                for a in range(2):
                    inverse(i + 1, a)
                    split_k(i, a)
            for a in range(2):
                split_k(PAIRS - 1, a)

        @block.scalar
        def _(act):
            for dst, src in ((wrow[:], w_rel_rows), (tabq[:], q_table), (tabk[:], k_table)):
                act.dma_start(dst, src).then_inc(bias_in, 16)
            for dst, src in ((ident[:], ident_in), (w[:, 0:DIM], w_qkv[:, 0:DIM]), (w[:, DIM:3 * DIM], w_qkv[:, DIM:3 * DIM])):
                act.dma_start(dst, src).then_inc(const_in, 16)
            for half in range(2):
                act.wait_ge(bias_ready, half + 1)
                for dst in (bias_q[:, half * CHUNK:(half + 1) * CHUNK], bias_p[:, 0, half * CHUNK:(half + 1) * CHUNK]):
                    nc.scalar.copy(dst, [psQ, psK][half][0][:]).then_inc(bias_read, 1)
            nc.scalar.copy(tabk_p[:, 0, :], tabk[:]).then_inc(table_split, 1)
            act.wait_ge(const_in, CONSTS)
            act.wait_ge(scaled_b, 1)
            with act.Fori(0, PAIRS) as i:
                for a in range(2):
                    act.wait_ge(turned[a], i + 2)
                    act.wait_ge(v_ready[a], i + 1)
                    nc.scalar.activation(xnT[a][:], psT[a][:], ACT.Identity, bias=bcol[:], scale=gcol[:]).then_inc(xnT_done[a], 1)
                    act.wait_ge(q_ready[a], i + 1)
                    act.wait_ge(q_split[a], i * 3 + 3)
                    act.wait_ge(stored[a], (i + 1) * STORES)
                    for dst in (q_full[a][:], q_piece[a][:, 0, :]):
                        nc.scalar.activation(dst, psQ[a][:], ACT.Identity, bias=bqcol[:], scale=SCALE).then_inc(q_full_done[a], 1)
                    act.wait_ge(k_ready[a], i + 1)
                    act.wait_ge(k_split[a], i * 3 + 3)
                    for dst in (k_full[a][:], k_piece[a][:, 0, :]):
                        nc.scalar.activation(dst, psK[a][:], ACT.Identity, bias=bkcol[:]).then_inc(k_full_done[a], 1)

        @block.tensor
        def _(pe):
            for a in range(2):
                pe.sem_inc(turned[a], 1)
                pe.sem_inc(v_ready[a], 1)
            pe.wait_ge(bias_in, BIAS_CONSTS)
            for half in range(2):
                nc.tensor.matmul([psQ, psK][half][0][:], wrow[:], tabq[:, half * CHUNK:(half + 1) * CHUNK],
                                 start=True, stop=True).then_inc(bias_ready, 1)
            pe.wait_ge(const_in, CONSTS)
            pe.wait_ge(bias_read, 4)
            with pe.Fori(0, PAIRS) as i:
                for a in range(2):
                    pe.wait_ge(xn_done[a], i + 2)
                    for j in range(PER):
                        mm = nc.tensor.transpose(psT[a][:, j * P:(j + 1) * P], xn[a][:, j, :], ident[:])
                    mm.then_inc(turned[a], 1)
                    pe.wait_ge(xnT_done[a], i + 1)
                    nc.tensor.matmul(psQ[a][:], w[:, 0:DIM], xnT[a][:], start=True, stop=True).then_inc(q_ready[a], 1)
                    nc.tensor.matmul(psK[a][:], w[:, DIM:2 * DIM], xnT[a][:], start=True, stop=True).then_inc(k_ready[a], 1)
                    pe.wait_ge(v_done[a], i + 1)
                    for j in range(PER):
                        mm = nc.tensor.matmul(psV[a][:, j * P:(j + 1) * P], xnT[a][:, j * P:(j + 1) * P],
                                              w[:, 2 * DIM:3 * DIM], start=True, stop=True)
                    mm.then_inc(v_ready[a], 1)


UNITS = 2 * GROUPS
STEPS = 32
BATCH_STEPS = UNITS * STEPS
LEAD = 48
ST_BANKS = 3
S_BANKS = 3
P_SLOTS = 16
PV_LAG = 6
J_UOUT, J_OTURN, J_OCOPY = 9, 12, 14
J_MTURN, J_MCOPY = 21, 22
LOADS = 2 * len(TERMS) + 1


def attend(nc, ident_in, q_image, k_image, v_columns, bias_q_image, bias_k_image, att, later, cleared_dram, spare_rows):
    with ExitStack() as ctx:
        sb = lambda name, shape, dt=F32: ctx.enter_context(nc.sbuf_tensor(name, shape, dt))
        ps = lambda name: ctx.enter_context(nc.psum_tensor(name, [P, CHUNK], F32))
        sem = lambda name: ctx.enter_context(nc.semaphore(name))

        q_stack = [sb(f"q_stack{g}", [STACK_ROWS, 2, HG, CHUNK], BF16) for g in range(GROUPS)]
        k_stack = [sb(f"k_stack{g}", [STACK_ROWS, 2, HG, CHUNK], BF16) for g in range(GROUPS)]
        values = [sb(f"values{g}", [P, T // P, HG, VW]) for g in range(GROUPS)]
        probs = sb("probs", [P, P_SLOTS, CHUNK])
        half_max = [sb(f"half_max{v}", [P, STEPS]) for v in range(2)]
        minus_max = sb("minus_max", [P, STEPS // 2])
        shift_rest = sb("shift_rest", [P, STEPS // 2])
        shift = sb("shift", [P, 3, STEPS // 2], BF16)
        shiftT = sb("shiftT", [3 * STEPS // 2, P], BF16)
        unit_out = sb("unit_out", [P, CHUNK])
        unit_rows = sb("unit_rows", [P, PER, HG, HD + 1])
        ident = sb("identB", [P, P])
        ident16 = sb("ident16", [P, P], BF16)

        st_bank = [ps(f"st_bank{v}") for v in range(ST_BANKS)]
        s_bank = [ps(f"s_bank{v}") for v in range(S_BANKS)]
        pv_bank = ps("pv_bank")
        misc = ps("misc")

        zeros = sb("zeros", [P, ROW])
        no_rows = sb("no_rows", [P, CHUNK], BF16)
        no_rows_done = sem("no_rows_done")
        ident_ready = sem("ident_ready")
        later_in, zeros_done, cleared = sem("later_in"), sem("zeros_done"), sem("cleared")
        ident16_done = sem("ident16_done")
        ones_done = sem("ones_done")
        bias_rows_in = [sem(f"bias_rows_in{g}") for g in range(GROUPS)]
        loaded = [sem(f"loaded{g}") for g in range(GROUPS)]
        s_ready = sem("s_ready")
        max_done = sem("max_done")
        row_max_done = sem("row_max_done")
        shift_done = sem("shift_done")
        shift_turned = sem("shift_turned")
        shiftT_done = sem("shiftT_done")
        shift_in = sem("shift_in")
        st_ready = sem("st_ready")
        exp_done = sem("exp_done")
        pv_done = sem("pv_done")
        unit_out_done = sem("unit_out_done")
        out_turned = sem("out_turned")
        rows_done = sem("rows_done")
        rows_stored = sem("rows_stored")

        block = ctx.enter_context(nc.Block())

        MAX0, EXP0, PV0 = S_BANKS, ST_BANKS, P_SLOTS // HG

        def before(s, ring):
            if s >= ring:
                return s - ring
            last = BATCH_STEPS - 1
            while last % ring != s:
                last -= 1
            return last - BATCH_STEPS

        def split(s):
            return s // STEPS, s % STEPS

        def load(sp, b, g):
            heads, chunks = slice(HG * g, HG * (g + 1)), bass.ds(b * 2, 2)
            for t, (piece, _) in enumerate(TERMS):
                sp.dma_start(q_stack[g][HD * t:HD * (t + 1)].rearrange("r c h i -> r c (h i)"), q_image[chunks, piece, :, heads, :]
                             .rearrange("c d h i -> d c (h i)")).then_inc(loaded[g], 16)
            for first, n in K_RUNS:
                rows = slice(HD * first, HD * (first + n))
                sp.dma_start(k_stack[g][rows].rearrange("r c h i -> r c (h i)"), k_image[chunks, 0:n, :, heads, :]
                             .rearrange("c p d h i -> (p d) c (h i)")).then_inc(loaded[g], 16)
            sp.dma_start(values[g][:].rearrange("p k h c -> p k (h c)"),
                         v_columns[:, bass.ds(b * (T // P), T // P), HG * VW * g:HG * VW * (g + 1)]).then_inc(loaded[g], 16)

        LOAD = 16 * (len(TERMS) + len(K_RUNS) + 1)

        def load_bias(sp, g):
            for t, (piece, _) in enumerate(TERMS):
                r = QK_ROWS + HD * t
                sp.dma_start(q_stack[g][r:r + HD].rearrange("r c h i -> r c (h i)"),
                             bias_q_image[:, piece, :, HG * g:HG * (g + 1), :].rearrange("c e h i -> e c (h i)")).then_inc(bias_rows_in[g], 16)
            for first, n in K_RUNS:
                rows = slice(QK_ROWS + HD * first, QK_ROWS + HD * (first + n))
                sp.dma_start(k_stack[g][rows].rearrange("r c h i -> r c (h i)"),
                             bias_k_image[:, 0:n].rearrange("c p e h i -> (p e) c (h i)")).then_inc(bias_rows_in[g], 16)

        LOAD_BIAS = 16 * (len(TERMS) + len(K_RUNS))

        def put_shift(sp, unit, n):
            g, half = unit // 2, unit % 2
            sp.wait_ge(shiftT_done, n + 1)
            for p in range(3):
                r = SCORE_ROWS + p
                sp.dma_start(q_stack[g][r:r + 1, half].rearrange("o h i -> o (h i)"),
                             shiftT[16 * p:16 * (p + 1), :]).then_inc(shift_in, 16)

        def store_rows(sp, b, unit, n):
            g, half = unit // 2, unit % 2
            sp.wait_ge(rows_done, n + 2)
            sp.dma_start(att[bass.ds(b * T + half * CHUNK, CHUNK), HG * g:HG * (g + 1), :].rearrange("(t p) h c -> p t (h c)", p=P),
                         unit_rows[:].rearrange("p t h c -> p t (h c)")).then_inc(rows_stored, 16)

        @block.sync
        def _(sp):
            counts = [sp.alloc_register(f"counts_bs{k}") for k in range(2)]
            sp.sem_inc(rows_stored, 16)
            sp.dma_start(ident[:], ident_in).then_inc(ident_ready, 16)
            for g in range(GROUPS):
                load(sp, 0, g)
                load_bias(sp, g)
                if g == 1:
                    put_shift(sp, 0, 0)

            def batch(b, last):
                for u in range(UNITS):
                    if u % 2 == 0 and u >= 2 and not last:
                        g = u // 2 - 1
                        wait_apart(sp, counts, (ident_ready, 16), (st_ready, b * BATCH_STEPS + 2 * STEPS * (g + 1)),
                                   (pv_done, b * (BATCH_STEPS // HG) + 2 * STEPS // HG * (g + 1) + PV0))
                        load(sp, b + 1, g)
                    if u >= 1:
                        store_rows(sp, b, u - 1, b * UNITS + u - 1)
                    if u < UNITS - 1 or not last:
                        put_shift(sp, (u + 1) % UNITS, b * UNITS + u + 1)
                    if u == 0 and last:
                        for dst, src in later:
                            sp.dma_start(dst, src, allow_slow_non_contiguous=True).then_inc(later_in, 16)
                if not last:
                    wait_apart(sp, counts, (ident_ready, 16), (st_ready, b * BATCH_STEPS + BATCH_STEPS),
                               (pv_done, b * (BATCH_STEPS // HG) + BATCH_STEPS // HG + PV0))
                    load(sp, b + 1, GROUPS - 1)
                store_rows(sp, b, UNITS - 1, b * UNITS + UNITS - 1)

            with sp.Fori(0, B - 1) as b:
                batch(b, False)
            batch(B - 1, True)
            sp.wait_ge(rows_stored, 16 * (B * UNITS + 1))
            sp.wait_ge(later_in, 16 * len(later))
            sp.wait_ge(cleared, 16 * (len(spare_rows) + B * UNITS * len(cleared_dram)))

        @block.vector
        def _(dve):
            dve.sem_inc(max_done, MAX0)
            nc.vector.memset(no_rows[:], 0.0).then_inc(no_rows_done, 1)
            dve.wait_ge(ident_ready, 16)
            nc.vector.tensor_copy(ident16[:], ident[:]).then_inc(ident16_done, 1)

            def step(b, s):
                unit, j = split(s)
                dve.wait_ge(s_ready, b * BATCH_STEPS + s + 1)
                nc.vector.tensor_reduce(half_max[unit % 2][:, j:j + 1], s_bank[s % S_BANKS][:], AX.X, ALU.max).then_inc(max_done, 1)
                if j == STEPS - 1:
                    dve.wait_ge(max_done, b * BATCH_STEPS + s + 1 + MAX0)
                    dve.wait_ge(shift_done, b * (4 * UNITS) + 4 * unit)
                    nc.vector.tensor_reduce(minus_max[:], half_max[unit % 2][:].rearrange("p (r k) -> p r k", k=2),
                                            AX.X, ALU.max, negate=True).then_inc(row_max_done, 1)

            for s in range(LEAD):
                step(0, s)
            with dve.Fori(0, B - 1) as b:
                for s in range(LEAD, BATCH_STEPS):
                    step(b, s)
                for s in range(LEAD):
                    step(b + 1, s)
            for s in range(LEAD, BATCH_STEPS):
                step(B - 1, s)

        @block.gpsimd
        def _(pool):
            counts = [pool.alloc_register(f"counts_b{k}") for k in range(2)]
            for g in range(GROUPS):
                nc.gpsimd.memset(k_stack[g][SCORE_ROWS:STACK_ROWS], 1.0).then_inc(ones_done, 1)
            pool.wait_ge(ones_done, GROUPS)
            nc.gpsimd.memset(zeros[:], 0.0).then_inc(zeros_done, 1)
            pool.wait_ge(zeros_done, 1)
            for rows in spare_rows:
                pool.dma_start(rows, zeros[:, 0:rows.shape[1]]).then_inc(cleared, 16)
            with pool.Fori(0, B * UNITS) as n:
                wait_apart(pool, counts, (ones_done, GROUPS), (row_max_done, n + 1), (shift_turned, n + 1))
                nc.gpsimd.tensor_copy(shift[:, 0, :], minus_max[:]).then_inc(shift_done, 1)
                pool.wait_ge(shift_done, n * 4 + 1)
                nc.gpsimd.tensor_tensor(shift_rest[:], minus_max[:], shift[:, 0, :], ALU.subtract).then_inc(shift_done, 1)
                wait_apart(pool, counts, (ones_done, GROUPS), (shift_done, n * 4 + 2))
                nc.gpsimd.tensor_copy(shift[:, 1, :], shift_rest[:]).then_inc(shift_done, 1)
                pool.wait_ge(shift_done, n * 4 + 3)
                nc.gpsimd.tensor_tensor(shift[:, 2, :], shift_rest[:], shift[:, 1, :], ALU.subtract).then_inc(shift_done, 1)
                for table in cleared_dram:
                    pool.dma_start(table[bass.ds(n * P, P), :], zeros[:, 0:DIM]).then_inc(cleared, 16)

        @block.scalar
        def _(act):
            act.sem_inc(exp_done, EXP0)
            act.sem_inc(unit_out_done, 1)
            act.sem_inc(rows_done, 1)

            def shift_copy(n):
                act.wait_ge(shift_turned, n + 2)
                act.wait_ge(shift_in, n * 48)
                nc.scalar.copy(shiftT[:], misc[0:48, 0:P]).then_inc(shiftT_done, 1)

            def out_copy(n):
                act.wait_ge(pv_done, n * (STEPS // HG) + STEPS // HG + PV0)
                act.wait_ge(out_turned, n + 1)
                nc.scalar.copy(unit_out[:], pv_bank[:]).then_inc(unit_out_done, 1)

            def rows_copy(n):
                act.wait_ge(out_turned, n + 2)
                act.wait_ge(rows_stored, n * 16 + 16)
                nc.scalar.copy(unit_rows[:], misc[:].rearrange("p (t h c) -> p t h c", t=PER, h=HG)[:, :, :, 0:HD + 1]).then_inc(rows_done, 1)

            shift_copy(0)

            def batch(b, last):
                for u in range(UNITS):
                    n = b * UNITS + u
                    for j in range(STEPS):
                        s = STEPS * u + j
                        act.wait_ge(st_ready, b * BATCH_STEPS + s + 1)
                        if j % HG == 0:
                            act.wait_ge(pv_done, b * (BATCH_STEPS // HG) + s // HG + 1)
                        nc.scalar.activation(probs[:, s % P_SLOTS, :], st_bank[s % ST_BANKS][:], ACT.Exp).then_inc(exp_done, 1)
                        if u >= 1 and j == J_UOUT:
                            out_copy(n - 1)
                        if u >= 1 and j == J_OCOPY:
                            rows_copy(n - 1)
                        if j == J_MCOPY and (u < UNITS - 1 or not last):
                            shift_copy(n + 1)
                out_copy(b * UNITS + UNITS - 1)
                rows_copy(b * UNITS + UNITS - 1)

            with act.Fori(0, B - 1) as b:
                batch(b, False)
            batch(B - 1, True)

        @block.tensor
        def _(pe):
            pe.wait_ge(ident_ready, 16)
            pe.wait_ge(ident16_done, 1)
            pe.sem_inc(pv_done, PV0)
            pe.sem_inc(shift_turned, 1)
            pe.sem_inc(out_turned, 1)
            pe.wait_ge(no_rows_done, 1)
            nc.tensor.matmul(pv_bank[:], no_rows[:, 0:P], no_rows[:], start=True, stop=True)

            def score(b, base, s):
                unit, j = split(s)
                g, half = unit // 2, unit % 2
                h, tile, keys = j // 8, j // 2 % 4, j % 2
                if j == 0 and half == 0:
                    pe.wait_ge(loaded[g], b * LOAD + LOAD)
                    pe.wait_ge(bias_rows_in[g], LOAD_BIAS)
                pe.wait_ge(max_done, base + before(s, S_BANKS) + 1 + MAX0)
                nc.tensor.matmul(s_bank[s % S_BANKS][:], q_stack[g][0:SCORE_ROWS, half, h, tile * P:(tile + 1) * P],
                                 k_stack[g][0:SCORE_ROWS, keys, h, :], start=True, stop=True).then_inc(s_ready, 1)

            def score_t(b, s):
                unit, j = split(s)
                g, half = unit // 2, unit % 2
                tile, h = j // HG, j % HG
                if j == 0:
                    pe.wait_ge(shift_in, b * (UNITS * 48) + (unit + 1) * 48)
                pe.wait_ge(exp_done, b * BATCH_STEPS + before(s, ST_BANKS) + 1 + EXP0)
                nc.tensor.matmul(st_bank[s % ST_BANKS][:], k_stack[g][:, tile // PER, h, tile % PER * P:(tile % PER + 1) * P],
                                 q_stack[g][:, half, h, :], start=True, stop=True).then_inc(st_ready, 1)

            def times_values(b, unit, tile):
                s = STEPS * unit + HG * tile
                pe.wait_ge(exp_done, b * BATCH_STEPS + s + HG + EXP0)
                if tile == 0:
                    pe.wait_ge(unit_out_done, b * UNITS + unit + 1)
                for h in range(HG):
                    mm = nc.tensor.matmul(pv_bank[PART * h:PART * h + VW, :], values[unit // 2][:, tile, h, :],
                                          probs[:, (s + h) % P_SLOTS, :], start=(tile == 0), stop=(tile == T // P - 1),
                                          tile_position=(0, PART * h))
                mm.then_inc(pv_done, 1)

            def turn_out(n, shifts):
                pe.wait_ge(unit_out_done, n + 2)
                pe.wait_ge(shiftT_done, shifts)
                for t in range(PER):
                    mm = nc.tensor.transpose(misc[:, t * P:(t + 1) * P], unit_out[:, t * P:(t + 1) * P], ident[:])
                mm.then_inc(out_turned, 1)

            def turn_shift(n, rows):
                pe.wait_ge(shift_done, n * 4 + 4)
                pe.wait_ge(rows_done, rows + 1)
                nc.tensor.matmul(misc[0:48, 0:P], shift[:].rearrange("p c r -> p (c r)"), ident16[:],
                                 start=True, stop=True).then_inc(shift_turned, 1)

            for s in range(LEAD):
                score(0, 0, s)
            pe.wait_ge(ones_done, GROUPS)
            turn_shift(0, 0)

            def batch(b, last):
                base = b * BATCH_STEPS if last else pe.snap(score_count, min_val=0, max_val=B * BATCH_STEPS)
                for u in range(UNITS + 1):
                    for j in range(STEPS):
                        s = STEPS * u + j
                        if u < UNITS:
                            score_t(b, s)
                            if s + LEAD < BATCH_STEPS:
                                score(b, base, s + LEAD)
                            elif not last:
                                score(b + 1, base + BATCH_STEPS, s + LEAD - BATCH_STEPS)
                        done = s - PV_LAG
                        if done >= 0 and done % HG == HG - 1 and done < BATCH_STEPS:
                            unit, jj = split(done)
                            times_values(b, unit, jj // HG)
                        if u >= 1 and j == J_OTURN:
                            turn_out(b * UNITS + u - 1, b * UNITS + (u if last and u == UNITS else u + 1))
                        if u < UNITS and j == J_MTURN and (u < UNITS - 1 or not last):
                            turn_shift(b * UNITS + u + 1, b * UNITS + u)

            score_count = pe.alloc_register("score_count")
            pe.reg_mov(score_count, 0)
            with pe.Fori(0, B - 1) as b:
                batch(b, False)
                pe.reg_add(score_count, score_count, BATCH_STEPS)
            batch(B - 1, True)


E, TOPK, NGROUPS, TOPG = 64, 8, 8, 4
GE = E // NGROUPS
CAP = 128
F = 64
ROUTE_SCALE = 2.5
ROW = DIM + E
ROWS = N + CAP
BIG = 1e30
STEPS_1, STEPS_2 = 2, 25


def inverse_std(pool, nc, out, var, minus_half, tmp, tmp_ready, tmp_count, done):
    nc.gpsimd.tensor_scalar(tmp, var, EPS, None, ALU.add).then_inc(tmp_ready, 1)
    pool.wait_ge(tmp_ready, tmp_count)
    nc.gpsimd.tensor_tensor(out, tmp, minus_half, ALU.pow).then_inc(done, 1)


def route(nc, x, att, consts, table, shared_sums):
    with ExitStack() as ctx:
        sb = lambda name, shape, dt=F32: ctx.enter_context(nc.sbuf_tensor(name, shape, dt))
        ps = lambda name: ctx.enter_context(nc.psum_tensor(name, [P, CHUNK], F32))
        sem = lambda name: ctx.enter_context(nc.semaphore(name))

        k = consts
        ones = sb("ones", [P, P], BF16)
        before = sb("before", [P, P], BF16)
        minus_half = sb("minus_half", [P, PER])
        tile_no = sb("tile_no", [P, PER])
        one_row = sb("one_row", [32, P])
        zero4 = sb("zero4", [P, PER])
        shift = {name: sb(f"shift_{name}", [P, PER]) for name in ("y", "x1")}

        attc = sb("attc", [P, PER, H, HD + 1])
        xc = sb("xcC", [P, PER, DIM])
        recip = sb("recip", [P, PER, H])
        normed = sb("normed", [P, PER, DIM])
        turned_sb = sb("turned_sb", [P, CHUNK])
        y = sb("y", [P, PER, DIM])
        stats = sb("statsC", [P, PER, 6])
        mv = sb("mvC", [P, PER, 2])
        veps = sb("veps", [P, PER])
        rstd = sb("rstdC", [P, PER])
        x1c = sb("x1c", [P, PER, DIM])
        xf = sb("xf", [P, PER, DIM])
        weights = sb("weights", [P, PER, E])
        xfT = sb("xfT", [P, CHUNK])
        scores = sb("scores", [P, PER, E])
        sg = sb("sg", [P, CHUNK])
        gate_sb, up_sb = sb("gate_sb", [P, CHUNK]), sb("up_sb", [P, CHUNK])
        sh = sb("sh", [P, CHUNK])
        shared = sb("shared", [P, PER, DIM])
        sfc = sb("sfc", [P, PER, E])
        top1 = sb("top1", [P, PER * NGROUPS])
        is_top = sb("is_top", [P, PER, E])
        count = sb("count", [P, PER * NGROUPS])
        second = sb("second", [P, PER * NGROUPS])
        gsum = sb("gsum", [P, PER, NGROUPS])
        above = sb("above", [P, PER, NGROUPS, NGROUPS])
        same = sb("same", [P, PER, NGROUPS, NGROUPS])
        grank = sb("grank", [P, PER * NGROUPS])
        tmp = sb("tmp", [P, PER, E])
        best = sb("best", [P, PER, TOPK])
        marked = sb("marked", [P, PER, E])
        chosen = sb("chosen", [P, PER, E], BF16)
        picked = sb("picked", [P, PER, E])
        wsum = sb("wsum", [P, PER])
        wrec = sb("wrec", [P, PER])
        sofar = sb("sofar", [P, E], BF16)
        key = sb("key", [P, PER, E])
        keys = sb("keys", [P, PER * TOPK])
        keys_i = sb("keys_i", [P, PER * TOPK], U32)
        part_i = sb("part_i", [P, 2, PER * TOPK], U32)
        part = sb("part", [P, 2, PER * TOPK])
        hot_e = sb("hot_e", [P, PER * TOPK, E], BF16)
        id_parts = sb("id_parts", [P, PER * TOPK, 2, E], BF16)
        hot_s = sb("hot_s", [P, PER * TOPK, CAP], BF16)
        nothing = sb("nothing", [P, P], BF16)
        lo = sb("lo", [P, E])
        token = sb("token", [P, E])
        is_free = sb("is_free", [P, E])

        psA, psB, psC, psD, psE, psF, psG, psY = [ps(f"psC{i}") for i in range(8)]

        own = {1: sem("stage1_steps"), 2: sem("stage2_steps")}
        setup_v, setup_p, final_steps = sem("setup_v"), sem("setup_p"), sem("final_steps")
        att_in, x_in = sem("att_inC"), sem("x_inC")
        signals = {}
        for name in ("normed_done", "attT_turned", "attT_done", "projected", "var_y", "x1_done",
                     "var_x1", "xf_done", "xf_turned", "xfT_done", "logits_ready", "scores_done",
                     "gate_up_ready", "shared_sig", "shared_h", "down_ready", "shared_done", "picked_done",
                     "chosen_done", "ranks_ready", "sofar_done", "weights_done", "hot_e_done",
                     "ids_parts_done", "hot_s_done", "x1_kept", "y_normed", "recip_done", "shift_y", "shift_x1", "ids_ready", ):
            signals[name] = sem(name)
        S = signals
        tile_no_steps, inverse_steps = sem("tile_no_steps"), sem("inverse_steps")
        sofar_steps = sem("sofar_steps")
        xf_stored, shared_stored, weights_stored = sem("xf_stored"), sem("shared_stored"), sem("weights_stored")

        def this(c):
            return c + 2

        def last(c):
            return c + 1

        def credit(engine, *names):
            for name in names:
                engine.sem_inc(S[name], 1)

        block = ctx.enter_context(nc.Block())

        @block.sync
        def _(sp):
            def rows(a, c):
                return a[bass.ds(c * CHUNK, CHUNK)].rearrange("(j p) d -> p j d", p=P)

            def load_att(c):
                sp.dma_start(attc[:].rearrange("p j h c -> p j (h c)"),
                             att[bass.ds(c * CHUNK, CHUNK)].rearrange("(j p) h c -> p j (h c)", p=P)).then_inc(att_in, 16)

            def load_x(c):
                sp.dma_start(xc[:], rows(x, c)).then_inc(x_in, 16)

            def next_att(c):
                wait_apart(sp, counts, (setup_v, 3), (S["normed_done"], this(c)))
                load_att(c + 1)

            def stage1(c, more):
                if more:
                    wait_apart(sp, counts, (setup_v, 3), (S["x1_done"], this(c)))
                    load_x(c + 1)

            def stage1_end(c):
                wait_apart(sp, counts, (setup_v, 3), (S["xf_done"], this(c)))
                sp.dma_start(rows(table, c)[:, :, 0:DIM], xf[:]).then_inc(xf_stored, 16)
                wait_apart(sp, counts, (setup_v, 3), (S["shared_done"], this(c)))
                sp.dma_start(rows(shared_sums, c), shared[:]).then_inc(shared_stored, 16)

            def stage2(c):
                wait_apart(sp, counts, (setup_v, 3), (S["weights_done"], this(c)))
                sp.dma_start(rows(table, c)[:, :, DIM:ROW], weights[:]).then_inc(weights_stored, 16)

            counts = [sp.alloc_register("counts_cs")]
            load_att(0)
            load_x(0)
            for stored in (xf_stored, shared_stored, weights_stored):
                sp.sem_inc(stored, 16)
            sp.wait_ge(setup_v, 3)
            next_att(0)
            stage1(0, True)
            stage1_end(0)
            next_att(1)
            with sp.Fori(0, CHUNKS - 3) as i:
                stage1(i + 1, True)
                stage2(i)
                stage1_end(i + 1)
                next_att(i + 2)
            stage1(CHUNKS - 2, True)
            stage2(CHUNKS - 3)
            stage1_end(CHUNKS - 2)
            stage1(CHUNKS - 1, False)
            stage2(CHUNKS - 2)
            stage1_end(CHUNKS - 1)
            stage2(CHUNKS - 1)
            for stored in (xf_stored, shared_stored, weights_stored):
                sp.wait_ge(stored, (CHUNKS + 1) * 16)

        @block.vector
        def _(dve):
            V = nc.vector
            counts = [dve.alloc_register("counts_cv")]
            credit(dve, "recip_done", "var_y", "var_x1", "picked_done",
                   "chosen_done", "weights_done", "hot_e_done", "hot_s_done")
            V.memset(one_row[:], 0.0)
            V.memset(ones[:], 1.0).then_inc(setup_v, 1)
            V.memset(nothing[:], 0.0).then_inc(setup_v, 1)
            dve.wait_ge(setup_v, 2)
            V.memset(one_row[0:1, :], 1.0)
            V.tensor_copy(before[:], k["before"][:]).then_inc(setup_v, 1)

            n = {1: 0, 2: 0}
            base = {1: 0, 2: 0}
            latest = {}

            def chunk(stage, c, steps):
                n[stage] = 0
                base[stage] = c * steps

            def step(stage, ins):
                ins.then_inc(own[stage], 1)
                n[stage] += 1
                latest[stage] = (own[stage], base[stage] + n[stage])

            def signal(stage, ins, name, c):
                ins.then_inc(S[name], 1)
                latest[stage] = (S[name], this(c))

            def settle(stage, plain=False):
                if plain:
                    wait_apart(dve, counts, (setup_v, 3), latest[stage])
                else:
                    dve.wait_ge(*latest[stage])

            by_tile = lambda a, width: a.rearrange("p (o d) -> p o d", o=1).to_broadcast([P, PER, width])

            def norm_stats(c, src, name):
                for j in range(PER):
                    ins = V.bn_stats(stats[:, j, :], src(j))
                step(1, ins)
                settle(1, plain=True)
                for j in range(PER):
                    ins = V.bn_aggr(mv[:, j, :], stats[:, j, :])
                signal(1, ins, name, c)

            def reciprocal_sums(c):
                dve.wait_ge(att_in, c * 16 + 16)
                dve.wait_ge(S["normed_done"], last(c))
                V.reciprocal(recip[:], attc[:, :, :, HD]).then_inc(S["recip_done"], 1)

            def output_stats(c):
                chunk(1, c, STEPS_1)
                dve.wait_ge(S["projected"], this(c))
                dve.wait_ge(S["xf_done"], last(c))
                norm_stats(c, lambda j: psY[:, j * P:(j + 1) * P], "var_y")

            def residual_stats(c):
                dve.wait_ge(S["x1_done"], this(c))
                norm_stats(c, lambda j: x1c[:, j, :], "var_x1")

            by_group = lambda a: a.rearrange("p j (g e) -> p (j g) e", e=GE)
            spread = lambda a: a.rearrange("p (g o) -> p g o", o=1).to_broadcast([P, PER * NGROUPS, GE])

            def then(ins, plain=False):
                step(2, ins)
                settle(2, plain)

            def two_best(c):
                chunk(2, c, STEPS_2)
                dve.wait_ge(S["scores_done"], this(c))
                then(V.tensor_tensor(sfc[:], scores[:], by_tile(k["e_bias"][:], E), ALU.add))
                then(V.tensor_reduce(top1[:], by_group(sfc[:]), AX.X, ALU.max))
                then(V.tensor_tensor(by_group(is_top[:]), by_group(sfc[:]), spread(top1[:]), ALU.is_equal))
                V.tensor_reduce(count[:], by_group(is_top[:]), AX.X, ALU.add)
                then(V.scalar_tensor_tensor(out=tmp[:], in0=is_top[:], scalar=-BIG, in1=sfc[:], op0=ALU.mult, op1=ALU.add))
                V.tensor_reduce(second[:], by_group(tmp[:]), AX.X, ALU.max)
                then(V.tensor_scalar(count[:], count[:], 2.0, -BIG, ALU.is_lt, ALU.mult))
                then(V.tensor_tensor(count[:], count[:], top1[:], ALU.add))
                then(V.tensor_tensor(second[:], second[:], count[:], ALU.max))
                then(V.tensor_tensor(gsum[:].rearrange("p j g -> p (j g)"), top1[:], second[:], ALU.add))

            def group_choice(c):
                settle(2)
                shape = [P, PER, NGROUPS, NGROUPS]
                mine = gsum[:].rearrange("p j (g o) -> p j g o", o=1).to_broadcast(shape)
                other = gsum[:].rearrange("p j (o g) -> p j o g", o=1).to_broadcast(shape)
                V.tensor_tensor(above[:], other, mine, ALU.is_gt)
                then(V.tensor_tensor(same[:], other, mine, ALU.is_equal))
                then(V.tensor_tensor(same[:], same[:], k["earlier"][:].rearrange("p (o g h) -> p o g h", o=1, g=NGROUPS).to_broadcast(shape), ALU.mult))
                then(V.tensor_tensor(above[:], above[:], same[:], ALU.add))
                then(V.tensor_reduce(grank[:], above[:].rearrange("p j g o -> p (j g) o"), AX.X, ALU.add))
                then(V.tensor_scalar(grank[:], grank[:], float(TOPG), None, ALU.is_lt))
                then(V.tensor_tensor(by_group(tmp[:]), by_group(sfc[:]), spread(grank[:]), ALU.mult), plain=True)
                for j in range(PER):
                    ins = V.max(best[:, j, :], tmp[:, j, :])
                then(ins, plain=True)
                for j in range(PER):
                    ins = V.match_replace(marked[:, j, :], best[:, j, :], tmp[:, j, :], -BIG)
                step(2, ins)

            def choice(c):
                settle(2)
                dve.wait_ge(S["sofar_done"], last(c))
                signal(2, V.tensor_scalar(chosen[:], marked[:], -0.5 * BIG, None, ALU.is_lt), "chosen_done", c)
                settle(2)
                signal(2, V.tensor_tensor(picked[:], scores[:], chosen[:], ALU.mult), "picked_done", c)
                settle(2)
                then(V.tensor_reduce(wsum[:], picked[:], AX.X, ALU.add))
                then(V.tensor_scalar(wsum[:], wsum[:], 1e-20, None, ALU.add))
                then(V.reciprocal(wrec[:], wsum[:]))
                dve.wait_ge(weights_stored, c * 16 + 16)
                signal(2, V.scalar_tensor_tensor(out=weights[:], in0=picked[:], scalar=ROUTE_SCALE,
                                                 in1=wrec[:].rearrange("p (j o) -> p j o", o=1).to_broadcast([P, PER, E]),
                                                 op0=ALU.mult, op1=ALU.mult), "weights_done", c)

            def rank_and_expert(c):
                dve.wait_ge(S["ranks_ready"], this(c))
                then(V.scalar_tensor_tensor(out=key[:], in0=psC[:, 0:PER * E].rearrange("p (j e) -> p j e", j=PER), scalar=float(E),
                                            in1=by_tile(k["expert_1"][:], E), op0=ALU.mult, op1=ALU.add))
                then(V.tensor_tensor(key[:], key[:], chosen[:], ALU.mult), plain=True)
                for j in range(PER):
                    ins = V.max(keys[:, j * TOPK:(j + 1) * TOPK], key[:, j, :])
                then(ins)
                then(V.tensor_scalar(keys_i[:], keys[:], -1.0, None, ALU.add))
                V.tensor_scalar(part_i[:, 0, :], keys_i[:], E - 1, None, ALU.bitwise_and)
                then(V.tensor_scalar(part_i[:, 1, :], keys_i[:], E.bit_length() - 1, None, ALU.logical_shift_right))
                then(V.tensor_copy(part[:], part_i[:]))
                dve.wait_ge(S["ids_parts_done"], last(c))
                signal(2, V.tensor_tensor(hot_e[:], k["iota"][:, 0:E].rearrange("p (o e) -> p o e", o=1).to_broadcast([P, PER * TOPK, E]),
                                          part[:, 0, :].rearrange("p (k o) -> p k o", o=1).to_broadcast([P, PER * TOPK, E]),
                                          ALU.is_equal), "hot_e_done", c)

            def slot_hot(c):
                dve.wait_ge(S["ids_ready"], last(c))
                signal(2, V.tensor_tensor(hot_s[:], k["iota"][:].rearrange("p (o s) -> p o s", o=1).to_broadcast([P, PER * TOPK, CAP]),
                                          part[:, 1, :].rearrange("p (k o) -> p k o", o=1).to_broadcast([P, PER * TOPK, CAP]),
                                          ALU.is_equal), "hot_s_done", c)

            def stage2(c, ahead, far):
                two_best(c)
                if ahead:
                    output_stats(c + 1)
                group_choice(c)
                if ahead:
                    residual_stats(c + 1)
                choice(c)
                if far:
                    reciprocal_sums(c + 2)
                rank_and_expert(c)
                slot_hot(c)

            dve.wait_ge(setup_p, 1)
            reciprocal_sums(0)
            output_stats(0)
            residual_stats(0)
            reciprocal_sums(1)
            assert n[1] == STEPS_1
            with dve.Fori(0, CHUNKS - 2) as i:
                stage2(i, True, True)
                assert n[2] == STEPS_2
            stage2(CHUNKS - 2, True, False)
            stage2(CHUNKS - 1, False, False)

            dve.wait_ge(S["ids_ready"], this(CHUNKS - 1))
            V.tensor_copy(lo[:], psF[:, 0:E]).then_inc(final_steps, 1)
            dve.wait_ge(final_steps, 1)
            V.scalar_tensor_tensor(out=token[:], in0=psF[:, E:2 * E], scalar=float(P), in1=lo[:], op0=ALU.mult, op1=ALU.add).then_inc(final_steps, 1)
            V.tensor_scalar(is_free[:], lo[:], 0.0, None, ALU.is_equal).then_inc(final_steps, 1)
            dve.wait_ge(final_steps, 3)
            V.tensor_scalar(is_free[:], is_free[:], k["free_id"][:], None, ALU.mult).then_inc(final_steps, 1)
            dve.wait_ge(final_steps, 4)
            V.tensor_tensor(token[:], token[:], is_free[:], ALU.add).then_inc(final_steps, 1)
            dve.wait_ge(final_steps, 5)
            V.tensor_scalar(k["slot_ids"][:], token[:], -1.0, None, ALU.add).then_inc(final_steps, 1)

        @block.gpsimd
        def _(pool):
            G = nc.gpsimd
            counts = [pool.alloc_register("counts_cp"), pool.alloc_register("counts_cp1")]
            credit(pool, "shared_h", "sofar_done", "normed_done", "x1_done", "shift_y", "shift_x1")
            G.memset(sofar[:], 0.0).then_inc(setup_p, 1)
            G.memset(minus_half[:], -0.5).then_inc(setup_p, 1)
            G.memset(zero4[:], 0.0).then_inc(setup_p, 1)
            for j in range(PER):
                G.memset(tile_no[:, j:j + 1], float(j)).then_inc(setup_p, 1)
            pool.wait_ge(setup_p, 3 + PER)
            pool.sem_inc(tile_no_steps, 1)

            def inverse(c, name):
                wait_apart(pool, counts, (setup_p, 3 + PER), (S["var_" + name], this(c)))
                n = c * 6 + (0 if name == "y" else 3)
                inverse_std(pool, nc, rstd[:], mv[:, :, 1], minus_half[:], veps[:], inverse_steps, n + 1, inverse_steps)
                pool.wait_ge(inverse_steps, n + 2)
                G.tensor_tensor(shift[name][:], mv[:, :, 0], rstd[:], ALU.mult).then_inc(inverse_steps, 1)
                pool.wait_ge(inverse_steps, n + 3)
                G.tensor_tensor(shift[name][:], zero4[:], shift[name][:], ALU.subtract).then_inc(S["shift_" + name], 1)

            def normalise(c):
                pool.wait_ge(S["recip_done"], this(c))
                pool.wait_ge(S["attT_turned"], last(c))
                G.tensor_tensor(normed[:].rearrange("p j (h d) -> p (j h) d", h=H),
                                attc[:].rearrange("p j h c -> p (j h) c")[:, :, 0:HD],
                                recip[:].rearrange("p j (h o) -> p (j h) o", o=1).to_broadcast([P, PER * H, HD]),
                                ALU.mult).then_inc(S["normed_done"], 1)

            def stage1(c):
                inverse(c, "y")
                wait_apart(pool, counts, (setup_p, 3 + PER), (S["y_normed"], this(c)), (x_in, c * 16 + 16))
                pool.wait_ge(S["x1_kept"], last(c))
                pool.wait_ge(S["xf_done"], last(c))
                G.tensor_tensor(x1c[:], xc[:], y[:], ALU.add).then_inc(S["x1_done"], 1)
                inverse(c, "x1")

            def stage2(c):
                pool.wait_ge(S["ranks_ready"], this(c))
                for j in range(PER):
                    ins = G.tensor_tensor(sofar[:], sofar[:], chosen[:, j, :], ALU.add)
                    if j < PER - 1:
                        ins.then_inc(sofar_steps, 1)
                        pool.wait_ge(sofar_steps, c * PER + 1 + (j + 1))
                ins.then_inc(S["sofar_done"], 1)

            def shared_expert(c):
                wait_apart(pool, counts, (setup_p, 3 + PER), (S["shared_sig"], this(c)))
                G.tensor_tensor(sg[:], gate_sb[:], sg[:], ALU.mult).then_inc(sofar_steps, 1)
                pool.wait_ge(sofar_steps, c * PER + 1)
                pool.wait_ge(S["down_ready"], last(c))
                G.tensor_tensor(sh[:], up_sb[:], sg[:], ALU.mult).then_inc(S["shared_h"], 1)

            def next_tiles(c):
                wait_apart(pool, counts, (setup_p, 3 + PER), (S["ids_parts_done"], this(c)))
                G.tensor_scalar(tile_no[:], tile_no[:], float(PER), None, ALU.add).then_inc(tile_no_steps, 1)

            normalise(0)
            stage1(0)
            normalise(1)
            shared_expert(0)
            with pool.Fori(0, CHUNKS - 2) as i:
                stage1(i + 1)
                stage2(i)
                normalise(i + 2)
                shared_expert(i + 1)
                next_tiles(i)
            stage1(CHUNKS - 1)
            stage2(CHUNKS - 2)
            shared_expert(CHUNKS - 1)
            next_tiles(CHUNKS - 2)
            stage2(CHUNKS - 1)

        @block.scalar
        def _(act):
            credit(act, "attT_done", "xfT_done", "scores_done", "shared_sig", "shared_done", "ids_parts_done", "x1_kept", "y_normed", "xf_done")

            def copy_attT(c):
                act.wait_ge(S["attT_turned"], this(c))
                nc.scalar.copy(turned_sb[:], psA[:]).then_inc(S["attT_done"], 1)

            def norm_rows(dst, src, name, done):
                for j in range(PER):
                    ins = nc.scalar.activation(dst[:, j, :], src(j), ACT.Identity, scale=rstd[:, j:j + 1], bias=shift[name][:, j:j + 1])
                ins.then_inc(S[done], 1)

            def stage1(c):
                act.wait_ge(S["shift_y"], this(c))
                act.wait_ge(S["x1_done"], last(c))
                norm_rows(y, lambda j: psY[:, j * P:(j + 1) * P], "y", "y_normed")
                act.wait_ge(S["shift_x1"], this(c))
                act.wait_ge(xf_stored, c * 16 + 16)
                act.wait_ge(S["xf_turned"], last(c))
                norm_rows(xf, lambda j: x1c[:, j, :], "x1", "xf_done")
                nc.scalar.copy(k["x1"][:, bass.ds(c * PER, PER), :], x1c[:]).then_inc(S["x1_kept"], 1)
                act.wait_ge(S["xf_turned"], this(c))
                nc.scalar.copy(xfT[:], psA[:]).then_inc(S["xfT_done"], 1)
                act.wait_ge(S["logits_ready"], this(c))
                act.wait_ge(S["picked_done"], last(c))
                nc.scalar.activation(scores[:].rearrange("p j e -> p (j e)"), psG[:, 0:PER * E], ACT.Sigmoid).then_inc(S["scores_done"], 1)

            def shared_gate(c):
                act.wait_ge(S["gate_up_ready"], this(c))
                act.wait_ge(S["shared_h"], last(c))
                nc.scalar.activation(sg[:], psD[:], ACT.Sigmoid)
                nc.scalar.copy(gate_sb[:], psD[:])
                nc.scalar.copy(up_sb[:], psE[:]).then_inc(S["shared_sig"], 1)

            def copy_shared(c):
                act.wait_ge(S["down_ready"], this(c))
                act.wait_ge(shared_stored, c * 16 + 16)
                nc.scalar.copy(shared[:].rearrange("p j d -> p (j d)"), psB[:]).then_inc(S["shared_done"], 1)

            def number(c):
                act.wait_ge(S["hot_e_done"], this(c))
                act.wait_ge(tile_no_steps, c + 1)
                act.wait_ge(S["ids_ready"], last(c))
                nc.scalar.activation(id_parts[:, :, 0, :], hot_e[:], ACT.Copy, scale=k["token_lo"][:])
                for j in range(PER):
                    ks = slice(j * TOPK, (j + 1) * TOPK)
                    ins = nc.scalar.activation(id_parts[:, ks, 1, :], hot_e[:, ks, :], ACT.Copy, scale=tile_no[:, j:j + 1])
                ins.then_inc(S["ids_parts_done"], 1)

            act.wait_ge(setup_p, 2)
            nc.scalar.activation(sg[:, 0:PER], minus_half[:], ACT.Sigmoid)
            copy_attT(0)
            stage1(0)
            copy_attT(1)
            shared_gate(0)
            copy_shared(0)
            with act.Fori(0, CHUNKS - 2) as i:
                stage1(i + 1)
                copy_attT(i + 2)
                shared_gate(i + 1)
                number(i)
                copy_shared(i + 1)
            stage1(CHUNKS - 1)
            shared_gate(CHUNKS - 1)
            number(CHUNKS - 2)
            copy_shared(CHUNKS - 1)
            number(CHUNKS - 1)

        @block.tensor
        def _(pe):
            M = nc.tensor.matmul
            credit(pe, "attT_turned", "projected", "xf_turned", "logits_ready", "gate_up_ready", "down_ready",
                   "ranks_ready", "ids_ready")
            pe.wait_ge(setup_v, 3)
            pe.wait_ge(setup_p, 1)
            M(psF[:, 0:2 * E], nothing[:], nothing[:], start=True, stop=False)

            def by_tile(bank, src, w, done, width=P):
                for j in range(PER):
                    mm = M(bank[:, j * width:(j + 1) * width], src[:, j * P:(j + 1) * P], w, start=True, stop=True)
                mm.then_inc(S[done], 1)

            def turn_att(c):
                pe.wait_ge(S["normed_done"], this(c))
                pe.wait_ge(S["xfT_done"], last(c))
                for j in range(PER):
                    mm = nc.tensor.transpose(psA[:, j * P:(j + 1) * P], normed[:, j, :], k["ident"][:])
                mm.then_inc(S["attT_turned"], 1)

            def project(c):
                pe.wait_ge(S["attT_done"], this(c))
                pe.wait_ge(S["y_normed"], last(c))
                for j in range(PER):
                    M(psY[:, j * P:(j + 1) * P], turned_sb[:, j * P:(j + 1) * P], k["w_o"][:], start=True, stop=False)
                    mm = M(psY[:, j * P:(j + 1) * P], one_row[:], k["b_o"][0:32, :], start=False, stop=True)
                mm.then_inc(S["projected"], 1)

            def experts_input(c):
                pe.wait_ge(S["xf_done"], this(c))
                for j in range(PER):
                    mm = nc.tensor.transpose(psA[:, j * P:(j + 1) * P], xf[:, j, :], k["ident"][:])
                mm.then_inc(S["xf_turned"], 1)
                pe.wait_ge(S["xfT_done"], this(c))
                pe.wait_ge(S["scores_done"], last(c))
                by_tile(psG, xfT, k["gate"][:], "logits_ready", E)

            def shared_gate_up(c):
                pe.wait_ge(S["shared_sig"], last(c))
                M(psD[:], k["s_gate"][:], xfT[:], start=True, stop=True)
                M(psE[:], k["s_up"][:], xfT[:], start=True, stop=True).then_inc(S["gate_up_ready"], 1)

            def shared_down(c):
                pe.wait_ge(S["shared_h"], this(c))
                pe.wait_ge(S["shared_done"], last(c))
                by_tile(psB, sh, k["s_down"][:], "down_ready")

            def ranks(c):
                pe.wait_ge(S["chosen_done"], this(c))
                pe.wait_ge(S["sofar_done"], last(c))
                for j in range(PER):
                    out = psC[:, j * E:(j + 1) * E]
                    M(out, before[:], chosen[:, j, :], start=True, stop=False)
                    for jj in range(j):
                        M(out, ones[:], chosen[:, jj, :], start=False, stop=False)
                    mm = M(out, ones[:], sofar[:], start=False, stop=True)
                mm.then_inc(S["ranks_ready"], 1)

            def slots(c, final):
                pe.wait_ge(S["ids_parts_done"], this(c))
                pe.wait_ge(S["hot_s_done"], this(c))
                for n_ in range(PER * TOPK):
                    mm = M(psF[:, 0:2 * E], hot_s[:, n_, :], id_parts[:, n_].rearrange("p a e -> p (a e)"),
                           start=False, stop=(final and n_ == PER * TOPK - 1))
                mm.then_inc(S["ids_ready"], 1)

            turn_att(0)
            project(0)
            experts_input(0)
            turn_att(1)
            shared_gate_up(0)
            project(1)
            shared_down(0)
            with pe.Fori(0, CHUNKS - 2) as i:
                ranks(i)
                experts_input(i + 1)
                turn_att(i + 2)
                shared_gate_up(i + 1)
                project(i + 2)
                shared_down(i + 1)
                slots(i, False)
            ranks(CHUNKS - 2)
            experts_input(CHUNKS - 1)
            shared_gate_up(CHUNKS - 1)
            shared_down(CHUNKS - 1)
            slots(CHUNKS - 2, False)
            ranks(CHUNKS - 1)
            slots(CHUNKS - 1, True)


def run_experts(nc, table, w13, w2_t, consts, sums):
    Q = 4
    PAIRS = E // (2 * Q)
    with ExitStack() as ctx:
        sb = lambda name, shape, dt=F32: ctx.enter_context(nc.sbuf_tensor(name, shape, dt))
        ps = lambda name: ctx.enter_context(nc.psum_tensor(name, [P, CHUNK], F32))
        sem = lambda name: ctx.enter_context(nc.semaphore(name))
        two = lambda make, name, *args: [make(f"{name}{a}", *args) for a in range(2)]
        ident = consts["ident"]
        up_w, down_w = two(sb, "up_w", [P, 2 * Q * F]), two(sb, "down_w", [P, Q // 2 * DIM])
        ids = consts["slot_ids"]
        ids_g, ids_s = two(sb, "ids_g", [P, Q], U32), two(sb, "ids_s", [P, Q], U32)
        xe = two(sb, "xe", [P, Q, ROW])
        w_cur = two(sb, "w_cur", [P, Q])
        xeT = two(sb, "xeT", [P, Q * P])
        gsig = two(sb, "gsig", [P, 2 * P])
        h = two(sb, "h", [P, 2 * P])
        out = two(sb, "out", [P, Q, DIM])
        psX, psH1, psH3, psY = two(ps, "psX"), two(ps, "psH1"), two(ps, "psH3"), two(ps, "psY")
        start = sem("start")
        gathered, w_in = two(sem, "gathered"), two(sem, "w_in")
        ids_g_ready, ids_s_ready = two(sem, "ids_g_ready"), two(sem, "ids_s_ready")
        turned, xeT_ready, up_ready = two(sem, "turnedD"), two(sem, "xeT_ready"), two(sem, "up_ready")
        sig_ready, half_ready, h_ready, y_ready = two(sem, "sig_ready"), two(sem, "half_ready"), two(sem, "h_ready"), two(sem, "y_ready")
        out_ready, gate_ready, w_ready = sem("out_ready"), sem("gate_ready"), sem("w_ready")
        added = [sem(f"added{k}") for k in range(Q)]

        def adds_before(pair, a, rounds):
            if isinstance(pair, int) and pair * 2 + a < rounds:
                return [[] for k in range(Q)]
            return [[(added[k], (pair * 2 + a) * 16 + 16 * (1 - rounds))] for k in range(Q)]

        block = ctx.enter_context(nc.Block())

        @block.sync
        def _(sp):
            sp.sem_inc(start, 1)
            with sp.Fori(0, PAIRS) as i:
                for a in range(2):
                    sp.wait_ge(y_ready[a], i + 1)
                    for dst, src in ((up_w[a], w13), (down_w[a], w2_t)):
                        width = dst.shape[1]
                        sp.dma_start(dst[:], src[:, bass.ds(i * (2 * width) + a * width, width)]).then_inc(w_in[a], 16)

        @block.gpsimd
        def _(pool):
            counts = [pool.alloc_register(f"counts_d{k}") for k in range(3)]

            def gather(pair, a):
                first = isinstance(pair, int) and pair == 0
                free = () if first else ((turned[a], pair), (w_ready, pair * 2 + (a - 1)))
                wait_apart(pool, counts, (start, 1), (ids_g_ready[a], pair + 1), *free)
                for k in range(Q):
                    pool.indirect_dma_start(out=xe[a][:, k, :], out_offset=None, in_=table,
                                            in_offset=bass.IndirectOffsetOnAxis(ap=ids_g[a][:, k:k + 1], axis=0)).then_inc(gathered[a], 16)

            def add(pair, a):
                n = pair * 2 + a
                for k in range(Q):
                    wait_apart(pool, counts, (start, 1), (ids_s_ready[a], pair + 1), (out_ready, n * Q + (Q + k + 1)),
                               *adds_before(pair, a, 1)[k])
                    pool.indirect_dma_start(out=sums[k], out_offset=bass.IndirectOffsetOnAxis(ap=ids_s[a][:, k:k + 1], axis=0),
                                            in_=out[a][:, k, :], in_offset=None, compute_op=ALU.add).then_inc(added[k], 16)

            def rounds(pair):
                for a in range(2):
                    gather(pair + 1, a)
                    add(pair, a)

            for a in range(2):
                gather(0, a)
            rounds(0)
            with pool.Fori(1, PAIRS - 1) as i:
                rounds(i)
            for a in range(2):
                add(PAIRS - 1, a)
            for k in range(Q):
                pool.wait_ge(added[k], 2 * PAIRS * 16)

        @block.vector
        def _(dve):
            counts = [dve.alloc_register(f"counts_dv{k}") for k in range(4)]
            V = nc.vector

            def gather_ids(pair, a):
                V.tensor_copy(ids_g[a][:], ids[:, bass.ds(pair * (2 * Q) + a * Q, Q)]).then_inc(ids_g_ready[a], 1)

            def weights(pair, a):
                n = pair * 2 + a
                free = () if isinstance(pair, int) and pair == 0 else ((out_ready, n * Q),)
                wait_apart(dve, counts, (start, 1), (gathered[a], pair * 64 + 64), *free)
                for k in range(Q):
                    ins = V.tensor_copy(w_cur[a][:, k:k + 1], xe[a][:, k, bass.ds(n * Q + (DIM + k), 1)])
                ins.then_inc(w_ready, 1)

            def hidden(pair, a):
                wait_apart(dve, counts, (start, 1), *sum(adds_before(pair, a, 2), []))
                V.tensor_copy(ids_s[a][:], ids[:, bass.ds(pair * (2 * Q) + a * Q, Q)]).then_inc(ids_s_ready[a], 1)
                dve.wait_ge(sig_ready[a], pair + 1)
                V.tensor_tensor(h[a][:], psH1[a][:, 0:2 * P], gsig[a][:], ALU.mult).then_inc(half_ready[a], 1)
                dve.wait_ge(half_ready[a], pair + 1)
                dve.wait_ge(up_ready[a], pair + 2)
                V.tensor_tensor(h[a][:], psH3[a][:, 0:2 * P], h[a][:], ALU.mult).then_inc(h_ready[a], 1)

            for a in range(2):
                gather_ids(0, a)

            def rounds(pair):
                for a in range(2):
                    weights(pair, a)
                    gather_ids(pair + 1, a)
                    hidden(pair, a)

            rounds(0)
            with dve.Fori(1, PAIRS - 1) as i:
                rounds(i)
            for a in range(2):
                weights(PAIRS - 1, a)
                hidden(PAIRS - 1, a)

        @block.scalar
        def _(act):
            def rounds(pair):
                for a in range(2):
                    n = pair * 2 + a
                    act.wait_ge(turned[a], pair + 1)
                    act.wait_ge(up_ready[a], pair + 1)
                    nc.scalar.copy(xeT[a][:], psX[a][:]).then_inc(xeT_ready[a], 1)
                    act.wait_ge(gate_ready, n + 1)
                    nc.scalar.activation(gsig[a][:], psH1[a][:, 0:2 * P], ACT.Sigmoid).then_inc(sig_ready[a], 1)
                    act.wait_ge(y_ready[a], pair + 2)
                    act.wait_ge(w_ready, n + 1)
                    for k in range(Q):
                        for buffer_free in adds_before(pair, a, 2)[k]:
                            act.wait_ge(*buffer_free)
                        nc.scalar.activation(out[a][:, k, :], psY[k % 2][:, k // 2 * P:(k // 2 + 1) * P], ACT.Copy,
                                             scale=w_cur[a][:, k:k + 1]).then_inc(out_ready, 1)

            rounds(0)
            with act.Fori(1, PAIRS) as i:
                rounds(i)

        @block.tensor
        def _(pe):
            M = nc.tensor.matmul
            for a in range(2):
                pe.sem_inc(up_ready[a], 1)
                pe.sem_inc(y_ready[a], 1)
            pe.sem_inc(out_ready, Q)
            with pe.Fori(0, PAIRS) as i:
                for a in range(2):
                    n = i * 2 + a
                    pe.wait_ge(gathered[a], i * 64 + 64)
                    for k in range(Q):
                        mm = nc.tensor.transpose(psX[a][:, k * P:(k + 1) * P], xe[a][:, k, 0:DIM], ident[:])
                    mm.then_inc(turned[a], 1)
                    pe.wait_ge(xeT_ready[a], i + 1)
                    pe.wait_ge(w_in[a], i * 32 + 32)
                    for which, bank in enumerate((psH1[a], psH3[a])):
                        for k in range(Q):
                            half = F * (k % 2)
                            mm = M(bank[half:half + F, k // 2 * P:(k // 2 + 1) * P], up_w[a][:, (which * Q + k) * F:(which * Q + k + 1) * F],
                                   xeT[a][:, k * P:(k + 1) * P], start=True, stop=True)
                        if which == 0:
                            mm.then_inc(gate_ready, 1)
                    mm.then_inc(up_ready[a], 1)
                    pe.wait_ge(h_ready[a], i + 1)
                    pe.wait_ge(out_ready, n * Q + Q)
                    for k in range(Q):
                        half, m = F * (k % 2), k // 2
                        mm = M(psY[k % 2][:, m * P:(m + 1) * P], h[a][half:half + F, m * P:(m + 1) * P],
                               down_w[a][half:half + F, m * DIM:(m + 1) * DIM], start=True, stop=True)
                    mm.then_inc(y_ready[a], 1)


def finish(nc, x1, sums, out):
    with ExitStack() as ctx:
        sb = lambda name, shape, dt=F32: ctx.enter_context(nc.sbuf_tensor(name, shape, dt))
        sem = lambda name: ctx.enter_context(nc.semaphore(name))
        two = lambda make, name, *args: [make(f"{name}{a}", *args) for a in range(2)]
        s = [sb(f"s{k}", [P, TILES, DIM]) for k in range(4)]
        part = two(sb, "part01_", [P, PER, DIM]), two(sb, "part23_", [P, PER, DIM])
        whole = two(sb, "whole", [P, PER, DIM])
        res = two(sb, "res", [P, PER, DIM])
        stats = sb("statsE", [P, PER, 6])
        mv, veps, rstd = two(sb, "mvE", [P, PER, 2]), two(sb, "vepsE", [P, PER]), two(sb, "rstdE", [P, PER])
        minus_half = sb("minus_halfE", [P, PER])
        loaded, stored = two(sem, "loadedE"), two(sem, "storedE")
        pool_sum, whole_sum = sem("pool_sum"), sem("whole_sum")
        stats_done, var_done, veps_done, rstd_done = sem("stats_doneE"), sem("var_doneE"), sem("veps_doneE"), sem("rstd_doneE")
        norm_done, res_done = sem("norm_doneE"), sem("res_doneE")
        half_made = sem("half_madeE")
        PAIRS = CHUNKS // 2
        block = ctx.enter_context(nc.Block())

        def rows(a_, pair, a):
            return a_[bass.ds(pair * (2 * CHUNK) + a * CHUNK, CHUNK), :].rearrange("(j p) d -> p j d", p=P)

        def tiles(pair, a):
            return bass.ds(pair * (2 * PER) + a * PER, PER)

        @block.sync
        def _(sp):
            for a in range(2):
                sp.sem_inc(stored[a], 16)

            def load(pair, a):
                for k in range(4):
                    sp.dma_start(s[k][:, tiles(pair, a), :], rows(sums[k], pair, a)).then_inc(loaded[a], 16)

            counts = [sp.alloc_register("counts_es")]
            sp.wait_ge(half_made, 1)
            for a in range(2):
                load(0, a)
            with sp.Fori(1, PAIRS) as i:
                for a in range(2):
                    wait_apart(sp, counts, (half_made, 1), (loaded[a], i * 64))
                    load(i, a)

        @block.scalar
        def _(act):
            with act.Fori(0, PAIRS) as i:
                for a in range(2):
                    act.wait_ge(res_done, i * 2 + (a + 3))
                    act.dma_start(rows(out, i, a), res[a][:]).then_inc(stored[a], 16)
            for a in range(2):
                act.wait_ge(stored[a], 16 * (PAIRS + 1))

        @block.gpsimd
        def _(pool):
            counts = [pool.alloc_register(f"counts_e{k}") for k in range(2)]
            nc.gpsimd.memset(minus_half[:], -0.5).then_inc(half_made, 1)
            pool.wait_ge(half_made, 1)

            def sum_two(pair, a):
                wait_apart(pool, counts, (half_made, 1), (loaded[a], pair * 64 + 64), (whole_sum, pair * 2 + (a + 1)))
                nc.gpsimd.tensor_tensor(part[0][a][:], s[0][:, tiles(pair, a), :], s[1][:, tiles(pair, a), :], ALU.add)
                nc.gpsimd.tensor_tensor(part[1][a][:], s[2][:, tiles(pair, a), :], s[3][:, tiles(pair, a), :], ALU.add).then_inc(pool_sum, 1)

            def inverse(pair, a):
                wait_apart(pool, counts, (half_made, 1), (var_done, pair * 2 + (a + 1)))
                inverse_std(pool, nc, rstd[a][:], mv[a][:, :, 1], minus_half[:], veps[a][:], veps_done, pair * 2 + (a + 1), rstd_done)

            sum_two(0, 0)
            with pool.Fori(0, PAIRS - 1) as i:
                sum_two(i, 1)
                inverse(i, 0)
                sum_two(i + 1, 0)
                inverse(i, 1)
            sum_two(PAIRS - 1, 1)
            for a in range(2):
                inverse(PAIRS - 1, a)

        @block.vector
        def _(dve):
            counts = [dve.alloc_register("counts_ev")]
            V = nc.vector
            dve.sem_inc(res_done, 2)
            dve.sem_inc(whole_sum, 2)

            def sum_and_stats(pair, a):
                dve.wait_ge(pool_sum, pair * 2 + (a + 1))
                dve.wait_ge(res_done, pair * 2 + (a + 1))
                V.tensor_tensor(whole[a][:], part[0][a][:], part[1][a][:], ALU.add).then_inc(whole_sum, 1)
                dve.wait_ge(whole_sum, pair * 2 + (a + 3))
                for j in range(PER):
                    ins = V.bn_stats(stats[:, j, :], whole[a][:, j, :])
                ins.then_inc(stats_done, 1)
                wait_apart(dve, counts, (half_made, 1), (stats_done, pair * 2 + (a + 1)))
                for j in range(PER):
                    ins = V.bn_aggr(mv[a][:, j, :], stats[:, j, :])
                ins.then_inc(var_done, 1)

            def norm_and_residual(pair, a):
                dve.wait_ge(rstd_done, pair * 2 + (a + 1))
                for j in range(PER):
                    ins = V.tensor_scalar(whole[a][:, j, :], whole[a][:, j, :], mv[a][:, j, 0:1], rstd[a][:, j:j + 1], ALU.subtract, ALU.mult)
                ins.then_inc(norm_done, 1)
                dve.wait_ge(norm_done, pair * 2 + (a + 1))
                dve.wait_ge(stored[a], pair * 16 + 16)
                V.tensor_tensor(res[a][:], whole[a][:], x1[:, bass.ds(pair * (2 * PER) + a * PER, PER), :], ALU.add).then_inc(res_done, 1)

            sum_and_stats(0, 0)
            with dve.Fori(0, PAIRS - 1) as i:
                sum_and_stats(i, 1)
                norm_and_residual(i, 0)
                sum_and_stats(i + 1, 0)
                norm_and_residual(i, 1)
            sum_and_stats(PAIRS - 1, 1)
            for a in range(2):
                norm_and_residual(PAIRS - 1, a)


def program(nc, x, ln_g, ln_b, w_qkv, b_qkv, w_rel_rows, w_out, b_out, gate_t, e_bias, w13, w2_t,
            shared_gate_t, shared_up_t, shared_down_t, q_table, k_table, ident, before, iota, out):
    dram = lambda name, shape, dt=F32: nc.dram_tensor(name, shape, dt).ap()
    q_image = dram("q_image", [CHUNKS, 3, HD, H, CHUNK], BF16)
    k_image = dram("k_image", [CHUNKS, 3, HD, H, CHUNK], BF16)
    bias_q_image = dram("bias_q_image", [2, 3, HD, H, CHUNK], BF16)
    bias_k_image = dram("bias_k_image", [2, 3, HD, HG, CHUNK], BF16)
    v_columns = dram("v_columns", [P, TILES, H * VW])
    att = dram("att", [N, H, HD + 1])
    table = dram("table", [ROWS, ROW])
    sums = [dram(f"sums{k}", [ROWS, DIM]) for k in range(4)]
    project_tokens(nc, x, ln_g, ln_b, w_qkv, b_qkv, w_rel_rows, q_table, k_table, ident,
                   q_image, k_image, v_columns, bias_q_image, bias_k_image)
    row = lambda a, n: a.rearrange("(o d) -> o d", o=1).to_broadcast([P, n])
    with ExitStack() as ctx:
        consts, later = {}, []
        for name, shape, src in (
            ("ident", [P, P], ident), ("before", [P, P], before), ("iota", [P, P], iota[0:1, :].to_broadcast([P, P])),
            ("token_lo", [P, 1], iota[1:2, :].rearrange("o p -> p o")), ("free_id", [P, 1], iota[2:3, :].rearrange("o p -> p o")),
            ("expert_1", [P, E], iota[1:2, 0:E].to_broadcast([P, E])), ("earlier", [P, E], iota[3:4, 0:E].to_broadcast([P, E])),
            ("w_o", [P, DIM], w_out), ("b_o", [P, DIM], row(b_out, DIM)), ("gate", [P, E], gate_t), ("e_bias", [P, E], row(e_bias, E)),
            ("s_gate", [P, P], shared_gate_t), ("s_up", [P, P], shared_up_t), ("s_down", [P, P], shared_down_t),
            ("x1", [P, TILES, DIM], None), ("slot_ids", [P, E], None),
        ):
            consts[name] = ctx.enter_context(nc.sbuf_tensor(f"const_{name}", shape, U32 if name == "slot_ids" else F32))
            if src is not None:
                later.append((consts[name][:], src))
        attend(nc, ident, q_image, k_image, v_columns, bias_q_image, bias_k_image, att, later, sums[1:],
               [a[N:ROWS, :] for a in (*sums, table)])
        route(nc, x, att, consts, table, sums[0])
        run_experts(nc, table, w13, w2_t, consts, sums)
        finish(nc, consts["x1"], sums, out)


def shape_constants():
    freq = np.exp(np.arange(0, HD, 2) * (-np.log(10000.0) / HD))
    angle = np.arange(T)[None, :] * freq[:, None]
    sin, cos = np.sin(angle), np.cos(angle)
    q_table = np.stack([sin, cos, -cos, sin], axis=1).reshape(2 * HD, T)
    k_table = np.stack([cos, sin], axis=1).reshape(HD, T)
    n = np.arange(P)
    earlier = np.arange(NGROUPS)[:, None] > np.arange(NGROUPS)[None, :]
    iota = np.stack([n, n + 1, N + n + 1, np.pad(earlier.reshape(-1), (0, P - E))])
    f = lambda a: np.ascontiguousarray(a, dtype=np.float32)
    return {"q_table": f(q_table), "k_table": f(k_table), "ident": f(np.eye(P)),
            "before": f(n[:, None] < n[None, :]), "iota": f(iota)}


def dims_first(w):
    qk = w[..., :2 * DIM].reshape(*w.shape[:-1], 2, H, HD).swapaxes(-1, -2)
    return np.concatenate([qk.reshape(*w.shape[:-1], 2 * DIM), w[..., 2 * DIM:]], axis=-1)


def place_w_rel(w_rel):
    rows = np.zeros((2 * HD, H * HD), w_rel.dtype)
    for f in range(HD // 2):
        for par in range(2):
            for s in range(2):
                e = 2 * f + par
                rows[4 * f + 2 * par + s, e * H:(e + 1) * H] = w_rel[2 * f + s]
    return rows


def kernel(**inputs):
    import concourse.bacc as bacc
    from concourse.bass_utils import run_bass_kernel_spmd

    a = {k: np.asarray(v) for k, v in inputs.items()}
    by_round = lambda w: w.transpose(2, 0, 1).reshape(DIM, E // 4, 4 * F)
    arrays = {
        "x": a["L0_attn_x"].reshape(N, DIM),
        "ln_g": a["L0_attn_ln_g"], "ln_b": a["L0_attn_ln_b"],
        "w_qkv": dims_first(a["L0_attn_w_qkv"]), "b_qkv": dims_first(a["L0_attn_b_qkv"]), "w_rel_rows": place_w_rel(a["L0_attn_w_rel"]),
        "w_out": a["L0_attn_w_out"], "b_out": a["L0_attn_b_out"],
        "gate_t": a["L0_ffn_gate_weight"].T, "e_bias": a["L0_ffn_e_bias"],
        "w13": np.stack([by_round(a["L0_ffn_w1"]), by_round(a["L0_ffn_w3"])], axis=2).reshape(DIM, -1),
        "w2_t": a["L0_ffn_w2"].transpose(0, 2, 1).reshape(E * F // P, P, DIM).transpose(1, 0, 2).reshape(P, -1),
        "shared_gate_t": a["L0_ffn_shared_gate"].T, "shared_up_t": a["L0_ffn_shared_up"].T,
        "shared_down_t": a["L0_ffn_shared_down"].T,
        **shape_constants(),
    }
    nc = bacc.Bacc("TRN2", target_bir_lowering=False, num_devices=1)
    sent, args = {}, []
    for name, v in arrays.items():
        v = np.ascontiguousarray(v)
        sent[f"in_{name}"] = v
        args.append(nc.dram_tensor(f"in_{name}", v.shape, mybir.dt.from_np(v.dtype), kind="ExternalInput").ap())
    out = nc.dram_tensor("result", (N, DIM), F32, kind="ExternalOutput").ap()
    program(nc, *args, out)
    r = run_bass_kernel_spmd(nc, [sent], core_ids=[0])
    return r.results[0]["result"].reshape(B, T, DIM)
```
